# Optimizing a Trainium2 kernel written in Bass

```python
import numpy as np
import jax
import jax.numpy as jnp

def _softmax(x, axis=-1):
    return jax.nn.softmax(x, axis=axis)

def _gelu(x):
    return jax.nn.gelu(x, approximate=True)

def _silu(x):
    return jax.nn.silu(x)

def _sigmoid(x):
    return jax.nn.sigmoid(x)

def _layernorm(x, axis=-1, eps=1e-05):
    m = jnp.mean(x, axis=axis, keepdims=True)
    v = jnp.var(x, axis=axis, keepdims=True)
    return (x - m) / jnp.sqrt(v + eps)

def _scatter_add(tgt, idx, src, axis=0):
    return tgt.at[idx].add(src)

def _segment_sum(src, seg, n):
    return jax.ops.segment_sum(src, seg, n)
kernel_name = 'mk_gnn_resnorm_d2_gnn_r16_c14c93'

def setup_inputs(seed: int=0):
    np.random.seed(seed)
    _w = jnp.asarray

    def _rec_inputs():
        import jax
        import jax.numpy as jnp
        _gk = jax.random.key(seed)
        x = -0.0009044 + 1 * jax.random.normal(jax.random.fold_in(_gk, 1), (6250, 16), jnp.float32)
        src = jax.random.randint(jax.random.fold_in(_gk, 2), (200000,), 0, 6250, jnp.int32)
        dst = jnp.minimum((6250 * jax.random.uniform(jax.random.fold_in(_gk, 3), (200000,)) ** 2.0).astype(jnp.int32), 99999)
        _o = jnp.argsort(dst, stable=True)
        src = src[_o]
        dst = dst[_o]
        edge_attr_16 = -3.57403e-05 + 0.999761 * jax.random.normal(jax.random.fold_in(_gk, 12), (200000, 16), jnp.float32)
        edge_attr_8 = -5.3897e-05 + 0.999841 * jax.random.normal(jax.random.fold_in(_gk, 13), (200000, 8), jnp.float32)
        node_vec1 = -0.00472126 + 0.997171 * jax.random.normal(jax.random.fold_in(_gk, 15), (6250, 1), jnp.float32)
        return (x, src, dst, edge_attr_16, edge_attr_8, node_vec1)
    x, src, dst, edge_attr_16, edge_attr_8, node_vec1 = _rec_inputs()

    def _L0_gnn_setup():
        import jax, jax.numpy as jnp
        import numpy as np
        N_NODES = 6250
        N_EDGES = 200000
        D_NODE = 16
        D_EDGE = 8
        D_HIDDEN = 16
        key = jax.random.key(seed)
        ks = jax.random.split(key, 8)
        node_features = jax.random.normal(ks[0], (N_NODES, D_NODE), dtype=jnp.float32)
        edge_attr_e3nn = jax.random.normal(ks[1], (N_EDGES, D_EDGE), dtype=jnp.float32)
        node_attr_scalar_raw = jax.random.normal(ks[2], (N_NODES, 1), dtype=jnp.float32)
        W_msg_tp = jax.random.normal(ks[3], (D_NODE, D_EDGE, D_HIDDEN), dtype=jnp.float32)
        W_msg_lin = jax.random.normal(ks[4], (D_HIDDEN, D_HIDDEN), dtype=jnp.float32)
        W_upd_tp = jax.random.normal(ks[5], (D_NODE, D_HIDDEN, D_HIDDEN), dtype=jnp.float32)
        W_upd_lin = jax.random.normal(ks[6], (D_HIDDEN, D_NODE), dtype=jnp.float32)
        edge_index = jax.random.randint(ks[7], (2, N_EDGES), 0, N_NODES, dtype=jnp.int64)
        return {'node_features': node_features, 'edge_attr_e3nn': edge_attr_e3nn, 'node_attr_scalar_raw': node_attr_scalar_raw, 'W_msg_tp': W_msg_tp, 'W_msg_lin': W_msg_lin, 'W_upd_tp': W_upd_tp, 'W_upd_lin': W_upd_lin, 'edge_index': edge_index}
    _L0_gnn_all = _L0_gnn_setup()
    _L0_gnn_in = {k: v for k, v in _L0_gnn_all.items() if k in ('W_msg_tp', 'W_msg_lin', 'W_upd_tp', 'W_upd_lin')}
    del _L0_gnn_all

    def _L1_gnn_setup():
        import jax, jax.numpy as jnp
        import numpy as np
        N_NODES = 1875
        N_EDGES = 18750
        IN_FEATS = 16
        OUT_FEATS = 16
        EDGE_DIM = 16
        key = jax.random.key(seed)
        ks = jax.random.split(key, 8)
        feat = jax.random.normal(ks[0], (N_NODES, IN_FEATS), dtype=jnp.float32)
        efeat = jax.random.normal(ks[1], (N_EDGES, EDGE_DIM), dtype=jnp.float32)
        W_msg = jax.random.normal(ks[2], (EDGE_DIM, IN_FEATS * OUT_FEATS), dtype=jnp.float32) * 0.1
        b_msg = jnp.zeros((IN_FEATS * OUT_FEATS,), dtype=jnp.float32)
        W_attn = jax.random.normal(ks[3], (EDGE_DIM, IN_FEATS * OUT_FEATS), dtype=jnp.float32) * 0.1
        b_attn = jnp.zeros((IN_FEATS * OUT_FEATS,), dtype=jnp.float32)
        src = jax.random.randint(ks[4], (N_EDGES,), 0, N_NODES, dtype=jnp.int32)
        dst = jax.random.randint(ks[5], (N_EDGES,), 0, N_NODES, dtype=jnp.int32)
        return {'feat': feat, 'efeat': efeat, 'W_msg': W_msg, 'b_msg': b_msg, 'W_attn': W_attn, 'b_attn': b_attn, 'src': src, 'dst': dst}
    _L1_gnn_all = _L1_gnn_setup()
    _L1_gnn_in = {k: v for k, v in _L1_gnn_all.items() if k in ('W_msg', 'b_msg', 'W_attn', 'b_attn')}
    del _L1_gnn_all
    return {'x': x, 'src': src, 'dst': dst, 'edge_attr_16': edge_attr_16, 'edge_attr_8': edge_attr_8, 'node_vec1': node_vec1, 'L0_gnn_W_msg_tp': _L0_gnn_in['W_msg_tp'], 'L0_gnn_W_msg_lin': _L0_gnn_in['W_msg_lin'], 'L0_gnn_W_upd_tp': _L0_gnn_in['W_upd_tp'], 'L0_gnn_W_upd_lin': _L0_gnn_in['W_upd_lin'], 'L1_gnn_W_msg': _L1_gnn_in['W_msg'], 'L1_gnn_b_msg': _L1_gnn_in['b_msg'], 'L1_gnn_W_attn': _L1_gnn_in['W_attn'], 'L1_gnn_b_attn': _L1_gnn_in['b_attn']}

def reference(x, src, dst, edge_attr_16, edge_attr_8, node_vec1, L0_gnn_W_msg_tp, L0_gnn_W_msg_lin, L0_gnn_W_upd_tp, L0_gnn_W_upd_lin, L1_gnn_W_msg, L1_gnn_b_msg, L1_gnn_W_attn, L1_gnn_b_attn):
    import jax
    import jax.numpy as jnp

    def _L0_gnn_ref(node_features, edge_attr_e3nn, node_attr_scalar_raw, W_msg_tp, W_msg_lin, W_upd_tp, W_upd_lin, edge_index):
        import jax, jax.numpy as jnp
        import numpy as np
        N_NODES = 6250
        N_EDGES = 200000
        D_NODE = 16
        D_EDGE = 8
        D_HIDDEN = 16
        n_nodes = node_features.shape[0]
        row = edge_index[0]
        col = edge_index[1]
        norm_msg_tp = 1.0 / np.float32(np.sqrt(D_NODE * D_EDGE))
        norm_upd_tp = 1.0 / np.float32(np.sqrt(D_NODE * D_HIDDEN))
        norm_lin = 1.0 / np.float32(np.sqrt(D_HIDDEN))
        x_j = node_features[col]
        m = jnp.einsum('ei,ej,ijh->eh', x_j, edge_attr_e3nn, W_msg_tp) * norm_msg_tp
        m = jax.nn.silu(m)
        m = m @ W_msg_lin * norm_lin
        agg = jax.ops.segment_sum(m, row, num_segments=n_nodes)
        u = jnp.einsum('ni,nh,ihk->nk', node_features, agg, W_upd_tp) * norm_upd_tp
        u = jax.nn.silu(u)
        u = u @ W_upd_lin * norm_lin
        return node_features + u

    def _L1_gnn_ref(feat, efeat, W_msg, b_msg, W_attn, b_attn, src, dst):
        import jax, jax.numpy as jnp
        import numpy as np
        N_NODES = 1875
        N_EDGES = 18750
        IN_FEATS = 16
        OUT_FEATS = 16
        EDGE_DIM = 16
        N, in_f = feat.shape
        E = efeat.shape[0]
        w_m = (efeat @ W_msg + b_msg).reshape(E, in_f, -1)
        w_a = (efeat @ W_attn + b_attn).reshape(E, in_f, -1)
        h_src = feat[src][:, :, None]
        e1 = w_m * h_src
        e2 = w_a * h_src
        seg_max = jax.ops.segment_max(e2, dst, num_segments=N)
        ex = jnp.exp(e2 - seg_max[dst])
        denom = jax.ops.segment_sum(ex, dst, num_segments=N)
        attn = ex / denom[dst]
        ft = jax.ops.segment_sum(e1 * attn, dst, num_segments=N)
        return ft.sum(axis=1)
    edge_index = jnp.stack([src, dst])
    x = _layernorm(x + _L0_gnn_ref(x, edge_attr_8, node_vec1, L0_gnn_W_msg_tp, L0_gnn_W_msg_lin, L0_gnn_W_upd_tp, L0_gnn_W_upd_lin, edge_index), axis=-1)
    x = _layernorm(x + _L1_gnn_ref(x, edge_attr_16, L1_gnn_W_msg, L1_gnn_b_msg, L1_gnn_W_attn, L1_gnn_b_attn, src, dst), axis=-1)
    return x

_drawn_inputs = setup_inputs


def setup_inputs(seed=0):
    import zlib

    import numpy as np

    out = dict(_drawn_inputs(seed))
    spreads = {'L1_gnn_b_msg': (0.0, 0.1), 'L1_gnn_b_attn': (0.0, 0.1)}
    factors = {}
    for name, (base, spread) in spreads.items():
        noise = np.random.default_rng([zlib.crc32(name.encode()), seed]).standard_normal(out[name].shape)
        drawn = base * np.exp(spread * noise) if base else spread * noise
        out[name] = jnp.asarray(drawn.astype(out[name].dtype))
    for name, factor in factors.items():
        out[name] = (out[name] * factor).astype(out[name].dtype)
    return out
```

```python
from contextlib import ExitStack

import concourse.bass as bass
from concourse import mybir

F32 = mybir.dt.float32
F16 = mybir.dt.float16
BF16 = mybir.dt.bfloat16
I32 = mybir.dt.int32
ALU = mybir.AluOpType
ACT = mybir.ActivationFunctionType
AX = mybir.AxisListType.X

N = 6250
E = 200000
D = 16
DE = 8
P = 125
CH = E // P
J = 8
NBLK = CH // J
LO = 8
HI = -(-N // LO)
NB = -(-HI // 128)
NG = NB * LO
NPAD = NB * 128 * LO
HIP = NB * 128
C = D * D
HEAD, TAIL = NPAD, NPAD + 128
ROWS = NPAD + 256
SKIP = ROWS
BIG = 1.0e38
Q = 4
EPS = 1e-5
FULL = N // (128 * LO)
REST = (N - FULL * 128 * LO) // LO
LAST = N - FULL * 128 * LO - REST * LO
CUT = 512


def gnn(nc, x, src, dst, ea16, ea8, node_vec1, Wmt, Wml, Wut, Wul, Wm, bm, Wa, ba, out):
    ctx = ExitStack()
    with ctx:
        def sb(name, shape, dt=F32):
            return ctx.enter_context(nc.sbuf_tensor(name, shape, dt))

        def sem(name):
            return ctx.enter_context(nc.semaphore(name))

        btab = nc.dram_tensor("btab", (NPAD, DE * D), F32, kind="Internal").ap()
        x1tab = nc.dram_tensor("x1tab", (NPAD, D), F32, kind="Internal").ap()
        rtab = nc.dram_tensor("rtab", (ROWS, 3 * C), F32, kind="Internal").ap()
        meta0 = nc.dram_tensor("meta0", (P, NBLK, 3 * J), I32, kind="Internal").ap()
        meta1 = nc.dram_tensor("meta1", (P, NBLK, 4 * J), I32, kind="Internal").ap()

        ident = sb("ident", [128, 128])
        ones = sb("ones", [128, 128])
        iota_i = sb("iota_i", [128, HI + 16], I32)
        iota_hi = sb("iota_hi", [128, HI], F16)
        iota_lo = sb("iota_lo", [128, LO])
        iota_p = sb("iota_p", [128, 3])
        xa = sb("xa", [128, NB, LO, D])
        y = sb("y", [128, NB, LO, D])
        yc = sb("yc", [128, NB, LO, D])
        stat = sb("stat", [128, 3, NG])
        w0 = sb("w0", [D, DE * D])
        wu = sb("wu", [D, C])
        wlin = sb("wlin", [128, 128])
        wul = sb("wul", [128, 128])
        w1 = sb("w1", [D + 1, 2, C])
        ends = sb("ends", [P, 8])
        endi = sb("endi", [P, 4], I32)

        consts_made = sem("consts_made")
        inputs_in = sem("inputs_in")
        index_in = sem("index_in")
        meta_step = sem("meta_step")
        meta_out = sem("meta_out")
        xt_made = sem("xt_made")
        xt_copied = sem("xt_copied")
        b_made = sem("b_made")
        b_copied = sem("b_copied")
        btab_out = [sem(f"btab_out{h}") for h in range(2)]
        table_cleared = sem("table_cleared")
        zero_made = sem("zero_made")
        x1_out = sem("x1_out")
        out_out = sem("out_out")

        with ExitStack() as st:
            def tsb(name, shape, dt=F32):
                return st.enter_context(nc.sbuf_tensor(name, shape, dt))

            xt = ctx.enter_context(nc.sbuf_tensor("xt", [D, NG, 128], F32))
            srci = tsb("srci", [P, CH], I32)
            dsti = tsb("dsti", [P, CH], I32)
            dstf = tsb("dstf", [P, CH])
            ta = tsb("ta", [P, CH])
            tb = tsb("tb", [P, CH])
            m0 = tsb("m0", [P, NBLK, 3 * J], I32)
            m1 = tsb("m1", [P, NBLK, 4 * J], I32)
            bst = tsb("bst", [128, 2, LO, DE * D])
            pt = st.enter_context(nc.psum_tensor("pt", [128, 2, CUT], F32))
            pb = st.enter_context(nc.psum_tensor("pb", [128, 2, 2, CUT], F32))
            zrow = tsb("zrow", [128, 4 * 3 * C])
            hrow = tsb("hrow", [128, 3 * C])

            blk0 = m0[:, :, :].rearrange("p b (a j) -> p a b j", a=3)
            blk1 = m1[:, :, :].rearrange("p b (a j) -> p a b j", a=4)
            bj = lambda t: t[:, :].rearrange("p (b j) -> p b j", j=J)
            block = st.enter_context(nc.Block())

            @block.sync
            def _(sp):
                sp.dma_start(srci[:, :], src.rearrange("(p j) -> p j", p=P)).then_inc(index_in, 16)
                sp.dma_start(dsti[:, :], dst.rearrange("(p j) -> p j", p=P)).then_inc(index_in, 16)
                sp.wait_ge(consts_made, 8)
                sp.dma_start(endi[0:P - 1, :],
                             dst.rearrange("(p j) -> p j", p=P)[1:P, 0:4]).then_inc(index_in, 16)
                nfull = FULL * 128 * LO
                sp.dma_start(xa[:, 0:FULL, :, :].rearrange("p b l c -> p b (l c)"),
                             x[0:nfull, :].rearrange("(b p l) c -> p b (l c)", p=128, l=LO)).then_inc(inputs_in, 16)
                sp.dma_start(xa[0:REST, FULL, :, :].rearrange("p l c -> p (l c)"),
                             x[nfull:nfull + REST * LO, :].rearrange("(p l) c -> p (l c)", l=LO)).then_inc(inputs_in, 16)
                sp.dma_start(xa[REST:REST + 1, FULL, 0:LAST, :].rearrange("p l c -> p (l c)"),
                             x[N - LAST:N, :].rearrange("(p l) c -> p (l c)", l=LAST)).then_inc(inputs_in, 16)
                sp.dma_start(w0[:, :], Wmt.rearrange("i j h -> i (j h)")).then_inc(inputs_in, 16)
                sp.dma_start(wu[:, :], Wut.rearrange("i h k -> i (h k)")).then_inc(inputs_in, 16)
                for l in range(LO):
                    s = slice(l * D, (l + 1) * D)
                    sp.dma_start(wlin[s, s], Wml).then_inc(inputs_in, 16)
                    sp.dma_start(wul[s, s], Wul).then_inc(inputs_in, 16)
                for n, (w, b) in enumerate(((Wa, ba), (Wm, bm))):
                    sp.dma_start(w1[0:D, n, :], w).then_inc(inputs_in, 16)
                    sp.dma_start(w1[D:D + 1, n, :], b.rearrange("(a c) -> a c", a=1)).then_inc(inputs_in, 16)
                sp.wait_ge(meta_step, 14)
                sp.dma_start(meta0, m0[:, :, :]).then_inc(meta_out, 16)
                sp.dma_start(meta1, m1[:, :, :]).then_inc(meta_out, 16)
                for b in range(NB):
                    sp.wait_ge(b_copied, 2 * (b + 1))
                    sp.dma_start(btab[b * 128 * LO:(b + 1) * 128 * LO, :].rearrange("(p l) c -> p (l c)", l=LO),
                                 bst[:, b % 2, :, :].rearrange("p l c -> p (l c)")).then_inc(btab_out[b % 2], 16)
                for h in range(2):
                    sp.wait_ge(btab_out[h], 16 * ((NB + 1 - h) // 2))
                sp.wait_ge(meta_out, 32)
                sp.wait_ge(inputs_in, 16 * (5 + 2 * LO + 4))

            @block.gpsimd
            def _(g):
                g.iota(iota_i[:, 0:HI], [[1, HI]], base=0, channel_multiplier=0).then_inc(consts_made, 1)
                g.iota(iota_i[:, HI:HI + 1], [[1, 1]], base=HEAD, channel_multiplier=1).then_inc(consts_made, 1)
                g.memset(ident[:, :], 0.0).then_inc(zero_made, 1)
                g.wait_ge(zero_made, 1)
                g.affine_select(out=ident[:, :], in_=ident[:, :], compare_op=ALU.not_equal, fill=1.0, base=0,
                                pattern=[[-1, 128]], channel_multiplier=1).then_inc(consts_made, 1)
                g.memset(xa[:, :, :, :], 0.0).then_inc(consts_made, 1)
                g.memset(wlin[:, :], 0.0).then_inc(consts_made, 1)
                g.memset(wul[:, :], 0.0).then_inc(consts_made, 1)
                g.memset(ones[:, :], 1.0).then_inc(consts_made, 1)
                g.memset(endi[:, :], -1).then_inc(consts_made, 1)
                g.memset(zrow[:, :], 0.0).then_inc(zero_made, 1)
                g.memset(hrow[:, 0:C], -BIG).then_inc(zero_made, 1)
                g.memset(hrow[:, C:3 * C], 0.0).then_inc(zero_made, 1)

            @block.vector
            def _(v):
                v.wait_ge(consts_made, 2)
                v.tensor_copy(iota_hi[:, :], iota_i[:, 0:HI]).then_inc(meta_step, 1)
                v.tensor_copy(iota_lo[:, :], iota_i[:, 0:LO]).then_inc(meta_step, 1)
                v.tensor_copy(iota_p[:, 0:1], iota_i[:, HI:HI + 1]).then_inc(meta_step, 1)
                v.wait_ge(index_in, 48)
                v.tensor_copy(dstf[:, :], dsti[:, :]).then_inc(meta_step, 1)
                v.tensor_copy(blk0[:, 0], bj(dsti)).then_inc(meta_step, 1)
                v.tensor_scalar(blk0[:, 1], bj(srci), 3, None, ALU.logical_shift_right).then_inc(meta_step, 1)
                v.tensor_scalar(blk0[:, 2], bj(srci), LO - 1, None, ALU.bitwise_and).then_inc(meta_step, 1)
                v.tensor_copy(blk1[:, 0], bj(srci)).then_inc(meta_step, 1)
                v.wait_ge(meta_step, 8)
                v.memset(ta[:, 0:1], 1.0)
                v.tensor_tensor(ta[:, 1:CH], dstf[:, 1:CH], dstf[:, 0:CH - 1], ALU.not_equal)
                v.tensor_scalar(tb[:, :], dstf[:, :], dstf[:, 0:1], None, ALU.is_equal).then_inc(meta_step, 1)
                v.wait_ge(meta_step, 9)
                v.tensor_scalar(blk1[:, 2].bitcast(F32), bj(ta), -BIG, None, ALU.mult)
                v.tensor_scalar(blk1[:, 3].bitcast(F32), bj(ta), -1.0, 1.0, ALU.mult, ALU.add)
                v.tensor_scalar(ends[:, 0:1], dstf[:, 0:1], 1.0, None, ALU.mult)
                v.tensor_scalar(ends[:, 1:2], dstf[:, CH - 1:CH], 1.0, None, ALU.mult)
                v.tensor_scalar(ends[:, 2:3], endi[0:P, 0:1], 1.0, None, ALU.mult)
                v.tensor_scalar(ends[:, 3:4], dstf[:, 0:1], -1.0, iota_p[0:P, 0:1], ALU.mult, ALU.add)
                v.tensor_scalar(iota_p[:, 1:2], iota_p[:, 0:1], 128.0, None, ALU.add).then_inc(meta_step, 1)
                v.wait_ge(meta_step, 10)
                v.scalar_tensor_tensor(out=tb[:, :], in0=tb[:, :], scalar=ends[:, 3:4], in1=dstf[:, :],
                                       op0=ALU.mult, op1=ALU.add).then_inc(meta_step, 1)
                v.wait_ge(meta_step, 11)
                v.tensor_scalar(tb[:, :], tb[:, :], -float(SKIP), None, ALU.add).then_inc(meta_step, 1)
                v.wait_ge(meta_step, 12)
                v.tensor_tensor(tb[:, 0:CH - 1], tb[:, 0:CH - 1], ta[:, 1:CH], ALU.mult)
                v.tensor_scalar(tb[:, CH - 1:CH], iota_p[0:P, 1:2], -float(SKIP), None, ALU.add).then_inc(meta_step, 1)
                v.wait_ge(meta_step, 13)
                v.tensor_scalar(blk1[:, 1], bj(tb), float(SKIP), None, ALU.add).then_inc(meta_step, 1)

            @block.tensor
            def _(pe):
                pe.wait_ge(inputs_in, 16 * (5 + 2 * LO + 4))
                pe.wait_ge(consts_made, 8)
                for s in range(NG // 4):
                    if s >= 2:
                        pe.wait_ge(xt_copied, s - 1)
                    for r in range(4):
                        g = 4 * s + r
                        ins = pe.transpose(pt[0:D, s % 2, r * 128:(r + 1) * 128], xa[:, g // LO, g % LO, :], ident[:, :])
                    ins.then_inc(xt_made, 1)
                for s in range(NG // 4):
                    pe.wait_ge(xt_copied, s + 1)
                    if s >= 4:
                        pe.wait_ge(b_copied, s - 3)
                    for r in range(4):
                        ins = pe.matmul(pb[:, (s // 2) % 2, s % 2, r * 128:(r + 1) * 128], xt[:, 4 * s + r, :], w0[:, :],
                                        start=True, stop=True)
                    ins.then_inc(b_made, 1)

            @block.scalar
            def _(act):
                for s in range(NG // 4):
                    act.wait_ge(xt_made, s + 1)
                    act.copy(xt[:, 4 * s:4 * s + 4, :].rearrange("c g n -> c (g n)"), pt[0:D, s % 2, :]).then_inc(xt_copied, 1)
                for s in range(NG // 4):
                    act.wait_ge(b_made, s + 1)
                    if s >= 4:
                        act.wait_ge(btab_out[(s // 2) % 2], 16 * (s // 4))
                    act.copy(bst[:, (s // 2) % 2, (s % 2) * 4:(s % 2) * 4 + 4, :].rearrange("p l c -> p (l c)"),
                             pb[:, (s // 2) % 2, s % 2, :]).then_inc(b_copied, 1)
                act.wait_ge(zero_made, 4)
                per = NPAD // 128
                view = rtab[0:NPAD, :].rearrange("(p r) c -> p (r c)", p=128)
                for r in range(per // 4):
                    act.dma_start(view[:, r * 12 * C:(r + 1) * 12 * C], zrow[:, :]).then_inc(table_cleared, 16)
                act.dma_start(rtab[HEAD:HEAD + 128, :], hrow[:, :]).then_inc(table_cleared, 16)
                act.dma_start(rtab[TAIL:TAIL + 128, :], hrow[:, :]).then_inc(table_cleared, 16)
                act.wait_ge(table_cleared, 16 * (per // 4 + 2))

        aggt = sb("aggt", [128, HIP])
        with ExitStack() as st:
            def tsb(name, shape, dt=F32):
                return st.enter_context(nc.sbuf_tensor(name, shape, dt))

            mt = tsb("mt", [P, 2, 3, J], I32)
            hilo = tsb("hilo", [P, 2, 2, J])
            e8 = tsb("e8", [P, 2, J, DE])
            bg = tsb("bg", [P, 2, J, DE * D])
            msg = tsb("msg", [P, 2, J, D])
            sact = tsb("sact", [P, 2, J, D])
            s1 = tsb("s1", [P, 2, J, D], BF16)
            s2 = tsb("s2", [P, 2, J, D], BF16)
            s3 = tsb("s3", [P, 2, J, D], BF16)
            res = tsb("res", [P, 2, J, D])
            ohl = tsb("ohl", [P, 2, J, LO], BF16)
            stt = tsb("stt", [P, 2, 3, J, LO, D], BF16)
            ohh = tsb("ohh", [P, 2, J, HI], BF16)
            zb = tsb("zb", [P, CUT], BF16)
            pagg = st.enter_context(nc.psum_tensor("pagg", [128, 2, CUT], F32))

            loaded = [sem(f"l0_loaded{h}") for h in range(2)]
            gathered = [sem(f"l0_gathered{h}") for h in range(2)]
            z_done = sem("l0_z_done")
            msg_done = sem("l0_msg_done")
            hilo_done = sem("l0_hilo_done")
            act_done = sem("l0_act_done")
            res_done = sem("l0_res_done")
            s2_done = sem("l0_s2_done")
            s3_done = sem("l0_s3_done")
            ohl_done = sem("l0_ohl_done")
            stt_done = sem("l0_stt_done")
            ohh_done = sem("l0_ohh_done")
            used = sem("l0_used")
            zeroed = sem("l0_zeroed")
            summed = sem("l0_summed")
            agg_copied = sem("agg_copied")
            block = st.enter_context(nc.Block())

            @block.sync
            def _(sp):
                def load(k, h):
                    sp.dma_start(mt[:, h, :, :].rearrange("p a j -> p (a j)"),
                                 meta0.rearrange("p b c -> p (b c)")[:, bass.ds(k * 3 * J, 3 * J)]).then_inc(loaded[h], 16)
                    sp.dma_start(e8[:, h, :, :].rearrange("p j c -> p (j c)"),
                                 ea8.rearrange("(p j) c -> p (j c)", p=P)[:, bass.ds(k * J * DE, J * DE)]).then_inc(loaded[h], 16)

                load(0, 0)
                load(1, 1)
                with sp.Fori(0, NBLK // 2 - 1) as t:
                    for h in range(2):
                        sp.wait_ge(z_done, 2 * t + h + 1)
                        sp.nop(nofuse=True)
                        sp.wait_ge(hilo_done, 2 * t + h + 1)
                        sp.nop(nofuse=True)
                        load(2 * t + h + 2, h)

            @block.gpsimd
            def _(g):
                def gather(k, h, t):
                    g.wait_ge(loaded[h], 32 * (t + 1))
                    if not isinstance(t, int):
                        g.wait_ge(msg_done, k - 1)
                    g.nop(nofuse=True)
                    for i in range(J):
                        g.indirect_dma_start(bg[:, h, i, :], None, btab,
                                             bass.IndirectOffsetOnAxis(ap=mt[:, h, 0, i:i + 1], axis=0)).then_inc(gathered[h], 16)

                gather(0, 0, 0)
                gather(1, 1, 0)
                with g.Fori(1, NBLK // 2) as t:
                    for h in range(2):
                        gather(2 * t + h, h, t)

            @block.vector
            def _(v):
                v.memset(zb[:, :], 0.0).then_inc(zeroed, 1)
                v.sem_inc(used, 2)

                def messages(k, h, t):
                    v.wait_ge(gathered[h], 16 * J * (t + 1))
                    z = bg[:, h, :, :].rearrange("p s (j h) -> p s j h", j=DE)
                    v.tensor_tensor(z, z, e8[:, h, :, :].unsqueeze(3).to_broadcast([P, J, DE, D]), ALU.mult).then_inc(z_done, 1)
                    v.wait_ge(z_done, k + 1)
                    v.tensor_copy(hilo[:, h, :, :], mt[:, h, 1:3, :]).then_inc(hilo_done, 1)
                    v.tensor_reduce(msg[:, h, :, :], bg[:, h, :, :].rearrange("p s (j h) -> p s h j", j=DE), AX,
                                    ALU.add).then_inc(msg_done, 1)

                def stationaries(k, h):
                    v.wait_ge(hilo_done, k + 1)
                    v.wait_ge(used, k + 1)
                    v.tensor_tensor(ohl[:, h, :, :], iota_lo[0:P, :].unsqueeze(1).to_broadcast([P, J, LO]),
                                    hilo[:, h, 1, :].unsqueeze(2).to_broadcast([P, J, LO]), ALU.is_equal).then_inc(ohl_done, 1)
                    v.wait_ge(act_done, 2 * k + 2)
                    v.tensor_tensor(res[:, h, :, :], sact[:, h, :, :], s1[:, h, :, :], ALU.subtract).then_inc(res_done, 1)
                    for i in range(J):
                        v.tensor_scalar(ohh[:, h, i, :], iota_hi[0:P, :], hilo[:, h, 0, i:i + 1], None,
                                        ALU.is_equal).then_inc(ohh_done, 1)
                        if i == 0:
                            v.wait_ge(res_done, k + 1)
                            v.tensor_copy(s2[:, h, :, :], res[:, h, :, :]).then_inc(s2_done, 1)
                        if i == 2:
                            v.wait_ge(s2_done, k + 1)
                            v.tensor_tensor(s3[:, h, :, :], res[:, h, :, :], s2[:, h, :, :], ALU.subtract).then_inc(s3_done, 1)
                        if i == 1:
                            v.wait_ge(ohl_done, k + 1)
                        if i in (3, 4, 5):
                            part = (s1, s2, s3)[i - 3]
                            if i == 5:
                                v.wait_ge(s3_done, k + 1)
                            v.tensor_tensor(stt[:, h, i - 3, :, :, :],
                                            part[:, h, :, :].unsqueeze(2).to_broadcast([P, J, LO, D]),
                                            ohl[:, h, :, :].unsqueeze(3).to_broadcast([P, J, LO, D]),
                                            ALU.mult).then_inc(stt_done, 1)

                def pair(t):
                    messages(2 * t + 1, 1, t)
                    stationaries(2 * t, 0)
                    messages(2 * t + 2, 0, t + 1)
                    stationaries(2 * t + 1, 1)

                messages(0, 0, 0)
                with v.Fori(0, NBLK // 2 - 1) as t:
                    pair(t)
                messages(NBLK - 1, 1, NBLK // 2 - 1)
                stationaries(NBLK - 2, 0)
                stationaries(NBLK - 1, 1)
                v.memset(aggt[:, HI:HIP], 0.0)
                v.wait_ge(summed, 1)
                v.tensor_copy(aggt[:, 0:CUT], pagg[:, 0, :]).then_inc(agg_copied, 1)
                v.tensor_copy(aggt[:, CUT:HI], pagg[:, 1, 0:HI - CUT]).then_inc(agg_copied, 1)

            @block.scalar
            def _(act):
                with act.Fori(0, NBLK // 2) as t:
                    for h in range(2):
                        k = 2 * t + h
                        act.wait_ge(msg_done, k + 1)
                        act.activation(sact[:, h, :, :], msg[:, h, :, :], ACT.Silu, scale=float((D * DE) ** -0.5)).then_inc(act_done, 1)
                        act.activation(s1[:, h, :, :], msg[:, h, :, :], ACT.Silu, scale=float((D * DE) ** -0.5)).then_inc(act_done, 1)

            @block.tensor
            def _(pe):
                pe.wait_ge(zeroed, 1)
                pe.matmul(pagg[:, 0, :], zb[:, 0:128], zb[:, :], start=True, stop=False, skip_group_check=True)
                pe.matmul(pagg[:, 1, 0:HI - CUT], zb[:, 0:128], zb[:, 0:HI - CUT], start=True, stop=False, skip_group_check=True)
                with pe.Fori(0, NBLK // 2) as t:
                    for h in range(2):
                        k = 2 * t + h
                        pe.wait_ge(stt_done, 3 * k + 3)
                        pe.wait_ge(ohh_done, J * k + J)
                        for i in range(J):
                            for a in range(3):
                                w = stt[:, h, a, i, :, :].rearrange("p l c -> p (l c)")
                                pe.matmul(pagg[:, 0, :], w, ohh[:, h, i, 0:CUT], start=False, stop=False, skip_group_check=True)
                                ins = pe.matmul(pagg[:, 1, 0:HI - CUT], w, ohh[:, h, i, CUT:HI], start=False, stop=False,
                                                skip_group_check=True)
                        ins.then_inc(used, 1)
                pe.matmul(pagg[:, 0, :], zb[:, 0:128], zb[:, :], start=False, stop=True, skip_group_check=True)
                pe.matmul(pagg[:, 1, 0:HI - CUT], zb[:, 0:128], zb[:, 0:HI - CUT], start=False, stop=True,
                          skip_group_check=True).then_inc(summed, 1)

        def layer_norm(v, step, base):
            a = lambda t: t[:, :, :, :].rearrange("p b l c -> p (b l) c")
            v.tensor_reduce(stat[:, 0, :], a(y), AX, ALU.add).then_inc(step, 1)
            v.wait_ge(step, base + 1)
            v.tensor_scalar(stat[:, 1, :], stat[:, 0, :], 1.0 / D, None, ALU.mult).then_inc(step, 1)
            v.wait_ge(step, base + 2)
            v.tensor_tensor(a(yc), a(y), stat[:, 1, :].unsqueeze(2).to_broadcast([128, NG, D]), ALU.subtract).then_inc(step, 1)
            v.wait_ge(step, base + 3)
            v.tensor_tensor(a(y), a(yc), a(yc), ALU.mult).then_inc(step, 1)
            v.wait_ge(step, base + 4)
            v.tensor_reduce(stat[:, 0, :], a(y), AX, ALU.add).then_inc(step, 1)
            v.wait_ge(step, base + 5)
            v.tensor_scalar(stat[:, 1, :], stat[:, 0, :], 1.0 / D, EPS, ALU.mult, ALU.add).then_inc(step, 1)
            return base + 6

        def layer_norm_end(v, step, base, root):
            a = lambda t: t[:, :, :, :].rearrange("p b l c -> p (b l) c")
            v.wait_ge(root, 1)
            v.reciprocal(stat[:, 0, :], stat[:, 2, :]).then_inc(step, 1)
            v.wait_ge(step, base + 1)
            v.tensor_tensor(a(y), a(yc), stat[:, 0, :].unsqueeze(2).to_broadcast([128, NG, D]), ALU.mult).then_inc(step, 1)
            return base + 2

        with ExitStack() as st:
            def tsb(name, shape, dt=F32):
                return st.enter_context(nc.sbuf_tensor(name, shape, dt))

            agg = tsb("agg", [128, NB, LO, D])
            prod = tsb("prod", [128, 2, 2, D, D])
            u = tsb("u", [128, NB, LO, D])
            us = tsb("us", [128, NB, LO, D])
            ut = tsb("ut", [128, NB, 128])
            pa = st.enter_context(nc.psum_tensor("pa", [128, 2, CUT], F32))
            pc = st.enter_context(nc.psum_tensor("pc", [128, 2, CUT], F32))
            pu = st.enter_context(nc.psum_tensor("pu", [128, 2, CUT], F32))
            pv = st.enter_context(nc.psum_tensor("pv", [128, 2, CUT], F32))
            agg_made = sem("agg_made")
            agg_in = sem("agg_in")
            c_made = sem("c_made")
            prod_done = sem("prod_done")
            u_done = sem("u_done")
            us_done = sem("us_done")
            ut_made = sem("ut_made")
            ut_copied = sem("ut_copied")
            v_made = sem("v_made")
            n_step = sem("l0_norm_step")
            n_root = sem("l0_norm_root")
            block = st.enter_context(nc.Block())

            def bank(t, b):
                return t[:, b // 4, (b % 4) * 128:(b % 4) * 128 + 128]

            @block.tensor
            def _(pe):
                for b in range(NB):
                    ins = pe.matmul(bank(pa, b), aggt[:, b * 128:(b + 1) * 128], wlin[:, :], start=True, stop=True)
                ins.then_inc(agg_made, 1)
                for s in range(NG // 2):
                    if s >= 2:
                        pe.wait_ge(prod_done, s - 1)
                    for r in range(2):
                        ins = pe.matmul(pc[:, s % 2, r * C:(r + 1) * C], xt[:, 2 * s + r, :], wu[:, :], start=True, stop=True)
                    ins.then_inc(c_made, 1)
                pe.wait_ge(us_done, 1)
                for b in range(NB):
                    ins = pe.transpose(bank(pu, b), us[:, b, :, :].rearrange("p l c -> p (l c)"), ident[:, :])
                ins.then_inc(ut_made, 1)
                pe.wait_ge(ut_copied, 1)
                for b in range(NB):
                    ins = pe.matmul(bank(pv, b), ut[:, b, :], wul[:, :], start=True, stop=True)
                ins.then_inc(v_made, 1)

            @block.vector
            def _(v):
                flat = lambda t: t[:, :, :, :].rearrange("p b l c -> p (b l c)")
                n = NB * 128
                psum_flat = lambda t: t[:, :, :].rearrange("p a c -> p (a c)")[:, 0:n]
                v.wait_ge(agg_made, 1)
                v.tensor_scalar(flat(agg), psum_flat(pa), D ** -0.5, None, ALU.mult).then_inc(agg_in, 1)
                v.wait_ge(agg_in, 1)
                ag = agg[:, :, :, :].rearrange("p b l c -> p (b l) c")
                uu = u[:, :, :, :].rearrange("p b l c -> p (b l) c")
                for s in range(NG // 2):
                    v.wait_ge(c_made, s + 1)
                    if s >= 2:
                        v.wait_ge(u_done, s - 1)
                    v.tensor_tensor(prod[:, s % 2, :, :, :], pc[:, s % 2, :].rearrange("p (r h k) -> p r h k", r=2, h=D),
                                    ag[:, 2 * s:2 * s + 2, :].unsqueeze(3).to_broadcast([128, 2, D, D]),
                                    ALU.mult).then_inc(prod_done, 1)
                    v.wait_ge(prod_done, s + 1)
                    v.tensor_reduce(uu[:, 2 * s:2 * s + 2, :], prod[:, s % 2, :, :, :].rearrange("p r h k -> p r k h"), AX,
                                    ALU.add).then_inc(u_done, 1)
                v.tensor_scalar(flat(yc), flat(xa), 2.0, None, ALU.mult).then_inc(n_step, 1)
                v.wait_ge(ut_made, 1)
                v.tensor_copy(ut[:, :, :].rearrange("p b c -> p (b c)"), psum_flat(pu)).then_inc(ut_copied, 1)
                v.wait_ge(v_made, 1)
                v.wait_ge(n_step, 1)
                v.scalar_tensor_tensor(out=flat(y), in0=psum_flat(pv), scalar=D ** -0.5, in1=flat(yc), op0=ALU.mult,
                                       op1=ALU.add).then_inc(n_step, 1)
                v.wait_ge(n_step, 2)
                base = layer_norm(v, n_step, 2)
                layer_norm_end(v, n_step, base, n_root)

            @block.scalar
            def _(act):
                act.wait_ge(u_done, NG // 2)
                act.activation(us[:, :, :, :], u[:, :, :, :], ACT.Silu, scale=float((D * D) ** -0.5)).then_inc(us_done, 1)
                act.wait_ge(n_step, 8)
                act.activation(stat[:, 2, :], stat[:, 1, :], ACT.Sqrt).then_inc(n_root, 1)

            @block.sync
            def _(sp):
                sp.wait_ge(n_step, 10)
                sp.dma_start(x1tab.rearrange("(b p l) c -> p b (l c)", p=128, l=LO),
                             y[:, :, :, :].rearrange("p b l c -> p b (l c)")).then_inc(x1_out, 16)
                sp.wait_ge(x1_out, 16)

        with ExitStack() as st:
            def tsb(name, shape, dt=F32):
                return st.enter_context(nc.sbuf_tensor(name, shape, dt))

            mt = tsb("mt1", [P, Q, 4, J], I32)
            e16 = tsb("e16", [P, Q, J, D])
            xg = tsb("xg", [P, Q, J, D])
            et = tsb("et", [D + 1, 2, J, 128])
            state = tsb("state", [P, Q, J, 3, C])
            gap = tsb("gap", [P, C])
            corr = tsb("corr", [P, C])
            carry = tsb("carry", [P, 2, C])
            pt = st.enter_context(nc.psum_tensor("pt1", [128, J, 128], F32))
            pw = st.enter_context(nc.psum_tensor("pw", [128, 4, CUT], F32))

            loaded = [sem(f"l1_loaded{q}") for q in range(Q)]
            gathered = [sem(f"l1_gathered{q}") for q in range(Q)]
            scattered = [sem(f"l1_scattered{q}") for q in range(Q)]
            primed = sem("l1_primed")
            et_made = sem("l1_et_made")
            et_copied = sem("l1_et_copied")
            w_made = sem("l1_w_made")
            w_used = sem("l1_w_used")
            fwd = sem("l1_fwd")
            bwd = sem("l1_bwd")
            gap_done = sem("l1_gap_done")
            less = sem("l1_less")
            exped = sem("l1_exped")
            corr_done = sem("l1_corr_done")
            p_done = sem("l1_p_done")
            carried = sem("l1_carried")
            st_done = sem("l1_st_done")
            block = st.enter_context(nc.Block())
            H = J // 2

            @block.sync
            def _(sp):
                def load(k, q):
                    sp.dma_start(mt[:, q, :, :].rearrange("p a j -> p (a j)"),
                                 meta1.rearrange("p b c -> p (b c)")[:, bass.ds(k * 4 * J, 4 * J)]).then_inc(loaded[q], 16)
                    sp.dma_start(e16[:, q, :, :].rearrange("p j c -> p (j c)"),
                                 ea16.rearrange("(p j) c -> p (j c)", p=P)[:, bass.ds(k * J * D, J * D)]).then_inc(loaded[q], 16)

                for q in range(Q):
                    load(q, q)
                with sp.Fori(0, NBLK // Q - 1) as t:
                    for q in range(Q):
                        sp.wait_ge(scattered[q], 16 * J * (t + 1))
                        sp.nop(nofuse=True)
                        sp.wait_ge(et_made, Q * t + q + 1)
                        sp.nop(nofuse=True)
                        load(Q * t + q + Q, q)

            @block.gpsimd
            def _(g):
                g.memset(state[:, Q - 1, J - 1, :, :], 0.0).then_inc(primed, 1)
                g.memset(et[:, :, :, :], 1.0).then_inc(primed, 1)

                def gather(k, q, t):
                    g.wait_ge(loaded[q], 32 * (t + 1))
                    g.nop(nofuse=True)
                    for i in range(J):
                        g.indirect_dma_start(xg[:, q, i, :], None, x1tab,
                                             bass.IndirectOffsetOnAxis(ap=mt[:, q, 0, i:i + 1], axis=0)).then_inc(gathered[q], 16)

                def scatter(k, q):
                    for i in range(J):
                        g.wait_ge(st_done, J * k + i + 1)
                        g.nop(nofuse=True)
                        g.indirect_dma_start(rtab, bass.IndirectOffsetOnAxis(ap=mt[:, q, 1, i:i + 1], axis=0),
                                             state[:, q, i, :, :].rearrange("p a c -> p (a c)"), None,
                                             bounds_check=ROWS - 1, oob_is_err=False).then_inc(scattered[q], 16)

                gather(0, 0, 0)
                gather(1, 1, 0)
                with g.Fori(0, NBLK // Q - 1) as t:
                    for q in range(Q):
                        gather(Q * t + q + 2, (q + 2) % Q, t + (q + 2) // Q)
                        scatter(Q * t + q, q)
                last = NBLK - Q
                for q in range(Q):
                    if q + 2 < Q:
                        gather(last + q + 2, q + 2, NBLK // Q - 1)
                    scatter(last + q, q)
                for q in range(Q):
                    g.wait_ge(scattered[q], 16 * J * (NBLK // Q))

            @block.tensor
            def _(pe):
                def products(k, q):
                    pe.wait_ge(et_copied, k + 1)
                    for i in range(J):
                        pe.wait_ge(w_used, J * k + i + 1)
                        ins = pe.matmul(pw[0:P, i % 4, :], et[:, q % 2, i, 0:P],
                                        w1[:, :, :].rearrange("k a c -> k (a c)"), start=True, stop=True)
                        ins.then_inc(w_made, 1)

                pe.wait_ge(primed, 2)
                pe.wait_ge(loaded[0], 32)
                for i in range(J):
                    ins = pe.transpose(pt[0:D, i, 0:P], e16[:, 0, i, :], ident[0:P, 0:P])
                ins.then_inc(et_made, 1)
                with pe.Fori(0, NBLK // Q - 1) as t:
                    for q in range(Q):
                        k = Q * t + q
                        pe.wait_ge(et_copied, k + 1)
                        turn_q, turn_t = (q + 1) % Q, t + (q + 1) // Q
                        pe.wait_ge(loaded[turn_q], 32 * (turn_t + 1))
                        for i in range(J):
                            ins = pe.transpose(pt[0:D, i, 0:P], e16[:, turn_q, i, :], ident[0:P, 0:P])
                        ins.then_inc(et_made, 1)
                        products(k, q)
                for q in range(Q):
                    k = NBLK - Q + q
                    pe.wait_ge(et_copied, k + 1)
                    if q + 1 < Q:
                        pe.wait_ge(loaded[q + 1], 32 * (NBLK // Q))
                        for i in range(J):
                            ins = pe.transpose(pt[0:D, i, 0:P], e16[:, q + 1, i, :], ident[0:P, 0:P])
                        ins.then_inc(et_made, 1)
                    products(k, q)

            @block.scalar
            def _(act):
                act.wait_ge(primed, 2)

                def copy_et(k, q):
                    act.wait_ge(et_made, k + 1)
                    if not (isinstance(k, int) and k == 0):
                        act.wait_ge(w_made, J * (k - 1) + 1)
                    act.copy(et[0:D, q % 2, :, 0:P], pt[0:D, :, 0:P]).then_inc(et_copied, 1)

                def exps(k, q):
                    act.wait_ge(gap_done, k + 1)
                    act.wait_ge(carried, k + 1)
                    act.activation(corr[:, :], gap[:, :], ACT.Exp).then_inc(corr_done, 1)
                    for b in range(2):
                        act.wait_ge(less, 2 * k + b + 1)
                        s = state[:, q, b * H:(b + 1) * H, 1, :]
                        act.activation(s, s, ACT.Exp).then_inc(exped, 1)

                copy_et(0, 0)
                with act.Fori(0, NBLK // Q - 1) as t:
                    for q in range(Q):
                        copy_et(Q * t + q + 1, q + 1)
                        exps(Q * t + q, q)
                for q in range(Q):
                    if q + 1 < Q:
                        copy_et(NBLK - Q + q + 1, q + 1)
                    exps(NBLK - Q + q, q)

            @block.vector
            def _(v):
                v.sem_inc(w_used, 4)
                v.sem_inc(carried, 1)
                v.wait_ge(primed, 2)

                def mask(q, row, i):
                    return mt[:, q, row, i:i + 1].bitcast(F32)

                def edge(k, q, i):
                    v.wait_ge(w_made, J * k + i + 1)
                    v.tensor_tensor(state[:, q, i, 1:3, :].rearrange("p a (i o) -> p a i o", i=D),
                                    pw[0:P, i % 4, :].rearrange("p (a i o) -> p a i o", a=2, i=D),
                                    xg[:, q, i, :].unsqueeze(1).unsqueeze(3).to_broadcast([P, 2, D, D]),
                                    ALU.mult).then_inc(w_used, 1)

                def forward(k, q, i):
                    v.wait_ge(fwd, J * k + i) if not (isinstance(k, int) and k == 0 and i == 0) else None
                    before = state[:, q, i - 1, 0, :] if i else state[:, (q - 1) % Q, J - 1, 0, :]
                    v.scalar_tensor_tensor(out=state[:, q, i, 0, :], in0=before, scalar=mask(q, 2, i),
                                           in1=state[:, q, i, 1, :], op0=ALU.add, op1=ALU.max).then_inc(fwd, 1)

                def backward(k, q, i):
                    v.wait_ge(bwd, (J - 1) * k + J - 2 - i) if not (isinstance(k, int) and k == 0 and i == J - 2) else None
                    v.scalar_tensor_tensor(out=state[:, q, i, 0, :], in0=state[:, q, i + 1, 0, :], scalar=mask(q, 2, i + 1),
                                           in1=state[:, q, i, 0, :], op0=ALU.add, op1=ALU.max).then_inc(bwd, 1)

                def sums(k, q, i):
                    now = state[:, q, i, 1:3, :].rearrange("p a c -> p (a c)")
                    if i == 0:
                        v.wait_ge(carried, 2 + k)
                        v.tensor_tensor(now, carry[:, :, :].rearrange("p a c -> p (a c)"), now, ALU.add).then_inc(st_done, 1)
                    else:
                        v.wait_ge(st_done, J * k + i)
                        v.scalar_tensor_tensor(out=now, in0=state[:, q, i - 1, 1:3, :].rearrange("p a c -> p (a c)"),
                                               scalar=mask(q, 3, i), in1=now, op0=ALU.mult, op1=ALU.add).then_inc(st_done, 1)

                def carry_over(k, q):
                    v.wait_ge(corr_done, k + 1)
                    if not (isinstance(k, int) and k == 0):
                        v.wait_ge(st_done, J * k)
                    v.tensor_tensor(carry[:, :, :], state[:, (q - 1) % Q, J - 1, 1:3, :],
                                    corr[:, :].unsqueeze(1).to_broadcast([P, 2, C]), ALU.mult).then_inc(carried, 1)

                def iteration(k, q, t, before=True, after=True):
                    if before:
                        carry_over(k - 1, (q - 1) % Q)
                    for i in range(J):
                        forward(k, q, i)
                        if before:
                            sums(k - 1, (q - 1) % Q, i)
                    n = (q + 1) % Q
                    if after:
                        v.wait_ge(gathered[n], 16 * J * (t + (q + 1) // Q + 1))
                    if after and not (isinstance(t, int) and t + (q + 1) // Q == 0):
                        v.wait_ge(scattered[n], 16 * J * (t + (q + 1) // Q))
                    v.wait_ge(fwd, J * k + J)
                    for i in range(J - 2, -1, -1):
                        backward(k, q, i)
                        if after and (J - 2 - i) % 2 == 0:
                            edge(k + 1, n, (J - 2 - i) // 2)
                    v.wait_ge(bwd, (J - 1) * (k + 1))
                    v.scalar_tensor_tensor(out=gap[:, :], in0=state[:, (q - 1) % Q, J - 1, 0, :], scalar=mask(q, 2, 0),
                                           in1=state[:, q, 0, 0, :], op0=ALU.add, op1=ALU.subtract).then_inc(gap_done, 1)
                    for b in range(2):
                        r = slice(b * H, (b + 1) * H)
                        v.tensor_tensor(state[:, q, r, 1, :], state[:, q, r, 1, :], state[:, q, r, 0, :],
                                        ALU.subtract).then_inc(less, 1)
                    if after:
                        for i in range((J - 2) // 2 + 1, J):
                            edge(k + 1, n, i)
                    for b in range(2):
                        r = slice(b * H, (b + 1) * H)
                        v.wait_ge(exped, 2 * k + b + 1)
                        v.tensor_tensor(state[:, q, r, 2, :], state[:, q, r, 2, :], state[:, q, r, 1, :],
                                        ALU.mult).then_inc(p_done, 1)
                    v.wait_ge(p_done, 2 * k + 2)
                    if after:
                        v.wait_ge(w_used, 4 + J * (k + 2))

                v.wait_ge(gathered[0], 16 * J)
                for i in range(J):
                    edge(0, 0, i)
                v.wait_ge(w_used, 4 + J)
                for q in range(Q):
                    iteration(q, q, 0, before=q > 0)
                with v.Fori(1, NBLK // Q - 1) as t:
                    for q in range(Q):
                        iteration(Q * t + q, q, t)
                for q in range(Q):
                    iteration(NBLK - Q + q, q, NBLK // Q - 1, after=q < Q - 1)
                carry_over(NBLK - 1, Q - 1)
                for i in range(J):
                    sums(NBLK - 1, Q - 1, i)

        with ExitStack() as st:
            def tsb(name, shape, dt=F32):
                return st.enter_context(nc.sbuf_tensor(name, shape, dt))

            ht = tsb("ht", [P, 2, 3, C])
            cs = tsb("cs", [128, 3, 2, P, 2])
            kd = tsb("kd", [P, 2, P])
            kr = tsb("kr", [128, P, 2])
            neg = tsb("neg", [128, 2 * P])
            top = tsb("top", [128, 2, 2 * P])
            dec = tsb("dec", [128, 2, 2 * P])
            wgt = tsb("wgt", [128, 2, 2 * P])
            run = tsb("run", [128, 2, 2, 2 * P])
            rows = tsb("rows", [P, 2], I32)
            rowf = tsb("rowf", [P, 4])
            pm = st.enter_context(nc.psum_tensor("pm", [128, 4, 4, 128], F32))
            ht_in = sem("ht_in")
            turned = sem("merge_turned")
            cs_made = sem("merge_cs_made")
            step = sem("merge_step")
            exped = sem("merge_exped")
            back = sem("merge_back")
            ht_made = sem("merge_ht_made")
            weighed = sem("merge_weighed")
            merged = sem("merged")
            block = st.enter_context(nc.Block())

            @block.sync
            def _(sp):
                sp.dma_start(ht[:, 0, :, :].rearrange("p a c -> p (a c)"), rtab[HEAD:HEAD + P, :]).then_inc(ht_in, 16)
                sp.dma_start(ht[:, 1, :, :].rearrange("p a c -> p (a c)"), rtab[TAIL:TAIL + P, :]).then_inc(ht_in, 16)

            @block.tensor
            def _(pe):
                pe.wait_ge(ht_in, 32)
                n = 0
                for a in range(3):
                    for f in range(2):
                        for s in range(2):
                            ins = pe.transpose(pm[:, n // 4, n % 4, 0:P], ht[:, s, a, f * 128:(f + 1) * 128], ident[0:P, 0:P])
                            n += 1
                pe.wait_ge(step, 2)
                for s in range(2):
                    ins = pe.matmul(pm[:, 3, s, 0:P], ones[0:P, :], kd[:, s, :], start=True, stop=True)
                ins.then_inc(turned, 1)
                pe.wait_ge(step, 20)
                n = 0
                for a in range(2):
                    for f in range(2):
                        for s in range(2):
                            ins = pe.transpose(pm[0:P, n // 4, n % 4, :],
                                               run[:, a, f, :].rearrange("c (p s) -> c p s", s=2)[:, :, s], ident[:, :])
                            n += 1
                ins.then_inc(back, 1)

            @block.vector
            def _(v):
                for s in range(2):
                    v.tensor_scalar(kd[:, s, :], ident[0:P, 0:P], ends[:, s:s + 1], None, ALU.mult).then_inc(step, 1)
                v.tensor_tensor(rowf[:, 0:1], ends[:, 0:1], ends[:, 1:2], ALU.not_equal).then_inc(step, 1)
                v.tensor_tensor(rowf[:, 1:2], ends[:, 1:2], ends[:, 2:3], ALU.not_equal).then_inc(step, 1)
                v.tensor_scalar(rowf[:, 2:4], ends[:, 0:2], -float(SKIP), None, ALU.add).then_inc(step, 1)
                v.wait_ge(step, 5)
                v.tensor_tensor(rowf[:, 0:2], rowf[:, 0:2], rowf[:, 2:4], ALU.mult).then_inc(step, 1)
                v.wait_ge(step, 6)
                v.tensor_scalar(rows[:, :], rowf[:, 0:2], float(SKIP), None, ALU.add).then_inc(step, 1)
                v.wait_ge(turned, 1)
                n = 0
                for a in range(3):
                    for f in range(2):
                        v.tensor_copy(cs[:, a, f, :, :].rearrange("c p s -> c s p"),
                                      pm[:, n // 4, n % 4:n % 4 + 2, 0:P]).then_inc(step, 1)
                        n += 2
                v.tensor_copy(kr[:, :, :].rearrange("c p s -> c s p"), pm[:, 3, 0:2, 0:P]).then_inc(step, 1)
                v.wait_ge(step, 14)
                k = kr[:, :, :].rearrange("c p s -> c (p s)")
                v.memset(neg[:, 0:1], 1.0)
                v.tensor_tensor(neg[:, 1:], k[:, 1:], k[:, 0:2 * P - 1], ALU.not_equal).then_inc(step, 1)
                v.wait_ge(step, 15)
                v.tensor_scalar(neg[:, :], neg[:, :], -BIG, None, ALU.mult).then_inc(step, 1)
                v.wait_ge(step, 16)
                seq = lambda a, f: cs[:, a, f, :, :].rearrange("c p s -> c (p s)")
                v.memset(dec[:, :, 0:1], -BIG)
                for f in range(2):
                    ins = v.tensor_tensor_scan(top[:, f, :], neg[:, :], seq(0, f), 0.0, ALU.add, ALU.max)
                ins.then_inc(step, 1)
                v.wait_ge(step, 17)
                for f in range(2):
                    v.tensor_tensor(dec[:, f, 1:], top[:, f, 0:2 * P - 1], neg[:, 1:], ALU.add)
                    ins = v.tensor_tensor(wgt[:, f, :], seq(0, f), top[:, f, :], ALU.subtract)
                ins.then_inc(step, 1)
                v.wait_ge(step, 18)
                v.tensor_tensor(dec[:, :, 1:], dec[:, :, 1:], top[:, :, 1:], ALU.subtract).then_inc(step, 1)
                v.wait_ge(exped, 2)
                for a in range(2):
                    for f in range(2):
                        v.tensor_tensor(seq(a + 1, f), seq(a + 1, f), wgt[:, f, :], ALU.mult).then_inc(weighed, 1)
                v.wait_ge(weighed, 4)
                for a in range(2):
                    for f in range(2):
                        ins = v.tensor_tensor_scan(run[:, a, f, :], dec[:, f, :], seq(a + 1, f), 0.0, ALU.mult, ALU.add)
                ins.then_inc(step, 1)
                v.wait_ge(back, 1)
                n = 0
                for a in range(2):
                    for f in range(2):
                        v.tensor_copy(ht[:, :, a + 1, f * 128:(f + 1) * 128], pm[0:P, n // 4, n % 4:n % 4 + 2, :]).then_inc(ht_made, 1)
                        n += 2

            @block.scalar
            def _(act):
                act.wait_ge(step, 19)
                act.activation(dec[:, :, :], dec[:, :, :], ACT.Exp).then_inc(exped, 1)
                act.activation(wgt[:, :, :], wgt[:, :, :], ACT.Exp).then_inc(exped, 1)

            @block.gpsimd
            def _(g):
                g.wait_ge(ht_made, 4)
                for s in range(2):
                    g.indirect_dma_start(rtab, bass.IndirectOffsetOnAxis(ap=rows[:, s:s + 1], axis=0),
                                         ht[:, s, :, :].rearrange("p a c -> p (a c)"), None,
                                         bounds_check=ROWS - 1, oob_is_err=False).then_inc(merged, 16)
                g.wait_ge(merged, 32)

        with ExitStack() as st:
            def tsb(name, shape, dt=F32):
                return st.enter_context(nc.sbuf_tensor(name, shape, dt))

            tab = tsb("tab", [128, 3, LO, 2, C])
            ft = tsb("ft", [128, NB, LO, D])
            row_in = [sem(f"row_in{b}") for b in range(NB)]
            f_step = sem("f_step")
            n_step = sem("l1_norm_step")
            n_root = sem("l1_norm_root")
            block = st.enter_context(nc.Block())
            view = rtab[0:NPAD, :].rearrange("(b p l) c -> b p l c", p=128, l=LO)

            @block.sync
            def _(sp):
                for b in range(NB):
                    if b >= 3:
                        sp.wait_ge(f_step, 4 * (b - 2))
                    sp.dma_start(tab[:, b % 3, :, :, :].rearrange("p l a c -> p l (a c)"), view[b, :, :, C:3 * C]).then_inc(row_in[b], 16)
                sp.wait_ge(n_step, 9)
                nfull = FULL * 128 * LO
                sp.dma_start(out[0:nfull, :].rearrange("(b p l) c -> p b (l c)", p=128, l=LO),
                             y[:, 0:FULL, :, :].rearrange("p b l c -> p b (l c)")).then_inc(out_out, 16)
                sp.dma_start(out[nfull:nfull + REST * LO, :].rearrange("(p l) c -> p (l c)", l=LO),
                             y[0:REST, FULL, :, :].rearrange("p l c -> p (l c)")).then_inc(out_out, 16)
                sp.dma_start(out[N - LAST:N, :].rearrange("(p l) c -> p (l c)", l=LAST),
                             y[REST:REST + 1, FULL, 0:LAST, :].rearrange("p l c -> p (l c)")).then_inc(out_out, 16)
                sp.wait_ge(out_out, 48)

            @block.vector
            def _(v):
                for b in range(NB):
                    s = tab[:, b % 3, :, 0, :]
                    t = tab[:, b % 3, :, 1, :]
                    v.wait_ge(row_in[b], 16)
                    v.tensor_scalar(s, s, 1.0, None, ALU.max).then_inc(f_step, 1)
                    v.wait_ge(f_step, 4 * b + 1)
                    v.reciprocal(s, s).then_inc(f_step, 1)
                    v.wait_ge(f_step, 4 * b + 2)
                    v.tensor_tensor(t, t, s, ALU.mult).then_inc(f_step, 1)
                    v.wait_ge(f_step, 4 * b + 3)
                    v.tensor_reduce(ft[:, b, :, :], t.rearrange("p l (i o) -> p l o i", i=D), AX, ALU.add).then_inc(f_step, 1)
                v.wait_ge(f_step, 4 * NB)
                v.tensor_tensor(y[:, :, :, :], y[:, :, :, :], ft[:, :, :, :], ALU.add).then_inc(n_step, 1)
                v.wait_ge(n_step, 1)
                base = layer_norm(v, n_step, 1)
                layer_norm_end(v, n_step, base, n_root)

            @block.scalar
            def _(act):
                act.wait_ge(n_step, 7)
                act.activation(stat[:, 2, :], stat[:, 1, :], ACT.Sqrt).then_inc(n_root, 1)


_INS = ['x', 'src', 'dst', 'edge_attr_16', 'edge_attr_8', 'node_vec1', 'L0_gnn_W_msg_tp', 'L0_gnn_W_msg_lin',
        'L0_gnn_W_upd_tp', 'L0_gnn_W_upd_lin', 'L1_gnn_W_msg', 'L1_gnn_b_msg', 'L1_gnn_W_attn', 'L1_gnn_b_attn']
_OUTS = [((N, D), 'float32')]


def kernel(**inputs):
    import numpy as _np
    import concourse.bacc as _bacc
    from concourse import mybir as _mybir
    from concourse.bass_utils import run_bass_kernel_spmd as _run

    nc = _bacc.Bacc("TRN2", target_bir_lowering=False, num_devices=1)
    arrays, args = {}, []
    for name in _INS:
        a = _np.ascontiguousarray(inputs[name])
        arrays[f"in_{name}_dram"] = a
        args.append(nc.dram_tensor(f"in_{name}_dram", a.shape, _mybir.dt.from_np(a.dtype), kind="ExternalInput").ap())
    for i, (shape, dtype) in enumerate(_OUTS):
        dt = _mybir.dt.from_np(_np.dtype(dtype))
        args.append(nc.dram_tensor(f"out_{i}_dram", shape, dt, kind="ExternalOutput").ap())
    gnn(nc, *args)
    r = _run(nc, [arrays], core_ids=[0])
    return r.results[0]["out_0_dram"]
```

```python
from contextlib import ExitStack

import concourse.bass as bass
from concourse import mybir

F32 = mybir.dt.float32
F16 = mybir.dt.float16
BF16 = mybir.dt.bfloat16
I32 = mybir.dt.int32
ALU = mybir.AluOpType
ACT = mybir.ActivationFunctionType
AX = mybir.AxisListType.X

N = 6250
E = 200000
D = 16
DE = 8
P = 125
CH = E // P
J = 8
NBLK = CH // J
LO = 8
HI = -(-N // LO)
NB = -(-HI // 128)
NG = NB * LO
NPAD = NB * 128 * LO
HIP = NB * 128
C = D * D
HEAD, TAIL = NPAD, NPAD + 128
ROWS = NPAD + 256
SKIP = ROWS
BIG = 1.0e38
SMP = 4
SBL = CH // SMP
TN = N // P
RN = 17
GP = 128
NT = 240
U = 8
MW = 12
KS = 99
assert GP * NT * J >= E + (J - 1) * N and NT % U == 0
EPS = 1e-5
FULL = N // (128 * LO)
REST = (N - FULL * 128 * LO) // LO
LAST = N - FULL * 128 * LO - REST * LO
CUT = 512


SAMPLE_STEP = 2
BLOCK_STEP = SAMPLE_STEP + 1 + TN + 1 + 2
TOTAL_STEP = BLOCK_STEP + TN + 1 + 7
PAY_STEP = TOTAL_STEP + 6
FILL_STEP = PAY_STEP + 5
OVER_STEP = FILL_STEP + 2
KEY_STEP = OVER_STEP + 1 + 4 + 3 + 1 + 2 + 2
GROUP_STEPS = KEY_STEP + 5


def gnn(nc, x, src, dst, ea16, ea8, node_vec1, Wmt, Wml, Wut, Wul, Wm, bm, Wa, ba, out):
    ctx = ExitStack()
    with ctx:
        def sb(name, shape, dt=F32):
            return ctx.enter_context(nc.sbuf_tensor(name, shape, dt))

        def sem(name):
            return ctx.enter_context(nc.semaphore(name))

        btab = nc.dram_tensor("btab", (NPAD, DE * D), F32, kind="Internal").ap()
        x1tab = nc.dram_tensor("x1tab", (NPAD, D), F32, kind="Internal").ap()
        rtab = nc.dram_tensor("rtab", (ROWS, 3 * C), F32, kind="Internal").ap()
        meta0 = nc.dram_tensor("meta0", (P, NBLK, 3 * J), I32, kind="Internal").ap()
        meta1 = nc.dram_tensor("meta1", (GP, NT, MW), I32, kind="Internal").ap()
        gtab = nc.dram_tensor("gtab", (GP * NT, 4), F32, kind="Internal").ap()

        ident = sb("ident", [128, 128])
        ones = sb("ones", [128, 128])
        iota_i = sb("iota_i", [128, HI + 16], I32)
        iota_hi = sb("iota_hi", [128, HI], F16)
        iota_lo = sb("iota_lo", [128, LO])
        iota_p = sb("iota_p", [128, 3])
        xa = sb("xa", [128, NB, LO, D])
        y = sb("y", [128, NB, LO, D])
        yc = sb("yc", [128, NB, LO, D])
        stat = sb("stat", [128, 3, NG])
        w0 = sb("w0", [D, DE * D])
        wu = sb("wu", [D, C])
        wlin = sb("wlin", [128, 128])
        wul = sb("wul", [128, 128])
        w1 = sb("w1", [D + 1, 2, C])
        w1p = sb("w1p", [D + 1, 3, 2, C], BF16)
        w1r = sb("w1r", [D + 1, 2, C])
        w99 = sb("w99", [KS, 2, C], BF16)
        identb = sb("identb", [128, 128], BF16)
        ends = sb("ends", [GP, 8])

        consts_made = sem("consts_made")
        inputs_in = sem("inputs_in")
        index_in = sem("index_in")
        meta_step = sem("meta_step")
        meta_out = sem("meta_out")
        xt_made = sem("xt_made")
        xt_copied = sem("xt_copied")
        b_made = sem("b_made")
        b_copied = sem("b_copied")
        btab_out = [sem(f"btab_out{h}") for h in range(2)]
        table_cleared = sem("table_cleared")
        zero_made = sem("zero_made")
        x1_out = sem("x1_out")
        out_out = sem("out_out")

        with ExitStack() as st:
            def tsb(name, shape, dt=F32):
                return st.enter_context(nc.sbuf_tensor(name, shape, dt))

            xt = ctx.enter_context(nc.sbuf_tensor("xt", [D, NG, 128], F32))
            srci = tsb("srci", [P, CH], I32)
            dsti = tsb("dsti", [P, CH], I32)
            m0 = tsb("m0", [P, NBLK, 3 * J], I32)
            m1 = tsb("m1", [GP, NT, MW], I32)
            smp = tsb("smp", [P, SMP])
            smpd = tsb("smpd", [P, P, SMP])
            srow = tsb("srow", [P, P * SMP])
            junk = tsb("junk", [P, 2, P * SMP])
            fone = tsb("fone", [P, P * SMP])
            node = tsb("node", [P, TN + 1])
            iota_n = tsb("iota_n", [128, TN + 1 + NT], I32)
            cnt = tsb("cnt", [P, 2, TN + 1])
            blkf = tsb("blkf", [P, TN + 1])
            blki = tsb("blki", [P, TN + 1], I32)
            near = tsb("near", [P, RN, SBL], I32)
            first = tsb("first", [P, TN + 1])
            ngi = tsb("ngi", [P, TN], I32)
            ngf = tsb("ngf", [P, 4, TN])
            pay = tsb("pay", [P, TN, 4])
            gidx = tsb("gidx", [P, TN], I32)
            tri = tsb("tri", [128, 128])
            shift = tsb("shift", [128, 128])
            base = tsb("base", [128, 4])
            gt = tsb("gt", [GP, NT, 4])
            fill = tsb("fill", [GP, 4, NT])
            grp = tsb("grp", [GP, NT])
            pre = tsb("pre", [4, 2, 128])
            prep = tsb("prep", [GP, 4])
            ta = tsb("ta", [GP, 4, NT])
            tb = tsb("tb", [GP, NT])
            va = tsb("va", [GP, NT, J])
            vb = tsb("vb", [GP, NT, J])
            pg = st.enter_context(nc.psum_tensor("pg", [128, 2, CUT], F32))
            g_step = sem("group_step")
            near_in = sem("near_in")
            gtab_set = sem("gtab_set")
            gtab_out = sem("gtab_out")
            gtab_in = sem("gtab_in")
            g_pe = sem("group_pe")
            w_step = sem("w_step")
            w99_in = sem("w99_in")
            bst = tsb("bst", [128, 2, LO, DE * D])
            pt = st.enter_context(nc.psum_tensor("pt", [128, 2, CUT], F32))
            pb = st.enter_context(nc.psum_tensor("pb", [128, 2, 2, CUT], F32))
            zrow = tsb("zrow", [128, 4 * 3 * C])
            hrow = tsb("hrow", [128, 3 * C])

            blk0 = m0[:, :, :].rearrange("p b (a j) -> p a b j", a=3)
            bj = lambda t: t[:, :].rearrange("p (b j) -> p b j", j=J)
            block = st.enter_context(nc.Block())

            @block.sync
            def _(sp):
                sp.dma_start(srci[:, :], src.rearrange("(p j) -> p j", p=P)).then_inc(index_in, 16)
                sp.dma_start(dsti[:, :], dst.rearrange("(p j) -> p j", p=P)).then_inc(index_in, 16)
                sp.wait_ge(consts_made, 12)
                sp.dma_start(gtab.rearrange("(p t) c -> p (t c)", p=GP),
                             gt[:, :, :].rearrange("p t c -> p (t c)")).then_inc(gtab_set, 16)
                nfull = FULL * 128 * LO
                sp.dma_start(xa[:, 0:FULL, :, :].rearrange("p b l c -> p b (l c)"),
                             x[0:nfull, :].rearrange("(b p l) c -> p b (l c)", p=128, l=LO)).then_inc(inputs_in, 16)
                sp.dma_start(xa[0:REST, FULL, :, :].rearrange("p l c -> p (l c)"),
                             x[nfull:nfull + REST * LO, :].rearrange("(p l) c -> p (l c)", l=LO)).then_inc(inputs_in, 16)
                sp.dma_start(xa[REST:REST + 1, FULL, 0:LAST, :].rearrange("p l c -> p (l c)"),
                             x[N - LAST:N, :].rearrange("(p l) c -> p (l c)", l=LAST)).then_inc(inputs_in, 16)
                sp.dma_start(w0[:, :], Wmt.rearrange("i j h -> i (j h)")).then_inc(inputs_in, 16)
                sp.dma_start(wu[:, :], Wut.rearrange("i h k -> i (h k)")).then_inc(inputs_in, 16)
                for l in range(LO):
                    s = slice(l * D, (l + 1) * D)
                    sp.dma_start(wlin[s, s], Wml).then_inc(inputs_in, 16)
                    sp.dma_start(wul[s, s], Wul).then_inc(inputs_in, 16)
                for n, (w, b) in enumerate(((Wa, ba), (Wm, bm))):
                    sp.dma_start(w1[0:D, n, :], w).then_inc(inputs_in, 16)
                    sp.dma_start(w1[D:D + 1, n, :], b.rearrange("(a c) -> a c", a=1)).then_inc(inputs_in, 16)
                sp.wait_ge(meta_step, 6)
                sp.dma_start(meta0, m0[:, :, :]).then_inc(meta_out, 16)
                for b in range(NB):
                    sp.wait_ge(b_copied, 2 * (b + 1))
                    sp.dma_start(btab[b * 128 * LO:(b + 1) * 128 * LO, :].rearrange("(p l) c -> p (l c)", l=LO),
                                 bst[:, b % 2, :, :].rearrange("p l c -> p (l c)")).then_inc(btab_out[b % 2], 16)
                for h in range(2):
                    sp.wait_ge(btab_out[h], 16 * ((NB + 1 - h) // 2))
                sp.wait_ge(gtab_out, 16 * TN)
                sp.dma_start(gt[:, :, :].rearrange("p t c -> p (t c)"),
                             gtab.rearrange("(p t) c -> p (t c)", p=GP)).then_inc(gtab_in, 16)
                sp.wait_ge(w_step, 5)
                for n, part in enumerate((0, 1, 2, 0, 1, 0)):
                    sp.dma_start(w99[n * D:(n + 1) * D, :, :], w1p[0:D, part, :, :]).then_inc(w99_in, 16)
                for n in range(3):
                    sp.dma_start(w99[6 * D + n:6 * D + n + 1, :, :], w1p[D:D + 1, n, :, :]).then_inc(w99_in, 16)
                sp.wait_ge(g_step, GROUP_STEPS)
                sp.dma_start(meta1, m1[:, :, :]).then_inc(meta_out, 16)
                sp.wait_ge(meta_out, 32)
                sp.wait_ge(w99_in, 16 * 9)
                sp.wait_ge(inputs_in, 16 * (5 + 2 * LO + 4))

            @block.gpsimd
            def _(g):
                g.iota(iota_i[:, 0:HI], [[1, HI]], base=0, channel_multiplier=0).then_inc(consts_made, 1)
                g.iota(iota_i[:, HI:HI + 1], [[1, 1]], base=HEAD, channel_multiplier=1).then_inc(consts_made, 1)
                g.iota(iota_n[:, 0:TN + 1], [[1, TN + 1]], base=0, channel_multiplier=TN).then_inc(consts_made, 1)
                g.iota(iota_n[:, TN + 1:], [[1, NT]], base=0, channel_multiplier=NT).then_inc(consts_made, 1)
                g.memset(ident[:, :], 0.0).then_inc(zero_made, 1)
                g.memset(tri[:, :], 1.0).then_inc(zero_made, 1)
                g.memset(shift[:, :], 0.0).then_inc(zero_made, 1)
                g.wait_ge(zero_made, 3)
                g.affine_select(out=tri[:, :], in_=tri[:, :], compare_op=ALU.is_gt, fill=0.0, base=0,
                                pattern=[[1, 128]], channel_multiplier=-1).then_inc(consts_made, 1)
                g.affine_select(out=shift[:, :], in_=shift[:, :], compare_op=ALU.not_equal, fill=1.0, base=-1,
                                pattern=[[-1, 128]], channel_multiplier=1).then_inc(consts_made, 1)
                g.affine_select(out=ident[:, :], in_=ident[:, :], compare_op=ALU.not_equal, fill=1.0, base=0,
                                pattern=[[-1, 128]], channel_multiplier=1).then_inc(consts_made, 1)
                g.memset(xa[:, :, :, :], 0.0).then_inc(consts_made, 1)
                g.memset(wlin[:, :], 0.0).then_inc(consts_made, 1)
                g.memset(wul[:, :], 0.0).then_inc(consts_made, 1)
                g.memset(ones[:, :], 1.0).then_inc(consts_made, 1)
                g.memset(gt[:, :, :], -1.0).then_inc(consts_made, 1)
                g.memset(zrow[:, :], 0.0).then_inc(zero_made, 1)
                g.memset(hrow[:, 0:C], -BIG).then_inc(zero_made, 1)
                g.memset(hrow[:, C:3 * C], 0.0).then_inc(zero_made, 1)
                for c in range((TN + 1) // RN):
                    g.wait_ge(g_step, BLOCK_STEP + c * RN)
                    for i in range(RN):
                        n = c * RN + i
                        g.indirect_dma_start(near[:, i, :], None, dst.rearrange("(b e) -> b e", e=SBL),
                                             bass.IndirectOffsetOnAxis(ap=blki[:, n:n + 1], axis=0)).then_inc(near_in, 16)
                g.wait_ge(g_step, PAY_STEP)
                g.wait_ge(gtab_set, 16)
                for n in range(TN):
                    g.indirect_dma_start(gtab, bass.IndirectOffsetOnAxis(ap=gidx[:, n:n + 1], axis=0), pay[:, n, :], None,
                                         bounds_check=GP * NT - 1, oob_is_err=False).then_inc(gtab_out, 16)

            @block.vector
            def _(v):
                v.wait_ge(consts_made, 12)
                v.tensor_copy(iota_hi[:, :], iota_i[:, 0:HI]).then_inc(meta_step, 1)
                v.tensor_copy(iota_lo[:, :], iota_i[:, 0:LO]).then_inc(meta_step, 1)
                v.tensor_copy(iota_p[:, 0:1], iota_i[:, HI:HI + 1]).then_inc(meta_step, 1)
                v.wait_ge(index_in, 32)
                v.tensor_copy(blk0[:, 0], bj(dsti)).then_inc(meta_step, 1)
                v.tensor_scalar(blk0[:, 1], bj(srci), 3, None, ALU.logical_shift_right).then_inc(meta_step, 1)
                v.tensor_scalar(blk0[:, 2], bj(srci), LO - 1, None, ALU.bitwise_and).then_inc(meta_step, 1)
                count = [0]

                def link(ins):
                    count[0] += 1
                    ins.then_inc(g_step, 1)
                    v.wait_ge(g_step, count[0])

                def note(ins):
                    count[0] += 1
                    ins.then_inc(g_step, 1)

                v.tensor_copy(identb[:, :], ident[:, :])
                v.tensor_copy(smp[:, :], dsti[:, :].rearrange("p (a e) -> p a e", a=SMP)[:, :, 0])
                v.memset(fone[:, :], 1.0)
                v.tensor_copy(grp[:, :], iota_n[:, TN + 1:])
                link(v.tensor_copy(node[:, :], iota_n[0:P, 0:TN + 1]))
                link(v.tensor_tensor(smpd[:, :, :], ident[0:P, 0:P].unsqueeze(2).to_broadcast([P, P, SMP]),
                                     smp[:, :].unsqueeze(1).to_broadcast([P, P, SMP]), ALU.mult))
                assert count[0] == SAMPLE_STEP
                v.wait_ge(g_pe, 1)
                link(v.tensor_copy(srow[:, :], pg[0:P, 0, 0:P * SMP]))
                for n in range(TN + 1):
                    if n >= 2:
                        v.wait_ge(g_step, count[0] - 1)
                    note(v.scalar_tensor_tensor(out=junk[:, n % 2, :], in0=srow[:, :], scalar=node[:, n:n + 1], in1=fone[:, :],
                                                op0=ALU.is_lt, op1=ALU.mult, accum_out=cnt[:, 0, n:n + 1]))
                v.wait_ge(g_step, count[0])
                link(v.tensor_scalar(blkf[:, :], cnt[:, 0, :], -1.0, 0.0, ALU.add, ALU.max))
                link(v.tensor_copy(blki[:, :], blkf[:, :]))
                assert count[0] == BLOCK_STEP
                for n in range(TN + 1):
                    if n % RN == 0:
                        v.wait_ge(near_in, 16 * (n + RN))
                    v.wait_ge(g_step, count[0] - 1)
                    note(v.scalar_tensor_tensor(out=junk[:, n % 2, 0:SBL], in0=near[:, n % RN, :], scalar=node[:, n:n + 1],
                                                in1=fone[:, 0:SBL], op0=ALU.is_lt, op1=ALU.mult,
                                                accum_out=cnt[:, 1, n:n + 1]))
                v.wait_ge(g_step, count[0])
                link(v.scalar_tensor_tensor(out=first[:, :], in0=blkf[:, :], scalar=float(SBL), in1=cnt[:, 1, :],
                                            op0=ALU.mult, op1=ALU.add))
                deg, num, run, has = (ngf[:, i, :] for i in range(4))
                link(v.tensor_tensor(deg, first[:, 1:], first[:, 0:TN], ALU.subtract))
                link(v.tensor_scalar(deg, deg, float(J - 1), None, ALU.add))
                link(v.tensor_copy(ngi[:, :], deg))
                link(v.tensor_scalar(ngi[:, :], ngi[:, :], 3, None, ALU.logical_shift_right))
                v.memset(junk[:, 0, 0:TN], 0.0)
                link(v.tensor_copy(num, ngi[:, :]))
                link(v.tensor_tensor_scan(run, junk[:, 0, 0:TN], num, 0.0, ALU.add, ALU.add))
                assert count[0] == TOTAL_STEP
                v.tensor_scalar(has, num, 0.0, None, ALU.is_gt)
                link(v.tensor_tensor(deg, run, num, ALU.subtract))
                v.wait_ge(g_pe, 2)
                link(v.tensor_copy(base[0:P, 0:1], pg[0:P, 1, 0:1]))
                v.tensor_copy(pay[:, :, 0], first[:, 0:TN])
                v.tensor_copy(pay[:, :, 1], node[:, 0:TN])
                v.tensor_copy(pay[:, :, 2], first[:, 1:])
                link(v.tensor_scalar(pay[:, :, 3], deg, base[0:P, 0:1], None, ALU.add))
                skip = float(GP * NT)
                link(v.tensor_scalar(deg, pay[:, :, 3], -skip, None, ALU.add))
                link(v.tensor_tensor(deg, deg, has, ALU.mult))
                link(v.tensor_scalar(gidx[:, :], deg, skip, None, ALU.add))
                assert count[0] == PAY_STEP
                v.wait_ge(inputs_in, 16 * (5 + 2 * LO + 4))
                v.tensor_copy(w1p[:, 0, :, :], w1[:, :, :]).then_inc(w_step, 1)
                v.wait_ge(w_step, 1)
                v.tensor_tensor(w1r[:, :, :], w1[:, :, :], w1p[:, 0, :, :], ALU.subtract).then_inc(w_step, 1)
                v.wait_ge(w_step, 2)
                v.tensor_copy(w1p[:, 1, :, :], w1r[:, :, :]).then_inc(w_step, 1)
                v.wait_ge(w_step, 3)
                v.tensor_tensor(w1r[:, :, :], w1r[:, :, :], w1p[:, 1, :, :], ALU.subtract).then_inc(w_step, 1)
                v.wait_ge(w_step, 4)
                v.tensor_copy(w1p[:, 2, :, :], w1r[:, :, :]).then_inc(w_step, 1)
                v.wait_ge(gtab_in, 16)
                for f in range(4):
                    note(v.tensor_tensor_scan(fill[:, f, :], gt[:, :, f], gt[:, :, f], -1.0, ALU.max, ALU.max))
                v.wait_ge(g_step, count[0])
                link(v.tensor_copy(prep[:, :], fill[:, :, NT - 1]))
                assert count[0] == FILL_STEP
                v.wait_ge(g_pe, 3)
                link(v.tensor_copy(pre[:, 0, :], pg[0:4, 0, 0:128]))
                v.memset(pre[:, 1, 0:1], -1.0)
                link(v.tensor_tensor_scan(pre[:, 1, 1:128], pre[:, 0, 0:127], pre[:, 0, 0:127], -1.0, ALU.max, ALU.max))
                assert count[0] == OVER_STEP
                v.wait_ge(g_pe, 4)
                link(v.tensor_copy(base[:, :], pg[:, 1, 0:4]))
                for f in range(4):
                    note(v.tensor_scalar(fill[:, f, :], fill[:, f, :], base[:, f:f + 1], None, ALU.max))
                v.wait_ge(g_step, count[0])
                begin, nd, end, gfirst = (fill[:, i, :] for i in range(4))
                aa, lowest, d1, d2 = (ta[:, i, :] for i in range(4))
                mask = lambda lo, n: m1[:, :, lo:lo + n].bitcast(F32)
                link(v.tensor_tensor(aa, grp[:, :], gfirst, ALU.subtract))
                link(v.scalar_tensor_tensor(out=aa, in0=aa, scalar=float(J), in1=begin, op0=ALU.mult, op1=ALU.add))
                link(v.tensor_scalar(lowest, aa, float(E - J), None, ALU.min))
                v.tensor_copy(m1[:, :, 0], lowest)
                v.tensor_tensor(d1, aa, lowest, ALU.subtract)
                link(v.tensor_tensor(d2, end, lowest, ALU.subtract))
                slot = iota_lo[:, 0:J].unsqueeze(1).to_broadcast([GP, NT, J])
                v.tensor_tensor(va[:, :, :], slot, d1.unsqueeze(2).to_broadcast([GP, NT, J]), ALU.is_ge)
                link(v.tensor_tensor(vb[:, :, :], slot, d2.unsqueeze(2).to_broadcast([GP, NT, J]), ALU.is_lt))
                link(v.tensor_tensor(va[:, :, :], va[:, :, :], vb[:, :, :], ALU.mult))
                v.tensor_scalar(mask(3, J), va[:, :, :], 3 * BIG, -3 * BIG, ALU.mult, ALU.add)
                v.memset(tb[:, 0:1], 1.0)
                link(v.tensor_tensor(tb[:, 1:NT], nd[:, 1:NT], nd[:, 0:NT - 1], ALU.not_equal))
                v.tensor_scalar(mask(2, 1)[:, :, 0], tb[:, :], -BIG, None, ALU.mult)
                v.tensor_copy(ends[:, 0:1], nd[:, 0:1])
                v.tensor_copy(ends[:, 1:2], nd[:, NT - 1:NT])
                v.tensor_scalar(ends[:, 4:5], nd[:, 0:1], 1.0, None, ALU.add)
                v.tensor_scalar(ends[:, 3:4], nd[:, 0:1], -1.0, iota_p[:, 0:1], ALU.mult, ALU.add)
                v.tensor_scalar(iota_p[:, 1:2], iota_p[:, 0:1], 128.0, None, ALU.add)
                link(v.tensor_scalar(d1, nd, nd[:, 0:1], None, ALU.is_equal))
                assert count[0] == KEY_STEP
                link(v.scalar_tensor_tensor(out=d1, in0=d1, scalar=ends[:, 3:4], in1=nd, op0=ALU.mult, op1=ALU.add))
                link(v.tensor_scalar(d1, d1, -float(SKIP), None, ALU.add))
                v.tensor_tensor(d2[:, 0:NT - 1], d1[:, 0:NT - 1], tb[:, 1:NT], ALU.mult)
                link(v.tensor_scalar(d2[:, NT - 1:NT], iota_p[:, 1:2], -float(SKIP), None, ALU.add))
                v.memset(m1[:, :, MW - 1], 0)
                link(v.tensor_scalar(m1[:, :, 1], d2, float(SKIP), None, ALU.add))
                v.wait_ge(g_pe, 5)
                link(v.tensor_scalar(ends[:, 2:3], pg[:, 0, 0:1], -1.0, None, ALU.add))
                assert count[0] == GROUP_STEPS, count[0]

            @block.tensor
            def _(pe):
                pe.wait_ge(inputs_in, 16 * (5 + 2 * LO + 4))
                pe.wait_ge(consts_made, 12)
                pe.wait_ge(g_step, SAMPLE_STEP)
                pe.matmul(pg[:, 0, 0:P * SMP], ones[0:P, :], smpd[:, :, :].rearrange("q p a -> q (p a)"),
                          start=True, stop=True).then_inc(g_pe, 1)
                for s in range(NG // 4):
                    if s >= 2:
                        pe.wait_ge(xt_copied, s - 1)
                    for r in range(4):
                        g = 4 * s + r
                        ins = pe.transpose(pt[0:D, s % 2, r * 128:(r + 1) * 128], xa[:, g // LO, g % LO, :], ident[:, :])
                    ins.then_inc(xt_made, 1)
                for s in range(NG // 4):
                    pe.wait_ge(xt_copied, s + 1)
                    if s >= 4:
                        pe.wait_ge(b_copied, s - 3)
                    for r in range(4):
                        ins = pe.matmul(pb[:, (s // 2) % 2, s % 2, r * 128:(r + 1) * 128], xt[:, 4 * s + r, :], w0[:, :],
                                        start=True, stop=True)
                    ins.then_inc(b_made, 1)
                pe.wait_ge(g_step, TOTAL_STEP)
                pe.matmul(pg[:, 1, 0:1], tri[0:P, :], ngf[:, 2, TN - 1:TN], start=True, stop=True).then_inc(g_pe, 1)
                pe.wait_ge(g_step, FILL_STEP)
                pe.transpose(pg[0:4, 0, 0:128], prep[:, :], ident[:, :]).then_inc(g_pe, 1)
                pe.wait_ge(g_step, OVER_STEP)
                pe.transpose(pg[:, 1, 0:4], pre[:, 1, :], ident[0:4, 0:4]).then_inc(g_pe, 1)
                pe.wait_ge(g_step, KEY_STEP)
                pe.matmul(pg[:, 0, 0:1], shift[:, :], ends[:, 4:5], start=True, stop=True).then_inc(g_pe, 1)

            @block.scalar
            def _(act):
                for s in range(NG // 4):
                    act.wait_ge(xt_made, s + 1)
                    act.copy(xt[:, 4 * s:4 * s + 4, :].rearrange("c g n -> c (g n)"), pt[0:D, s % 2, :]).then_inc(xt_copied, 1)
                for s in range(NG // 4):
                    act.wait_ge(b_made, s + 1)
                    if s >= 4:
                        act.wait_ge(btab_out[(s // 2) % 2], 16 * (s // 4))
                    act.copy(bst[:, (s // 2) % 2, (s % 2) * 4:(s % 2) * 4 + 4, :].rearrange("p l c -> p (l c)"),
                             pb[:, (s // 2) % 2, s % 2, :]).then_inc(b_copied, 1)
                act.wait_ge(zero_made, 6)
                per = NPAD // 128
                view = rtab[0:NPAD, :].rearrange("(p r) c -> p (r c)", p=128)
                for r in range(per // 4):
                    act.dma_start(view[:, r * 12 * C:(r + 1) * 12 * C], zrow[:, :]).then_inc(table_cleared, 16)
                act.dma_start(rtab[HEAD:HEAD + 128, :], hrow[:, :]).then_inc(table_cleared, 16)
                act.dma_start(rtab[TAIL:TAIL + 128, :], hrow[:, :]).then_inc(table_cleared, 16)
                act.wait_ge(table_cleared, 16 * (per // 4 + 2))

        aggt = sb("aggt", [128, HIP])
        with ExitStack() as st:
            def tsb(name, shape, dt=F32):
                return st.enter_context(nc.sbuf_tensor(name, shape, dt))

            mt = tsb("mt", [P, 2, 3, J], I32)
            hilo = tsb("hilo", [P, 2, 2, J])
            e8 = tsb("e8", [P, 2, J, DE])
            bg = tsb("bg", [P, 2, J, DE * D])
            msg = tsb("msg", [P, 2, J, D])
            sact = tsb("sact", [P, 2, J, D])
            s1 = tsb("s1", [P, 2, J, D], BF16)
            s2 = tsb("s2", [P, 2, J, D], BF16)
            s3 = tsb("s3", [P, 2, J, D], BF16)
            res = tsb("res", [P, 2, J, D])
            ohl = tsb("ohl", [P, 2, J, LO], BF16)
            stt = tsb("stt", [P, 2, 3, J, LO, D], BF16)
            ohh = tsb("ohh", [P, 2, J, HI], BF16)
            zb = tsb("zb", [P, CUT], BF16)
            pagg = st.enter_context(nc.psum_tensor("pagg", [128, 2, CUT], F32))

            loaded = [sem(f"l0_loaded{h}") for h in range(2)]
            gathered = [sem(f"l0_gathered{h}") for h in range(2)]
            z_done = sem("l0_z_done")
            msg_done = sem("l0_msg_done")
            hilo_done = sem("l0_hilo_done")
            act_done = sem("l0_act_done")
            res_done = sem("l0_res_done")
            s2_done = sem("l0_s2_done")
            s3_done = sem("l0_s3_done")
            ohl_done = sem("l0_ohl_done")
            stt_done = sem("l0_stt_done")
            ohh_done = sem("l0_ohh_done")
            used = sem("l0_used")
            zeroed = sem("l0_zeroed")
            summed = sem("l0_summed")
            agg_copied = sem("agg_copied")
            block = st.enter_context(nc.Block())

            @block.sync
            def _(sp):
                def load(k, h):
                    sp.dma_start(mt[:, h, :, :].rearrange("p a j -> p (a j)"),
                                 meta0.rearrange("p b c -> p (b c)")[:, bass.ds(k * 3 * J, 3 * J)]).then_inc(loaded[h], 16)
                    sp.dma_start(e8[:, h, :, :].rearrange("p j c -> p (j c)"),
                                 ea8.rearrange("(p j) c -> p (j c)", p=P)[:, bass.ds(k * J * DE, J * DE)]).then_inc(loaded[h], 16)

                load(0, 0)
                load(1, 1)
                with sp.Fori(0, NBLK // 2 - 1) as t:
                    for h in range(2):
                        sp.wait_ge(z_done, 2 * t + h + 1)
                        sp.nop(nofuse=True)
                        sp.wait_ge(hilo_done, 2 * t + h + 1)
                        sp.nop(nofuse=True)
                        load(2 * t + h + 2, h)

            @block.gpsimd
            def _(g):
                def gather(k, h, t):
                    g.wait_ge(loaded[h], 32 * (t + 1))
                    if not isinstance(t, int):
                        g.wait_ge(msg_done, k - 1)
                    g.nop(nofuse=True)
                    for i in range(J):
                        g.indirect_dma_start(bg[:, h, i, :], None, btab,
                                             bass.IndirectOffsetOnAxis(ap=mt[:, h, 0, i:i + 1], axis=0)).then_inc(gathered[h], 16)

                gather(0, 0, 0)
                gather(1, 1, 0)
                with g.Fori(1, NBLK // 2) as t:
                    for h in range(2):
                        gather(2 * t + h, h, t)

            @block.vector
            def _(v):
                v.memset(zb[:, :], 0.0).then_inc(zeroed, 1)
                v.sem_inc(used, 2)

                def messages(k, h, t):
                    v.wait_ge(gathered[h], 16 * J * (t + 1))
                    z = bg[:, h, :, :].rearrange("p s (j h) -> p s j h", j=DE)
                    v.tensor_tensor(z, z, e8[:, h, :, :].unsqueeze(3).to_broadcast([P, J, DE, D]), ALU.mult).then_inc(z_done, 1)
                    v.wait_ge(z_done, k + 1)
                    v.tensor_copy(hilo[:, h, :, :], mt[:, h, 1:3, :]).then_inc(hilo_done, 1)
                    v.tensor_reduce(msg[:, h, :, :], bg[:, h, :, :].rearrange("p s (j h) -> p s h j", j=DE), AX,
                                    ALU.add).then_inc(msg_done, 1)

                def stationaries(k, h):
                    v.wait_ge(hilo_done, k + 1)
                    v.wait_ge(used, k + 1)
                    v.tensor_tensor(ohl[:, h, :, :], iota_lo[0:P, :].unsqueeze(1).to_broadcast([P, J, LO]),
                                    hilo[:, h, 1, :].unsqueeze(2).to_broadcast([P, J, LO]), ALU.is_equal).then_inc(ohl_done, 1)
                    v.wait_ge(act_done, 2 * k + 2)
                    v.tensor_tensor(res[:, h, :, :], sact[:, h, :, :], s1[:, h, :, :], ALU.subtract).then_inc(res_done, 1)
                    for i in range(J):
                        v.tensor_scalar(ohh[:, h, i, :], iota_hi[0:P, :], hilo[:, h, 0, i:i + 1], None,
                                        ALU.is_equal).then_inc(ohh_done, 1)
                        if i == 0:
                            v.wait_ge(res_done, k + 1)
                            v.tensor_copy(s2[:, h, :, :], res[:, h, :, :]).then_inc(s2_done, 1)
                        if i == 2:
                            v.wait_ge(s2_done, k + 1)
                            v.tensor_tensor(s3[:, h, :, :], res[:, h, :, :], s2[:, h, :, :], ALU.subtract).then_inc(s3_done, 1)
                        if i == 1:
                            v.wait_ge(ohl_done, k + 1)
                        if i in (3, 4, 5):
                            part = (s1, s2, s3)[i - 3]
                            if i == 5:
                                v.wait_ge(s3_done, k + 1)
                            v.tensor_tensor(stt[:, h, i - 3, :, :, :],
                                            part[:, h, :, :].unsqueeze(2).to_broadcast([P, J, LO, D]),
                                            ohl[:, h, :, :].unsqueeze(3).to_broadcast([P, J, LO, D]),
                                            ALU.mult).then_inc(stt_done, 1)

                def pair(t):
                    messages(2 * t + 1, 1, t)
                    stationaries(2 * t, 0)
                    messages(2 * t + 2, 0, t + 1)
                    stationaries(2 * t + 1, 1)

                messages(0, 0, 0)
                with v.Fori(0, NBLK // 2 - 1) as t:
                    pair(t)
                messages(NBLK - 1, 1, NBLK // 2 - 1)
                stationaries(NBLK - 2, 0)
                stationaries(NBLK - 1, 1)
                v.memset(aggt[:, HI:HIP], 0.0)
                v.wait_ge(summed, 1)
                v.tensor_copy(aggt[:, 0:CUT], pagg[:, 0, :]).then_inc(agg_copied, 1)
                v.tensor_copy(aggt[:, CUT:HI], pagg[:, 1, 0:HI - CUT]).then_inc(agg_copied, 1)

            @block.scalar
            def _(act):
                with act.Fori(0, NBLK // 2) as t:
                    for h in range(2):
                        k = 2 * t + h
                        act.wait_ge(msg_done, k + 1)
                        act.activation(sact[:, h, :, :], msg[:, h, :, :], ACT.Silu, scale=float((D * DE) ** -0.5)).then_inc(act_done, 1)
                        act.activation(s1[:, h, :, :], msg[:, h, :, :], ACT.Silu, scale=float((D * DE) ** -0.5)).then_inc(act_done, 1)

            @block.tensor
            def _(pe):
                pe.wait_ge(zeroed, 1)
                pe.matmul(pagg[:, 0, :], zb[:, 0:128], zb[:, :], start=True, stop=False, skip_group_check=True)
                pe.matmul(pagg[:, 1, 0:HI - CUT], zb[:, 0:128], zb[:, 0:HI - CUT], start=True, stop=False, skip_group_check=True)
                with pe.Fori(0, NBLK // 2) as t:
                    for h in range(2):
                        k = 2 * t + h
                        pe.wait_ge(stt_done, 3 * k + 3)
                        pe.wait_ge(ohh_done, J * k + J)
                        for i in range(J):
                            for a in range(3):
                                w = stt[:, h, a, i, :, :].rearrange("p l c -> p (l c)")
                                pe.matmul(pagg[:, 0, :], w, ohh[:, h, i, 0:CUT], start=False, stop=False, skip_group_check=True)
                                ins = pe.matmul(pagg[:, 1, 0:HI - CUT], w, ohh[:, h, i, CUT:HI], start=False, stop=False,
                                                skip_group_check=True)
                        ins.then_inc(used, 1)
                pe.matmul(pagg[:, 0, :], zb[:, 0:128], zb[:, :], start=False, stop=True, skip_group_check=True)
                pe.matmul(pagg[:, 1, 0:HI - CUT], zb[:, 0:128], zb[:, 0:HI - CUT], start=False, stop=True,
                          skip_group_check=True).then_inc(summed, 1)

        def layer_norm(v, step, base):
            a = lambda t: t[:, :, :, :].rearrange("p b l c -> p (b l) c")
            v.tensor_reduce(stat[:, 0, :], a(y), AX, ALU.add).then_inc(step, 1)
            v.wait_ge(step, base + 1)
            v.tensor_scalar(stat[:, 1, :], stat[:, 0, :], 1.0 / D, None, ALU.mult).then_inc(step, 1)
            v.wait_ge(step, base + 2)
            v.tensor_tensor(a(yc), a(y), stat[:, 1, :].unsqueeze(2).to_broadcast([128, NG, D]), ALU.subtract).then_inc(step, 1)
            v.wait_ge(step, base + 3)
            v.tensor_tensor(a(y), a(yc), a(yc), ALU.mult).then_inc(step, 1)
            v.wait_ge(step, base + 4)
            v.tensor_reduce(stat[:, 0, :], a(y), AX, ALU.add).then_inc(step, 1)
            v.wait_ge(step, base + 5)
            v.tensor_scalar(stat[:, 1, :], stat[:, 0, :], 1.0 / D, EPS, ALU.mult, ALU.add).then_inc(step, 1)
            return base + 6

        def layer_norm_end(v, step, base, root):
            a = lambda t: t[:, :, :, :].rearrange("p b l c -> p (b l) c")
            v.wait_ge(root, 1)
            v.reciprocal(stat[:, 0, :], stat[:, 2, :]).then_inc(step, 1)
            v.wait_ge(step, base + 1)
            v.tensor_tensor(a(y), a(yc), stat[:, 0, :].unsqueeze(2).to_broadcast([128, NG, D]), ALU.mult).then_inc(step, 1)
            return base + 2

        with ExitStack() as st:
            def tsb(name, shape, dt=F32):
                return st.enter_context(nc.sbuf_tensor(name, shape, dt))

            agg = tsb("agg", [128, NB, LO, D])
            prod = tsb("prod", [128, 2, 2, D, D])
            u = tsb("u", [128, NB, LO, D])
            us = tsb("us", [128, NB, LO, D])
            ut = tsb("ut", [128, NB, 128])
            pa = st.enter_context(nc.psum_tensor("pa", [128, 2, CUT], F32))
            pc = st.enter_context(nc.psum_tensor("pc", [128, 2, CUT], F32))
            pu = st.enter_context(nc.psum_tensor("pu", [128, 2, CUT], F32))
            pv = st.enter_context(nc.psum_tensor("pv", [128, 2, CUT], F32))
            agg_made = sem("agg_made")
            agg_in = sem("agg_in")
            c_made = sem("c_made")
            prod_done = sem("prod_done")
            u_done = sem("u_done")
            us_done = sem("us_done")
            ut_made = sem("ut_made")
            ut_copied = sem("ut_copied")
            v_made = sem("v_made")
            n_step = sem("l0_norm_step")
            n_root = sem("l0_norm_root")
            block = st.enter_context(nc.Block())

            def bank(t, b):
                return t[:, b // 4, (b % 4) * 128:(b % 4) * 128 + 128]

            @block.tensor
            def _(pe):
                for b in range(NB):
                    ins = pe.matmul(bank(pa, b), aggt[:, b * 128:(b + 1) * 128], wlin[:, :], start=True, stop=True)
                ins.then_inc(agg_made, 1)
                for s in range(NG // 2):
                    if s >= 2:
                        pe.wait_ge(prod_done, s - 1)
                    for r in range(2):
                        ins = pe.matmul(pc[:, s % 2, r * C:(r + 1) * C], xt[:, 2 * s + r, :], wu[:, :], start=True, stop=True)
                    ins.then_inc(c_made, 1)
                pe.wait_ge(us_done, 1)
                for b in range(NB):
                    ins = pe.transpose(bank(pu, b), us[:, b, :, :].rearrange("p l c -> p (l c)"), ident[:, :])
                ins.then_inc(ut_made, 1)
                pe.wait_ge(ut_copied, 1)
                for b in range(NB):
                    ins = pe.matmul(bank(pv, b), ut[:, b, :], wul[:, :], start=True, stop=True)
                ins.then_inc(v_made, 1)

            @block.vector
            def _(v):
                flat = lambda t: t[:, :, :, :].rearrange("p b l c -> p (b l c)")
                n = NB * 128
                psum_flat = lambda t: t[:, :, :].rearrange("p a c -> p (a c)")[:, 0:n]
                v.wait_ge(agg_made, 1)
                v.tensor_scalar(flat(agg), psum_flat(pa), D ** -0.5, None, ALU.mult).then_inc(agg_in, 1)
                v.wait_ge(agg_in, 1)
                ag = agg[:, :, :, :].rearrange("p b l c -> p (b l) c")
                uu = u[:, :, :, :].rearrange("p b l c -> p (b l) c")
                for s in range(NG // 2):
                    v.wait_ge(c_made, s + 1)
                    if s >= 2:
                        v.wait_ge(u_done, s - 1)
                    v.tensor_tensor(prod[:, s % 2, :, :, :], pc[:, s % 2, :].rearrange("p (r h k) -> p r h k", r=2, h=D),
                                    ag[:, 2 * s:2 * s + 2, :].unsqueeze(3).to_broadcast([128, 2, D, D]),
                                    ALU.mult).then_inc(prod_done, 1)
                    v.wait_ge(prod_done, s + 1)
                    v.tensor_reduce(uu[:, 2 * s:2 * s + 2, :], prod[:, s % 2, :, :, :].rearrange("p r h k -> p r k h"), AX,
                                    ALU.add).then_inc(u_done, 1)
                v.tensor_scalar(flat(yc), flat(xa), 2.0, None, ALU.mult).then_inc(n_step, 1)
                v.wait_ge(ut_made, 1)
                v.tensor_copy(ut[:, :, :].rearrange("p b c -> p (b c)"), psum_flat(pu)).then_inc(ut_copied, 1)
                v.wait_ge(v_made, 1)
                v.wait_ge(n_step, 1)
                v.scalar_tensor_tensor(out=flat(y), in0=psum_flat(pv), scalar=D ** -0.5, in1=flat(yc), op0=ALU.mult,
                                       op1=ALU.add).then_inc(n_step, 1)
                v.wait_ge(n_step, 2)
                base = layer_norm(v, n_step, 2)
                layer_norm_end(v, n_step, base, n_root)

            @block.scalar
            def _(act):
                act.wait_ge(u_done, NG // 2)
                act.activation(us[:, :, :, :], u[:, :, :, :], ACT.Silu, scale=float((D * D) ** -0.5)).then_inc(us_done, 1)
                act.wait_ge(n_step, 8)
                act.activation(stat[:, 2, :], stat[:, 1, :], ACT.Sqrt).then_inc(n_root, 1)

            @block.sync
            def _(sp):
                sp.wait_ge(n_step, 10)
                sp.dma_start(x1tab.rearrange("(b p l) c -> p b (l c)", p=128, l=LO),
                             y[:, :, :, :].rearrange("p b l c -> p b (l c)")).then_inc(x1_out, 16)
                sp.wait_ge(x1_out, 16)

        with ExitStack() as st:
            def tsb(name, shape, dt=F32):
                return st.enter_context(nc.sbuf_tensor(name, shape, dt))

            mt = tsb("mt1", [GP, U, MW], I32)
            srcs = tsb("srcs", [GP, U, J], I32)
            feat = tsb("feat", [GP, U, J, D])
            xg = tsb("xg", [GP, 4, J, D])
            res = tsb("res1", [GP, 4, J, D])
            parts = tsb("parts", [GP, 4, J, 128], BF16)
            et = tsb("et", [KS, 2, J, 128], BF16)
            work = tsb("work", [GP, 4, J, 2, C])
            state = tsb("state", [GP, U, 3, C])
            top = tsb("top1", [GP, 7, C])
            gap = tsb("gap", [GP, C])
            corr = tsb("corr", [GP, 4, C])
            carry = tsb("carry", [GP, 2, C])
            pt = st.enter_context(nc.psum_tensor("pt1", [128, 2, J, 128], BF16))
            pw = st.enter_context(nc.psum_tensor("pw", [128, 4, CUT], F32))
            ps = st.enter_context(nc.psum_tensor("ps", [128, 2, CUT], F32))

            meta_in = [sem(f"l1_meta_in{q}") for q in range(U)]
            srcs_in = [sem(f"l1_srcs_in{q}") for q in range(4)]
            feat_in = [sem(f"l1_feat_in{q}") for q in range(4)]
            x_in = [sem(f"l1_x_in{q}") for q in range(4)]
            scattered = [sem(f"l1_scattered{q}") for q in range(U)]
            primed = sem("l1_primed")
            high_cut = sem("l1_high_cut")
            rest_cut = sem("l1_rest_cut")
            mid_cut = sem("l1_mid_cut")
            low_cut = sem("l1_low_cut")
            turned = sem("l1_turned")
            et_copied = sem("l1_et_copied")
            w_made = sem("l1_w_made")
            w_used = sem("l1_w_used")
            masked = sem("l1_masked")
            chain = sem("l1_chain")
            gap_done = sem("l1_gap_done")
            less = sem("l1_less")
            corr_done = sem("l1_corr_done")
            exped = sem("l1_exped")
            p_done = sem("l1_p_done")
            summed = sem("l1_summed")
            carried = sem("l1_carried")
            st_done = sem("l1_st_done")
            block = st.enter_context(nc.Block())
            H = J // 2
            MS = 4

            def tile(t, q, off):
                m = q + off
                if isinstance(t, int) and not 0 <= U * t + m < NT:
                    return None
                return U * t + m, m % U, t + m // U

            def wait(eng, what, value):
                if not isinstance(value, int) or value > 0:
                    eng.wait_ge(what, value)

            def rounds(eng, body, before, after):
                for n in range(-before, U):
                    body(n // U, n % U)
                with eng.Fori(1, NT // U - 1) as t:
                    for q in range(U):
                        body(t, q)
                for n in range(NT - U, NT + after):
                    body(n // U, n % U)

            @block.sync
            def _(sp):
                def load(n, q):
                    sp.dma_start(mt[:, q, :], meta1.rearrange("p t c -> p (t c)")[:, bass.ds(n * MW, MW)]).then_inc(meta_in[q], 16)

                for q in range(U):
                    load(q, q)
                with sp.Fori(0, NT // U - 1) as t:
                    for q in range(U):
                        sp.wait_ge(scattered[q], 16 * (t + 1))
                        sp.nop(nofuse=True)
                        load(U * t + q + U, q)

            @block.gpsimd
            def _(g):
                g.memset(state[:, U - 1, :, :], 0.0).then_inc(primed, 1)
                g.memset(parts[:, :, :, :], 1.0).then_inc(primed, 1)

                def body(t, q):
                    if at := tile(t, q, -2):
                        n, b, r = at
                        g.wait_ge(st_done, n + 1)
                        g.nop(nofuse=True)
                        g.indirect_dma_start(rtab, bass.IndirectOffsetOnAxis(ap=mt[:, b, 1:2], axis=0),
                                             state[:, b, :, :].rearrange("p a c -> p (a c)"), None,
                                             bounds_check=ROWS - 1, oob_is_err=False).then_inc(scattered[b], 16)
                    if at := tile(t, q, 2):
                        n, b, r = at
                        g.wait_ge(srcs_in[b % 4], 16 * (2 * r + b // 4 + 1))
                        wait(g, w_used, 4 + J * (n - 3) if not isinstance(n, int) or n >= 4 else 0)
                        g.nop(nofuse=True)
                        for i in range(J):
                            g.indirect_dma_start(xg[:, b % 4, i, :], None, x1tab,
                                                 bass.IndirectOffsetOnAxis(ap=srcs[:, b, i:i + 1], axis=0)).then_inc(x_in[b % 4], 16)
                    if at := tile(t, q, 5):
                        n, b, r = at
                        g.wait_ge(meta_in[b], 16 * (r + 1))
                        g.nop(nofuse=True)
                        where = bass.IndirectOffsetOnAxis(ap=mt[:, b, 0:1], axis=0)
                        g.indirect_dma_start(srcs[:, b, :], None, src.rearrange("(e o) -> e o", o=1), where).then_inc(srcs_in[b % 4], 16)
                        g.indirect_dma_start(feat[:, b, :, :].rearrange("p j c -> p (j c)"), None, ea16, where).then_inc(feat_in[b % 4], 16)

                rounds(g, body, 5, 2)
                for q in range(U):
                    g.wait_ge(scattered[q], 16 * (NT // U))

            @block.scalar
            def _(act):
                act.wait_ge(primed, 2)

                def body(t, q):
                    now, ahead = tile(t, q, 0), tile(t, q, 1)
                    if now:
                        n, b, r = now
                        act.wait_ge(gap_done, n + 1)
                        act.activation(corr[:, b % 4, :], gap[:, :], ACT.Exp).then_inc(corr_done, 1)
                        for half in range(2):
                            act.wait_ge(less, 2 * n + half + 1)
                            s = work[:, b % 4, half * H:(half + 1) * H, 0, :]
                            act.activation(s, s, ACT.Exp).then_inc(exped, 1)
                    if at := tile(t, q, 3):
                        n, b, r = at
                        act.wait_ge(rest_cut, n + 1)
                        act.copy(parts[:, b % 4, :, 3 * D:5 * D].rearrange("p j (a c) -> p j a c", a=2),
                                 res[:, b % 4, :, :].unsqueeze(2).to_broadcast([GP, J, 2, D])).then_inc(mid_cut, 1)
                    if ahead:
                        n, b, r = ahead
                        for i in range(J):
                            act.wait_ge(w_used, 4 + J * n + i + 1)
                            s = work[:, b % 4, i, 0, :]
                            act.activation(s, s, ACT.Identity, bias=mt[:, b, 3 + i:4 + i].bitcast(F32)).then_inc(masked, 1)
                    if at := tile(t, q, 2):
                        n, b, r = at
                        act.wait_ge(turned, n + 1)
                        wait(act, w_made, J * (n - 1))
                        act.copy(et[:, b % 2, :, :], pt[0:KS, b % 2, :, :]).then_inc(et_copied, 1)
                    if at := tile(t, q, 4):
                        n, b, r = at
                        act.wait_ge(feat_in[b % 4], 16 * (2 * r + b // 4 + 1))
                        wait(act, turned, n - 3)
                        act.copy(parts[:, b % 4, :, 0:3 * D].rearrange("p j (a c) -> p j a c", a=3),
                                 feat[:, b, :, :].unsqueeze(2).to_broadcast([GP, J, 3, D])).then_inc(high_cut, 1)

                rounds(act, body, 4, 0)

            @block.tensor
            def _(pe):
                pe.wait_ge(primed, 2)

                def body(t, q):
                    def weigh(at, i):
                        n, b, r = at
                        wait(pe, w_used, J * n + i + 1)
                        pe.matmul(pw[:, i % 4, :], et[:, b % 2, i, :], w99[:, :, :].rearrange("k a c -> k (a c)"),
                                  start=True, stop=True).then_inc(w_made, 1)

                    ahead = tile(t, q, 1)
                    if ahead:
                        pe.wait_ge(et_copied, ahead[0] + 1)
                        for i in range(4):
                            weigh(ahead, i)
                    if at := tile(t, q, -1):
                        n, b, r = at
                        wait(pe, st_done, n - 1)
                        for i in range(J):
                            if i % H == 0:
                                pe.wait_ge(p_done, 2 * n + i // H + 1)
                            ins = pe.matmul(ps[:, b % 2, :], ident[:, :], work[:, b % 4, i, :, :].rearrange("p a c -> p (a c)"),
                                            start=i == 0, stop=i == J - 1)
                        ins.then_inc(summed, 1)
                    if ahead:
                        for i in range(4, J):
                            weigh(ahead, i)
                    if at := tile(t, q, 2):
                        n, b, r = at
                        pe.wait_ge(low_cut, n + 1)
                        wait(pe, et_copied, n - 1)
                        for i in range(J):
                            ins = pe.transpose(pt[0:KS, b % 2, i, :], parts[:, b % 4, i, 0:KS], identb[:, :])
                        ins.then_inc(turned, 1)

                rounds(pe, body, 2, 1)

            @block.vector
            def _(v):
                v.sem_inc(w_used, 4)
                v.wait_ge(primed, 2)

                def word(b, i):
                    return mt[:, b, i:i + 1].bitcast(F32)

                def edge(at, i):
                    n, b, r = at
                    v.wait_ge(w_made, J * n + i + 1)
                    v.tensor_tensor(work[:, b % 4, i, :, :].rearrange("p a (i o) -> p a i o", i=D),
                                    pw[:, i % 4, :].rearrange("p (a i o) -> p a i o", a=2, i=D),
                                    xg[:, b % 4, i, :].unsqueeze(1).unsqueeze(3).to_broadcast([GP, 2, D, D]),
                                    ALU.mult).then_inc(w_used, 1)

                def maxima(at):
                    n, b, r = at
                    s = work[:, b % 4, :, 0, :]
                    v.wait_ge(masked, J * (n + 1))
                    v.tensor_tensor(top[:, 0:4, :], s[:, 0:4, :], s[:, 4:8, :], ALU.max).then_inc(chain, 1)
                    v.wait_ge(chain, MS * n + 1)
                    v.tensor_tensor(top[:, 4:6, :], top[:, 0:2, :], top[:, 2:4, :], ALU.max).then_inc(chain, 1)
                    v.wait_ge(chain, MS * n + 2)
                    v.tensor_tensor(top[:, 6, :], top[:, 4, :], top[:, 5, :], ALU.max).then_inc(chain, 1)
                    v.wait_ge(chain, MS * n + 3)
                    wait(v, scattered[b], 16 * r)
                    v.scalar_tensor_tensor(out=state[:, b, 0, :], in0=state[:, (b - 1) % U, 0, :], scalar=word(b, 2),
                                           in1=top[:, 6, :], op0=ALU.add, op1=ALU.max).then_inc(chain, 1)
                    v.wait_ge(chain, MS * n + 4)

                def products(at, half):
                    n, b, r = at
                    v.wait_ge(exped, 2 * n + half + 1)
                    s = slice(half * H, (half + 1) * H)
                    v.tensor_tensor(work[:, b % 4, s, 1, :], work[:, b % 4, s, 1, :], work[:, b % 4, s, 0, :],
                                    ALU.mult).then_inc(p_done, 1)

                def body(t, q):
                    now, ahead, cut, late = tile(t, q, 0), tile(t, q, 1), tile(t, q, 3), tile(t, q, -2)
                    if late:
                        n, b, r = late
                        v.wait_ge(corr_done, n + 1)
                        wait(v, st_done, n)
                        v.tensor_tensor(carry[:, :, :], state[:, (b - 1) % U, 1:3, :],
                                        corr[:, b % 4, :].unsqueeze(1).to_broadcast([GP, 2, C]), ALU.mult).then_inc(carried, 1)
                    if now:
                        maxima(now)
                    if late:
                        v.wait_ge(summed, n + 1)
                        v.wait_ge(carried, n + 1)
                        v.tensor_tensor(state[:, b, 1:3, :].rearrange("p a c -> p (a c)"),
                                        carry[:, :, :].rearrange("p a c -> p (a c)"), ps[:, b % 2, :], ALU.add).then_inc(st_done, 1)
                    if now:
                        n, b, r = now
                        wait(v, corr_done, n)
                        v.scalar_tensor_tensor(out=gap[:, :], in0=state[:, (b - 1) % U, 0, :], scalar=word(b, 2),
                                               in1=state[:, b, 0, :], op0=ALU.add, op1=ALU.subtract).then_inc(gap_done, 1)
                        for half in range(2):
                            s = slice(half * H, (half + 1) * H)
                            v.tensor_tensor(work[:, b % 4, s, 0, :], work[:, b % 4, s, 0, :],
                                            state[:, b, 0, :].unsqueeze(1).to_broadcast([GP, H, C]), ALU.subtract).then_inc(less, 1)
                    if cut:
                        n, b, r = cut
                        v.wait_ge(high_cut, n + 1)
                        v.tensor_tensor(res[:, b % 4, :, :], feat[:, b, :, :], parts[:, b % 4, :, 0:D],
                                        ALU.subtract).then_inc(rest_cut, 1)
                    if ahead:
                        v.wait_ge(x_in[ahead[1] % 4], 16 * J * (2 * ahead[2] + ahead[1] // 4 + 1))
                        for i in range(J):
                            edge(ahead, i)
                    if now:
                        for half in range(2):
                            products(now, half)
                    if cut:
                        n, b, r = cut
                        v.wait_ge(mid_cut, n + 1)
                        v.tensor_tensor(parts[:, b % 4, :, 5 * D:6 * D], res[:, b % 4, :, :], parts[:, b % 4, :, 3 * D:4 * D],
                                        ALU.subtract).then_inc(low_cut, 1)

                rounds(v, body, 3, 2)

        with ExitStack() as st:
            def tsb(name, shape, dt=F32):
                return st.enter_context(nc.sbuf_tensor(name, shape, dt))

            ht = tsb("ht", [GP, 2, 3, C])
            cs = tsb("cs", [128, 3, 2, GP, 2])
            kd = tsb("kd", [GP, 2, GP])
            kr = tsb("kr", [128, GP, 2])
            neg = tsb("neg", [128, 2 * GP])
            top = tsb("top", [128, 2, 2 * GP])
            dec = tsb("dec", [128, 2, 2 * GP])
            wgt = tsb("wgt", [128, 2, 2 * GP])
            run = tsb("run", [128, 2, 2, 2 * GP])
            rows = tsb("rows", [GP, 2], I32)
            rowf = tsb("rowf", [GP, 4])
            pm = st.enter_context(nc.psum_tensor("pm", [128, 4, 4, 128], F32))
            ht_in = sem("ht_in")
            turned = sem("merge_turned")
            cs_made = sem("merge_cs_made")
            step = sem("merge_step")
            exped = sem("merge_exped")
            back = sem("merge_back")
            ht_made = sem("merge_ht_made")
            weighed = sem("merge_weighed")
            merged = sem("merged")
            block = st.enter_context(nc.Block())

            @block.sync
            def _(sp):
                sp.dma_start(ht[:, 0, :, :].rearrange("p a c -> p (a c)"), rtab[HEAD:HEAD + GP, :]).then_inc(ht_in, 16)
                sp.dma_start(ht[:, 1, :, :].rearrange("p a c -> p (a c)"), rtab[TAIL:TAIL + GP, :]).then_inc(ht_in, 16)

            @block.tensor
            def _(pe):
                pe.wait_ge(ht_in, 32)
                n = 0
                for a in range(3):
                    for f in range(2):
                        for s in range(2):
                            ins = pe.transpose(pm[:, n // 4, n % 4, 0:GP], ht[:, s, a, f * 128:(f + 1) * 128], ident[0:GP, 0:GP])
                            n += 1
                pe.wait_ge(step, 2)
                for s in range(2):
                    ins = pe.matmul(pm[:, 3, s, 0:GP], ones[0:GP, :], kd[:, s, :], start=True, stop=True)
                ins.then_inc(turned, 1)
                pe.wait_ge(step, 20)
                n = 0
                for a in range(2):
                    for f in range(2):
                        for s in range(2):
                            ins = pe.transpose(pm[0:GP, n // 4, n % 4, :],
                                               run[:, a, f, :].rearrange("c (p s) -> c p s", s=2)[:, :, s], ident[:, :])
                            n += 1
                ins.then_inc(back, 1)

            @block.vector
            def _(v):
                for s in range(2):
                    v.tensor_scalar(kd[:, s, :], ident[0:GP, 0:GP], ends[:, s:s + 1], None, ALU.mult).then_inc(step, 1)
                v.tensor_tensor(rowf[:, 0:1], ends[:, 0:1], ends[:, 1:2], ALU.not_equal).then_inc(step, 1)
                v.tensor_tensor(rowf[:, 1:2], ends[:, 1:2], ends[:, 2:3], ALU.not_equal).then_inc(step, 1)
                v.tensor_scalar(rowf[:, 2:4], ends[:, 0:2], -float(SKIP), None, ALU.add).then_inc(step, 1)
                v.wait_ge(step, 5)
                v.tensor_tensor(rowf[:, 0:2], rowf[:, 0:2], rowf[:, 2:4], ALU.mult).then_inc(step, 1)
                v.wait_ge(step, 6)
                v.tensor_scalar(rows[:, :], rowf[:, 0:2], float(SKIP), None, ALU.add).then_inc(step, 1)
                v.wait_ge(turned, 1)
                n = 0
                for a in range(3):
                    for f in range(2):
                        v.tensor_copy(cs[:, a, f, :, :].rearrange("c p s -> c s p"),
                                      pm[:, n // 4, n % 4:n % 4 + 2, 0:GP]).then_inc(step, 1)
                        n += 2
                v.tensor_copy(kr[:, :, :].rearrange("c p s -> c s p"), pm[:, 3, 0:2, 0:GP]).then_inc(step, 1)
                v.wait_ge(step, 14)
                k = kr[:, :, :].rearrange("c p s -> c (p s)")
                v.memset(neg[:, 0:1], 1.0)
                v.tensor_tensor(neg[:, 1:], k[:, 1:], k[:, 0:2 * GP - 1], ALU.not_equal).then_inc(step, 1)
                v.wait_ge(step, 15)
                v.tensor_scalar(neg[:, :], neg[:, :], -BIG, None, ALU.mult).then_inc(step, 1)
                v.wait_ge(step, 16)
                seq = lambda a, f: cs[:, a, f, :, :].rearrange("c p s -> c (p s)")
                v.memset(dec[:, :, 0:1], -BIG)
                for f in range(2):
                    ins = v.tensor_tensor_scan(top[:, f, :], neg[:, :], seq(0, f), 0.0, ALU.add, ALU.max)
                ins.then_inc(step, 1)
                v.wait_ge(step, 17)
                for f in range(2):
                    v.tensor_tensor(dec[:, f, 1:], top[:, f, 0:2 * GP - 1], neg[:, 1:], ALU.add)
                    ins = v.tensor_tensor(wgt[:, f, :], seq(0, f), top[:, f, :], ALU.subtract)
                ins.then_inc(step, 1)
                v.wait_ge(step, 18)
                v.tensor_tensor(dec[:, :, 1:], dec[:, :, 1:], top[:, :, 1:], ALU.subtract).then_inc(step, 1)
                v.wait_ge(exped, 2)
                for a in range(2):
                    for f in range(2):
                        v.tensor_tensor(seq(a + 1, f), seq(a + 1, f), wgt[:, f, :], ALU.mult).then_inc(weighed, 1)
                v.wait_ge(weighed, 4)
                for a in range(2):
                    for f in range(2):
                        ins = v.tensor_tensor_scan(run[:, a, f, :], dec[:, f, :], seq(a + 1, f), 0.0, ALU.mult, ALU.add)
                ins.then_inc(step, 1)
                v.wait_ge(back, 1)
                n = 0
                for a in range(2):
                    for f in range(2):
                        v.tensor_copy(ht[:, :, a + 1, f * 128:(f + 1) * 128], pm[0:GP, n // 4, n % 4:n % 4 + 2, :]).then_inc(ht_made, 1)
                        n += 2

            @block.scalar
            def _(act):
                act.wait_ge(step, 19)
                act.activation(dec[:, :, :], dec[:, :, :], ACT.Exp).then_inc(exped, 1)
                act.activation(wgt[:, :, :], wgt[:, :, :], ACT.Exp).then_inc(exped, 1)

            @block.gpsimd
            def _(g):
                g.wait_ge(ht_made, 4)
                for s in range(2):
                    g.indirect_dma_start(rtab, bass.IndirectOffsetOnAxis(ap=rows[:, s:s + 1], axis=0),
                                         ht[:, s, :, :].rearrange("p a c -> p (a c)"), None,
                                         bounds_check=ROWS - 1, oob_is_err=False).then_inc(merged, 16)
                g.wait_ge(merged, 32)

        with ExitStack() as st:
            def tsb(name, shape, dt=F32):
                return st.enter_context(nc.sbuf_tensor(name, shape, dt))

            tab = tsb("tab", [128, 3, LO, 2, C])
            ft = tsb("ft", [128, NB, LO, D])
            row_in = [sem(f"row_in{b}") for b in range(NB)]
            f_step = sem("f_step")
            n_step = sem("l1_norm_step")
            n_root = sem("l1_norm_root")
            block = st.enter_context(nc.Block())
            view = rtab[0:NPAD, :].rearrange("(b p l) c -> b p l c", p=128, l=LO)

            @block.sync
            def _(sp):
                for b in range(NB):
                    if b >= 3:
                        sp.wait_ge(f_step, 4 * (b - 2))
                    sp.dma_start(tab[:, b % 3, :, :, :].rearrange("p l a c -> p l (a c)"), view[b, :, :, C:3 * C]).then_inc(row_in[b], 16)
                sp.wait_ge(n_step, 9)
                nfull = FULL * 128 * LO
                sp.dma_start(out[0:nfull, :].rearrange("(b p l) c -> p b (l c)", p=128, l=LO),
                             y[:, 0:FULL, :, :].rearrange("p b l c -> p b (l c)")).then_inc(out_out, 16)
                sp.dma_start(out[nfull:nfull + REST * LO, :].rearrange("(p l) c -> p (l c)", l=LO),
                             y[0:REST, FULL, :, :].rearrange("p l c -> p (l c)")).then_inc(out_out, 16)
                sp.dma_start(out[N - LAST:N, :].rearrange("(p l) c -> p (l c)", l=LAST),
                             y[REST:REST + 1, FULL, 0:LAST, :].rearrange("p l c -> p (l c)")).then_inc(out_out, 16)
                sp.wait_ge(out_out, 48)

            @block.vector
            def _(v):
                for b in range(NB):
                    s = tab[:, b % 3, :, 0, :]
                    t = tab[:, b % 3, :, 1, :]
                    v.wait_ge(row_in[b], 16)
                    v.tensor_scalar(s, s, 1.0, None, ALU.max).then_inc(f_step, 1)
                    v.wait_ge(f_step, 4 * b + 1)
                    v.reciprocal(s, s).then_inc(f_step, 1)
                    v.wait_ge(f_step, 4 * b + 2)
                    v.tensor_tensor(t, t, s, ALU.mult).then_inc(f_step, 1)
                    v.wait_ge(f_step, 4 * b + 3)
                    v.tensor_reduce(ft[:, b, :, :], t.rearrange("p l (i o) -> p l o i", i=D), AX, ALU.add).then_inc(f_step, 1)
                v.wait_ge(f_step, 4 * NB)
                v.tensor_tensor(y[:, :, :, :], y[:, :, :, :], ft[:, :, :, :], ALU.add).then_inc(n_step, 1)
                v.wait_ge(n_step, 1)
                base = layer_norm(v, n_step, 1)
                layer_norm_end(v, n_step, base, n_root)

            @block.scalar
            def _(act):
                act.wait_ge(n_step, 7)
                act.activation(stat[:, 2, :], stat[:, 1, :], ACT.Sqrt).then_inc(n_root, 1)


_INS = ['x', 'src', 'dst', 'edge_attr_16', 'edge_attr_8', 'node_vec1', 'L0_gnn_W_msg_tp', 'L0_gnn_W_msg_lin',
        'L0_gnn_W_upd_tp', 'L0_gnn_W_upd_lin', 'L1_gnn_W_msg', 'L1_gnn_b_msg', 'L1_gnn_W_attn', 'L1_gnn_b_attn']
_OUTS = [((N, D), 'float32')]


def kernel(**inputs):
    import numpy as _np
    import concourse.bacc as _bacc
    from concourse import mybir as _mybir
    from concourse.bass_utils import run_bass_kernel_spmd as _run

    nc = _bacc.Bacc("TRN2", target_bir_lowering=False, num_devices=1)
    arrays, args = {}, []
    for name in _INS:
        a = _np.ascontiguousarray(inputs[name])
        arrays[f"in_{name}_dram"] = a
        args.append(nc.dram_tensor(f"in_{name}_dram", a.shape, _mybir.dt.from_np(a.dtype), kind="ExternalInput").ap())
    for i, (shape, dtype) in enumerate(_OUTS):
        dt = _mybir.dt.from_np(_np.dtype(dtype))
        args.append(nc.dram_tensor(f"out_{i}_dram", shape, dt, kind="ExternalOutput").ap())
    gnn(nc, *args)
    r = _run(nc, [arrays], core_ids=[0])
    return r.results[0]["out_0_dram"]
```

```python
from contextlib import ExitStack

import concourse.bass as bass
from concourse import mybir

F32 = mybir.dt.float32
F16 = mybir.dt.float16
BF16 = mybir.dt.bfloat16
I32 = mybir.dt.int32
ALU = mybir.AluOpType
ACT = mybir.ActivationFunctionType
AX = mybir.AxisListType.X

N = 6250
E = 200000
D = 16
DE = 8
P = 125
CH = E // P
J = 8
NBLK = CH // J
LO = 8
HI = -(-N // LO)
NB = -(-HI // 128)
NG = NB * LO
NPAD = NB * 128 * LO
HIP = NB * 128
C = D * D
HEAD, TAIL = NPAD, NPAD + 128
ROWS = NPAD + 256
SKIP = ROWS
BIG = 1.0e38
SMP = 4
SBL = CH // SMP
TN = N // P
RN = 17
GP = 128
NT = 240
U = 8
MW = 12
KS = 99
assert GP * NT * J >= E + (J - 1) * N and NT % U == 0
EPS = 1e-5
FULL = N // (128 * LO)
REST = (N - FULL * 128 * LO) // LO
LAST = N - FULL * 128 * LO - REST * LO
CUT = 512


SAMPLE_STEP = 2
SEARCHES = (TN + 1) // RN
KNOWN_STEP = [SAMPLE_STEP + 1 + (n + 1) * (RN + 2) for n in range(SEARCHES)]
BLOCK_STEP = KNOWN_STEP[-1]
TOTAL_STEP = BLOCK_STEP + TN + 1 + 7
PAY_STEP = TOTAL_STEP + 6
FILL_STEP = PAY_STEP + 5
OVER_STEP = FILL_STEP + 2
KEY_STEP = OVER_STEP + 1 + 4 + 3 + 1 + 2 + 2
GROUP_STEPS = KEY_STEP + 5


def gnn(nc, x, src, dst, ea16, ea8, node_vec1, Wmt, Wml, Wut, Wul, Wm, bm, Wa, ba, out):
    ctx = ExitStack()
    with ctx:
        def sb(name, shape, dt=F32):
            return ctx.enter_context(nc.sbuf_tensor(name, shape, dt))

        def sem(name):
            return ctx.enter_context(nc.semaphore(name))

        btab = nc.dram_tensor("btab", (NPAD, DE * D), F32, kind="Internal").ap()
        x1tab = nc.dram_tensor("x1tab", (NPAD, D), F32, kind="Internal").ap()
        rtab = nc.dram_tensor("rtab", (ROWS, 3 * C), F32, kind="Internal").ap()
        meta0 = nc.dram_tensor("meta0", (P, NBLK, 4 * J), I32, kind="Internal").ap()
        etab = nc.dram_tensor("etab", (E, D + 1), I32, kind="Internal").ap()
        meta1 = nc.dram_tensor("meta1", (GP, NT, MW), I32, kind="Internal").ap()
        gtab = nc.dram_tensor("gtab", (GP * NT, 4), F32, kind="Internal").ap()

        ident = sb("ident", [128, 128])
        ones = sb("ones", [128, 128])
        iota_i = sb("iota_i", [128, HI + 16], I32)
        iota_hi = sb("iota_hi", [128, HI], F16)
        iota_lo = sb("iota_lo", [128, LO])
        iota_p = sb("iota_p", [128, 3])
        xa = sb("xa", [128, NB, LO, D])
        y = sb("y", [128, NB, LO, D])
        yc = sb("yc", [128, NB, LO, D])
        stat = sb("stat", [128, 3, NG])
        w0 = sb("w0", [128, DE * D])
        wu = sb("wu", [128, C])
        wlin = sb("wlin", [128, 128])
        wul = sb("wul", [128, 128])
        w1 = sb("w1", [D + 1, D, 2, D])
        w1p = sb("w1p", [D + 1, 3, 2 * C], BF16)
        w1r = sb("w1r", [D + 1, 2 * C])
        w99 = sb("w99", [KS, 2 * C], BF16)
        identb = sb("identb", [128, 128], BF16)
        ends = sb("ends", [GP, 8])

        consts_made = sem("consts_made")
        inputs_in = sem("inputs_in")
        index_in = sem("index_in")
        meta_step = sem("meta_step")
        meta_out = sem("meta_out")
        xt_made = sem("xt_made")
        xt_copied = sem("xt_copied")
        b_made = sem("b_made")
        b_copied = sem("b_copied")
        btab_out = [sem(f"btab_out{h}") for h in range(2)]
        table_cleared = sem("table_cleared")
        zero_made = sem("zero_made")
        x1_out = sem("x1_out")
        out_out = sem("out_out")

        with ExitStack() as st:
            def tsb(name, shape, dt=F32):
                return st.enter_context(nc.sbuf_tensor(name, shape, dt))

            xt = ctx.enter_context(nc.sbuf_tensor("xt", [128, NG, 128], F32))
            srci = tsb("srci", [P, CH], I32)
            dsti = tsb("dsti", [P, CH], I32)
            m0 = tsb("m0", [P, NBLK, 4 * J], I32)
            m1 = tsb("m1", [GP, NT, MW], I32)
            smp = tsb("smp", [P, SMP])
            smpd = tsb("smpd", [P, P, SMP])
            srow = tsb("srow", [P, P * SMP])
            junk = tsb("junk", [P, 2, P * SMP])
            fone = tsb("fone", [P, P * SMP])
            node = tsb("node", [P, TN + 1])
            iota_n = tsb("iota_n", [128, TN + 1 + NT], I32)
            cnt = tsb("cnt", [P, 2, TN + 1])
            blkf = tsb("blkf", [P, TN + 1])
            blki = tsb("blki", [P, TN + 1], I32)
            near = tsb("near", [P, 2, RN, SBL], I32)
            first = tsb("first", [P, TN + 1])
            ngi = tsb("ngi", [P, TN], I32)
            ngf = tsb("ngf", [P, 4, TN])
            pay = tsb("pay", [P, TN, 4])
            gidx = tsb("gidx", [P, TN], I32)
            tri = tsb("tri", [128, 128])
            shift = tsb("shift", [128, 128])
            base = tsb("base", [128, 4])
            gt = tsb("gt", [GP, NT, 4])
            fill = tsb("fill", [GP, 4, NT])
            grp = tsb("grp", [GP, NT])
            pre = tsb("pre", [4, 2, 128])
            prep = tsb("prep", [GP, 4])
            ta = tsb("ta", [GP, 4, NT])
            tb = tsb("tb", [GP, NT])
            va = tsb("va", [GP, NT, J], BF16)
            vb = tsb("vb", [GP, NT, J], BF16)
            pg = st.enter_context(nc.psum_tensor("pg", [128, 2, CUT], F32))
            g_step = sem("group_step")
            near_in = [sem(f"near_in{c}") for c in range(SEARCHES)]
            gtab_set = sem("gtab_set")
            gtab_out = sem("gtab_out")
            gtab_in = sem("gtab_in")
            g_pe = sem("group_pe")
            w_step = sem("w_step")
            w99_in = sem("w99_in")
            bst = tsb("bst", [128, 2, LO, DE * D])
            pt = st.enter_context(nc.psum_tensor("pt", [128, 2, CUT], F32))
            pb = st.enter_context(nc.psum_tensor("pb", [128, 2, 2, CUT], F32))

            blk0 = m0[:, :, :].rearrange("p b (a j) -> p a b j", a=4)
            bj = lambda t: t[:, :].rearrange("p (b j) -> p b j", j=J)
            block = st.enter_context(nc.Block())

            @block.sync
            def _(sp):
                sp.dma_start(srci[:, :], src.rearrange("(p j) -> p j", p=P)).then_inc(index_in, 16)
                sp.dma_start(dsti[:, :], dst.rearrange("(p j) -> p j", p=P)).then_inc(index_in, 16)
                sp.wait_ge(consts_made, 15)
                sp.dma_start(gtab.rearrange("(p t) c -> p (t c)", p=GP),
                             gt[:, :, :].rearrange("p t c -> p (t c)")).then_inc(gtab_set, 16)
                nfull = FULL * 128 * LO
                sp.dma_start(xa[:, 0:FULL, :, :].rearrange("p b l c -> p b (l c)"),
                             x[0:nfull, :].rearrange("(b p l) c -> p b (l c)", p=128, l=LO)).then_inc(inputs_in, 16)
                sp.dma_start(xa[0:REST, FULL, :, :].rearrange("p l c -> p (l c)"),
                             x[nfull:nfull + REST * LO, :].rearrange("(p l) c -> p (l c)", l=LO)).then_inc(inputs_in, 16)
                sp.dma_start(xa[REST:REST + 1, FULL, 0:LAST, :].rearrange("p l c -> p (l c)"),
                             x[N - LAST:N, :].rearrange("(p l) c -> p (l c)", l=LAST)).then_inc(inputs_in, 16)
                sp.dma_start(w0[0:D, :], Wmt.rearrange("i j h -> i (j h)")).then_inc(inputs_in, 16)
                sp.dma_start(wu[0:D, :], Wut.rearrange("i h k -> i (h k)")).then_inc(inputs_in, 16)
                for l in range(LO):
                    s = slice(l * D, (l + 1) * D)
                    sp.dma_start(wlin[s, s], Wml).then_inc(inputs_in, 16)
                    sp.dma_start(wul[s, s], Wul).then_inc(inputs_in, 16)
                for n, (w, b) in enumerate(((Wa, ba), (Wm, bm))):
                    sp.dma_start(w1[0:D, :, n, :], w.rearrange("k (i o) -> k i o", i=D)).then_inc(inputs_in, 16)
                    sp.dma_start(w1[D:D + 1, :, n, :], b.rearrange("(a i o) -> a i o", a=1, i=D)).then_inc(inputs_in, 16)
                sp.wait_ge(meta_step, 7)
                sp.dma_start(meta0, m0[:, :, :]).then_inc(meta_out, 16)
                for b in range(NB):
                    sp.wait_ge(b_copied, 2 * (b + 1))
                    sp.dma_start(btab[b * 128 * LO:(b + 1) * 128 * LO, :].rearrange("(p l) c -> p (l c)", l=LO),
                                 bst[:, b % 2, :, :].rearrange("p l c -> p (l c)")).then_inc(btab_out[b % 2], 16)
                for h in range(2):
                    sp.wait_ge(btab_out[h], 16 * ((NB + 1 - h) // 2))
                sp.wait_ge(gtab_out, 16 * TN)
                sp.dma_start(gt[:, :, :].rearrange("p t c -> p (t c)"),
                             gtab.rearrange("(p t) c -> p (t c)", p=GP)).then_inc(gtab_in, 16)
                sp.wait_ge(w_step, 5)
                for n, part in enumerate((0, 1, 2, 0, 1, 0)):
                    sp.dma_start(w99[n * D:(n + 1) * D, :], w1p[0:D, part, :]).then_inc(w99_in, 16)
                for n in range(3):
                    sp.dma_start(w99[6 * D + n:6 * D + n + 1, :], w1p[D:D + 1, n, :]).then_inc(w99_in, 16)
                sp.wait_ge(g_step, GROUP_STEPS)
                sp.dma_start(meta1, m1[:, :, :]).then_inc(meta_out, 16)
                sp.wait_ge(meta_out, 32)
                sp.wait_ge(w99_in, 16 * 9)
                sp.wait_ge(inputs_in, 16 * (5 + 2 * LO + 4))

            @block.gpsimd
            def _(g):
                g.iota(iota_i[:, 0:HI], [[1, HI]], base=0, channel_multiplier=0).then_inc(consts_made, 1)
                g.iota(iota_i[:, HI:HI + 1], [[1, 1]], base=HEAD, channel_multiplier=1).then_inc(consts_made, 1)
                g.iota(iota_n[:, 0:TN + 1], [[1, TN + 1]], base=0, channel_multiplier=TN).then_inc(consts_made, 1)
                g.iota(iota_n[:, TN + 1:], [[1, NT]], base=0, channel_multiplier=NT).then_inc(consts_made, 1)
                g.memset(ident[:, :], 0.0).then_inc(zero_made, 1)
                g.memset(tri[:, :], 1.0).then_inc(zero_made, 1)
                g.memset(shift[:, :], 0.0).then_inc(zero_made, 1)
                g.wait_ge(zero_made, 3)
                g.affine_select(out=tri[:, :], in_=tri[:, :], compare_op=ALU.is_gt, fill=0.0, base=0,
                                pattern=[[1, 128]], channel_multiplier=-1).then_inc(consts_made, 1)
                g.affine_select(out=shift[:, :], in_=shift[:, :], compare_op=ALU.not_equal, fill=1.0, base=-1,
                                pattern=[[-1, 128]], channel_multiplier=1).then_inc(consts_made, 1)
                g.affine_select(out=ident[:, :], in_=ident[:, :], compare_op=ALU.not_equal, fill=1.0, base=0,
                                pattern=[[-1, 128]], channel_multiplier=1).then_inc(consts_made, 1)
                g.memset(ones[:, :], 1.0).then_inc(consts_made, 1)
                g.memset(xa[:, :, :, :], 0.0).then_inc(consts_made, 1)
                g.memset(wlin[:, :], 0.0).then_inc(consts_made, 1)
                g.memset(wul[:, :], 0.0).then_inc(consts_made, 1)
                g.memset(w0[:, :], 0.0).then_inc(consts_made, 1)
                g.memset(wu[:, :], 0.0).then_inc(consts_made, 1)
                g.memset(xt[:, :, :], 0.0).then_inc(consts_made, 1)
                g.memset(gt[:, :, :], -1.0).then_inc(consts_made, 1)
                for c in range(SEARCHES):
                    g.wait_ge(g_step, KNOWN_STEP[c] if c < 2 else BLOCK_STEP + (c - 1) * RN)
                    for i in range(RN):
                        n = c * RN + i
                        g.indirect_dma_start(near[:, c % 2, i, :], None, dst.rearrange("(b e) -> b e", e=SBL),
                                             bass.IndirectOffsetOnAxis(ap=blki[:, n:n + 1], axis=0)).then_inc(near_in[c], 16)
                g.wait_ge(g_step, PAY_STEP)
                g.wait_ge(gtab_set, 16)
                for n in range(TN):
                    g.indirect_dma_start(gtab, bass.IndirectOffsetOnAxis(ap=gidx[:, n:n + 1], axis=0), pay[:, n, :], None,
                                         bounds_check=GP * NT - 1, oob_is_err=False).then_inc(gtab_out, 16)

            @block.vector
            def _(v):
                v.wait_ge(consts_made, 7)
                v.tensor_copy(iota_hi[:, :], iota_i[:, 0:HI]).then_inc(meta_step, 1)
                v.tensor_copy(iota_lo[:, :], iota_i[:, 0:LO]).then_inc(meta_step, 1)
                v.tensor_copy(iota_p[:, 0:1], iota_i[:, HI:HI + 1]).then_inc(meta_step, 1)
                v.wait_ge(index_in, 32)
                v.tensor_copy(blk0[:, 0], bj(dsti)).then_inc(meta_step, 1)
                v.tensor_scalar(blk0[:, 1], bj(srci), 3, None, ALU.logical_shift_right).then_inc(meta_step, 1)
                v.tensor_scalar(blk0[:, 2], bj(srci), LO - 1, None, ALU.bitwise_and).then_inc(meta_step, 1)
                count = [0]

                def link(ins):
                    count[0] += 1
                    ins.then_inc(g_step, 1)
                    v.wait_ge(g_step, count[0])

                def note(ins):
                    count[0] += 1
                    ins.then_inc(g_step, 1)

                v.tensor_copy(identb[:, :], ident[:, :])
                v.tensor_copy(smp[:, :], dsti[:, :].rearrange("p (a e) -> p a e", a=SMP)[:, :, 0])
                v.memset(fone[:, :], 1.0)
                v.tensor_copy(grp[:, :], iota_n[:, TN + 1:])
                link(v.tensor_copy(node[:, :], iota_n[0:P, 0:TN + 1]))
                link(v.tensor_tensor(smpd[:, :, :], ident[0:P, 0:P].unsqueeze(2).to_broadcast([P, P, SMP]),
                                     smp[:, :].unsqueeze(1).to_broadcast([P, P, SMP]), ALU.mult))
                assert count[0] == SAMPLE_STEP
                v.wait_ge(g_pe, 1)
                link(v.tensor_copy(srow[:, :], pg[0:P, 0, 0:P * SMP]))
                for c in range(SEARCHES):
                    for n in range(c * RN, (c + 1) * RN):
                        if n >= 2:
                            v.wait_ge(g_step, count[0] - 1)
                        note(v.scalar_tensor_tensor(out=junk[:, n % 2, :], in0=srow[:, :], scalar=node[:, n:n + 1],
                                                    in1=fone[:, :], op0=ALU.is_lt, op1=ALU.mult,
                                                    accum_out=cnt[:, 0, n:n + 1]))
                    v.wait_ge(g_step, count[0])
                    these = slice(c * RN, (c + 1) * RN)
                    link(v.tensor_scalar(blkf[:, these], cnt[:, 0, these], -1.0, 0.0, ALU.add, ALU.max))
                    link(v.tensor_copy(blki[:, these], blkf[:, these]))
                    assert count[0] == KNOWN_STEP[c]
                assert count[0] == BLOCK_STEP
                for n in range(TN + 1):
                    if n % RN == 0:
                        v.wait_ge(near_in[n // RN], 16 * RN)
                    v.wait_ge(g_step, count[0] - 1)
                    note(v.scalar_tensor_tensor(out=junk[:, n % 2, 0:SBL], in0=near[:, n // RN % 2, n % RN, :], scalar=node[:, n:n + 1],
                                                in1=fone[:, 0:SBL], op0=ALU.is_lt, op1=ALU.mult,
                                                accum_out=cnt[:, 1, n:n + 1]))
                v.wait_ge(g_step, count[0])
                link(v.scalar_tensor_tensor(out=first[:, :], in0=blkf[:, :], scalar=float(SBL), in1=cnt[:, 1, :],
                                            op0=ALU.mult, op1=ALU.add))
                deg, num, run, has = (ngf[:, i, :] for i in range(4))
                link(v.tensor_tensor(deg, first[:, 1:], first[:, 0:TN], ALU.subtract))
                link(v.tensor_scalar(deg, deg, float(J - 1), None, ALU.add))
                link(v.tensor_copy(ngi[:, :], deg))
                link(v.tensor_scalar(ngi[:, :], ngi[:, :], 3, None, ALU.logical_shift_right))
                v.memset(junk[:, 0, 0:TN], 0.0)
                link(v.tensor_copy(num, ngi[:, :]))
                link(v.tensor_tensor_scan(run, junk[:, 0, 0:TN], num, 0.0, ALU.add, ALU.add))
                assert count[0] == TOTAL_STEP
                v.tensor_scalar(has, num, 0.0, None, ALU.is_gt)
                link(v.tensor_tensor(deg, run, num, ALU.subtract))
                v.wait_ge(g_pe, 2)
                link(v.tensor_copy(base[0:P, 0:1], pg[0:P, 1, 0:1]))
                v.tensor_copy(pay[:, :, 0], first[:, 0:TN])
                v.tensor_copy(pay[:, :, 1], node[:, 0:TN])
                v.tensor_copy(pay[:, :, 2], first[:, 1:])
                link(v.tensor_scalar(pay[:, :, 3], deg, base[0:P, 0:1], None, ALU.add))
                skip = float(GP * NT)
                link(v.tensor_scalar(deg, pay[:, :, 3], -skip, None, ALU.add))
                link(v.tensor_tensor(deg, deg, has, ALU.mult))
                link(v.tensor_scalar(gidx[:, :], deg, skip, None, ALU.add))
                assert count[0] == PAY_STEP
                w1f = w1[:, :, :, :].rearrange("k i a o -> k (i a o)")
                v.wait_ge(inputs_in, 16 * (5 + 2 * LO + 4))
                v.tensor_copy(w1p[:, 0, :], w1f).then_inc(w_step, 1)
                v.wait_ge(w_step, 1)
                v.tensor_tensor(w1r[:, :], w1f, w1p[:, 0, :], ALU.subtract).then_inc(w_step, 1)
                v.wait_ge(w_step, 2)
                v.tensor_copy(w1p[:, 1, :], w1r[:, :]).then_inc(w_step, 1)
                v.wait_ge(w_step, 3)
                v.tensor_tensor(w1r[:, :], w1r[:, :], w1p[:, 1, :], ALU.subtract).then_inc(w_step, 1)
                v.wait_ge(w_step, 4)
                v.tensor_copy(w1p[:, 2, :], w1r[:, :]).then_inc(w_step, 1)
                v.wait_ge(gtab_in, 16)
                for f in range(4):
                    note(v.tensor_tensor_scan(fill[:, f, :], gt[:, :, f], gt[:, :, f], -1.0, ALU.max, ALU.max))
                v.wait_ge(g_step, count[0])
                link(v.tensor_copy(prep[:, :], fill[:, :, NT - 1]))
                assert count[0] == FILL_STEP
                v.wait_ge(g_pe, 3)
                link(v.tensor_copy(pre[:, 0, :], pg[0:4, 0, 0:128]))
                v.memset(pre[:, 1, 0:1], -1.0)
                link(v.tensor_tensor_scan(pre[:, 1, 1:128], pre[:, 0, 0:127], pre[:, 0, 0:127], -1.0, ALU.max, ALU.max))
                assert count[0] == OVER_STEP
                v.wait_ge(g_pe, 4)
                link(v.tensor_copy(base[:, :], pg[:, 1, 0:4]))
                for f in range(4):
                    note(v.tensor_scalar(fill[:, f, :], fill[:, f, :], base[:, f:f + 1], None, ALU.max))
                v.wait_ge(g_step, count[0])
                begin, nd, end, gfirst = (fill[:, i, :] for i in range(4))
                aa, lowest, d1, d2 = (ta[:, i, :] for i in range(4))
                mask = lambda lo, n: m1[:, :, lo:lo + n].bitcast(F32)
                link(v.tensor_tensor(aa, grp[:, :], gfirst, ALU.subtract))
                link(v.scalar_tensor_tensor(out=aa, in0=aa, scalar=float(J), in1=begin, op0=ALU.mult, op1=ALU.add))
                link(v.tensor_scalar(lowest, aa, float(E - J), None, ALU.min))
                v.tensor_copy(m1[:, :, 0], lowest)
                v.tensor_tensor(d1, aa, lowest, ALU.subtract)
                link(v.tensor_tensor(d2, end, lowest, ALU.subtract))
                slot = iota_lo[:, 0:J].unsqueeze(1).to_broadcast([GP, NT, J])
                v.tensor_tensor(va[:, :, :], slot, d1.unsqueeze(2).to_broadcast([GP, NT, J]), ALU.is_ge)
                link(v.tensor_tensor(vb[:, :, :], slot, d2.unsqueeze(2).to_broadcast([GP, NT, J]), ALU.is_lt))
                link(v.tensor_tensor(va[:, :, :], va[:, :, :], vb[:, :, :], ALU.mult))
                v.tensor_scalar(mask(3, J), va[:, :, :], 3 * BIG, -3 * BIG, ALU.mult, ALU.add)
                v.memset(tb[:, 0:1], 1.0)
                link(v.tensor_tensor(tb[:, 1:NT], nd[:, 1:NT], nd[:, 0:NT - 1], ALU.not_equal))
                v.tensor_scalar(mask(2, 1)[:, :, 0], tb[:, :], -BIG, None, ALU.mult)
                v.tensor_copy(ends[:, 0:1], nd[:, 0:1])
                v.tensor_copy(ends[:, 1:2], nd[:, NT - 1:NT])
                v.tensor_scalar(ends[:, 4:5], nd[:, 0:1], 1.0, None, ALU.add)
                v.tensor_scalar(ends[:, 3:4], nd[:, 0:1], -1.0, iota_p[:, 0:1], ALU.mult, ALU.add)
                v.tensor_scalar(iota_p[:, 1:2], iota_p[:, 0:1], 128.0, None, ALU.add)
                link(v.tensor_scalar(d1, nd, nd[:, 0:1], None, ALU.is_equal))
                assert count[0] == KEY_STEP
                link(v.scalar_tensor_tensor(out=d1, in0=d1, scalar=ends[:, 3:4], in1=nd, op0=ALU.mult, op1=ALU.add))
                link(v.tensor_scalar(d1, d1, -float(SKIP), None, ALU.add))
                v.tensor_tensor(d2[:, 0:NT - 1], d1[:, 0:NT - 1], tb[:, 1:NT], ALU.mult)
                link(v.tensor_scalar(d2[:, NT - 1:NT], iota_p[:, 1:2], -float(SKIP), None, ALU.add))
                v.memset(m1[:, :, MW - 1], 0)
                link(v.tensor_scalar(m1[:, :, 1], d2, float(SKIP), None, ALU.add))
                v.wait_ge(g_pe, 5)
                link(v.tensor_scalar(ends[:, 2:3], pg[:, 0, 0:1], -1.0, None, ALU.add))
                assert count[0] == GROUP_STEPS, count[0]

            @block.tensor
            def _(pe):
                pe.wait_ge(consts_made, 8)
                pe.wait_ge(g_step, SAMPLE_STEP)
                pe.matmul(pg[:, 0, 0:P * SMP], ones[0:P, :], smpd[:, :, :].rearrange("q p a -> q (p a)"),
                          start=True, stop=True).then_inc(g_pe, 1)
                pe.wait_ge(consts_made, 15)
                pe.wait_ge(inputs_in, 16 * (5 + 2 * LO + 4))
                for s in range(NG // 4):
                    if s >= 2:
                        pe.wait_ge(xt_copied, s - 1)
                    for r in range(4):
                        g = 4 * s + r
                        ins = pe.transpose(pt[0:D, s % 2, r * 128:(r + 1) * 128], xa[:, g // LO, g % LO, :], ident[:, :])
                    ins.then_inc(xt_made, 1)
                for s in range(NG // 4):
                    pe.wait_ge(xt_copied, s + 1)
                    if s >= 4:
                        pe.wait_ge(b_copied, s - 3)
                    for r in range(4):
                        ins = pe.matmul(pb[:, (s // 2) % 2, s % 2, r * 128:(r + 1) * 128], xt[:, 4 * s + r, :], w0[:, :],
                                        start=True, stop=True)
                    ins.then_inc(b_made, 1)
                pe.wait_ge(g_step, TOTAL_STEP)
                pe.matmul(pg[:, 1, 0:1], tri[0:P, :], ngf[:, 2, TN - 1:TN], start=True, stop=True).then_inc(g_pe, 1)
                pe.wait_ge(g_step, FILL_STEP)
                pe.transpose(pg[0:4, 0, 0:128], prep[:, :], ident[:, :]).then_inc(g_pe, 1)
                pe.wait_ge(g_step, OVER_STEP)
                pe.transpose(pg[:, 1, 0:4], pre[:, 1, :], ident[0:4, 0:4]).then_inc(g_pe, 1)
                pe.wait_ge(g_step, KEY_STEP)
                pe.matmul(pg[:, 0, 0:1], shift[:, :], ends[:, 4:5], start=True, stop=True).then_inc(g_pe, 1)

            @block.scalar
            def _(act):
                act.wait_ge(index_in, 32)
                act.copy(blk0[:, 3], bj(srci)).then_inc(meta_step, 1)
                act.wait_ge(consts_made, 15)
                for s in range(NG // 4):
                    act.wait_ge(xt_made, s + 1)
                    act.copy(xt[0:D, 4 * s:4 * s + 4, :].rearrange("c g n -> c (g n)"), pt[0:D, s % 2, :]).then_inc(xt_copied, 1)
                for s in range(NG // 4):
                    act.wait_ge(b_made, s + 1)
                    if s >= 4:
                        act.wait_ge(btab_out[(s // 2) % 2], 16 * (s // 4))
                    act.copy(bst[:, (s // 2) % 2, (s % 2) * 4:(s % 2) * 4 + 4, :].rearrange("p l c -> p (l c)"),
                             pb[:, (s // 2) % 2, s % 2, :]).then_inc(b_copied, 1)

        aggt = sb("aggt", [128, HIP])
        with ExitStack() as st:
            def tsb(name, shape, dt=F32):
                return st.enter_context(nc.sbuf_tensor(name, shape, dt))

            mt = tsb("mt", [P, 2, 4, J], I32)
            hilo = tsb("hilo", [P, 2, 2, J])
            e8 = tsb("e8", [P, 2, J, DE])
            e16 = tsb("e16", [P, 2, J, D])
            joined = tsb("joined", [P, 2, J, D + 1], I32)
            bg = tsb("bg", [P, 2, J, DE * D])
            msg = tsb("msg", [P, 2, J, D])
            sact = tsb("sact", [P, 2, J, D])
            s1 = tsb("s1", [P, 2, J, D], BF16)
            s2 = tsb("s2", [P, 2, J, D], BF16)
            s3 = tsb("s3", [P, 2, J, D], BF16)
            res = tsb("res", [P, 2, J, D])
            ohl = tsb("ohl", [P, 2, J, LO], BF16)
            stt = tsb("stt", [P, 2, 3, J, LO, D], BF16)
            ohh = tsb("ohh", [P, 2, J, HI], BF16)
            zb = tsb("zb", [P, CUT], BF16)
            zrow = tsb("zrow", [128, 3 * C])
            hrow = tsb("hrow", [128, 3 * C])
            ohx = tsb("ohx", [P, 2, J, LO, D], BF16)
            pagg = st.enter_context(nc.psum_tensor("pagg", [128, 2, CUT], F32))

            loaded = [sem(f"l0_loaded{h}") for h in range(2)]
            gathered = [sem(f"l0_gathered{h}") for h in range(2)]
            join_done = sem("l0_join_done")
            join_out = [sem(f"l0_join_out{h}") for h in range(2)]
            z_done = sem("l0_z_done")
            msg_done = sem("l0_msg_done")
            hilo_done = sem("l0_hilo_done")
            act_done = sem("l0_act_done")
            res_done = sem("l0_res_done")
            s2_done = sem("l0_s2_done")
            s3_done = sem("l0_s3_done")
            ohl_done = sem("l0_ohl_done")
            ohx_done = sem("l0_ohx_done")
            rows_made = sem("rows_made")
            stt_done = sem("l0_stt_done")
            ohh_done = sem("l0_ohh_done")
            used = sem("l0_used")
            zeroed = sem("l0_zeroed")
            summed = sem("l0_summed")
            agg_copied = sem("agg_copied")
            block = st.enter_context(nc.Block())

            @block.sync
            def _(sp):
                def load(k, h):
                    sp.dma_start(mt[:, h, :, :].rearrange("p a j -> p (a j)"),
                                 meta0.rearrange("p b c -> p (b c)")[:, bass.ds(k * 4 * J, 4 * J)]).then_inc(loaded[h], 16)
                    sp.dma_start(e8[:, h, :, :].rearrange("p j c -> p (j c)"),
                                 ea8.rearrange("(p j) c -> p (j c)", p=P)[:, bass.ds(k * J * DE, J * DE)]).then_inc(loaded[h], 16)
                    sp.dma_start(e16[:, h, :, :].rearrange("p j c -> p (j c)"),
                                 ea16.rearrange("(p j) c -> p (j c)", p=P)[:, bass.ds(k * J * D, J * D)]).then_inc(loaded[h], 16)

                def store(k, h):
                    sp.dma_start(etab.rearrange("(p j) c -> p (j c)", p=P)[:, bass.ds(k * J * (D + 1), J * (D + 1))],
                                 joined[:, h, :, :].rearrange("p j c -> p (j c)")).then_inc(join_out[h], 16)

                def next_pair(t):
                    for h in range(2):
                        sp.wait_ge(z_done, 2 * t + h + 1)
                        sp.nop(nofuse=True)
                        sp.wait_ge(hilo_done, 2 * t + h + 1)
                        sp.nop(nofuse=True)
                        sp.wait_ge(join_done, 2 * t + h + 1)
                        sp.nop(nofuse=True)
                        load(2 * t + h + 2, h)
                        store(2 * t + h, h)

                load(0, 0)
                load(1, 1)
                sp.wait_ge(rows_made, 4)
                sp.dma_start(rtab[HEAD:HEAD + 128, :], hrow[:, :]).then_inc(table_cleared, 16)
                sp.dma_start(rtab[TAIL:TAIL + 128, :], hrow[:, :]).then_inc(table_cleared, 16)
                per = NPAD // 128
                view = rtab[0:NPAD, :].rearrange("(p r) c -> p (r c)", p=128)
                with sp.Fori(0, per) as t:
                    next_pair(t)
                    sp.dma_start(view[:, bass.ds(t * 3 * C, 3 * C)], zrow[:, :]).then_inc(table_cleared, 16)
                with sp.Fori(per, NBLK // 2 - 1) as t:
                    next_pair(t)
                for h in range(2):
                    sp.wait_ge(join_done, NBLK - 1 + h)
                    store(NBLK - 2 + h, h)
                for h in range(2):
                    sp.wait_ge(join_out[h], 16 * (NBLK // 2 + 1))
                sp.wait_ge(table_cleared, 16 * (per + 2))

            @block.gpsimd
            def _(g):
                def gather(k, h, t):
                    g.wait_ge(loaded[h], 48 * (t + 1))
                    if not isinstance(t, int):
                        g.wait_ge(msg_done, k - 1)
                    g.nop(nofuse=True)
                    for i in range(J):
                        g.indirect_dma_start(bg[:, h, i, :], None, btab,
                                             bass.IndirectOffsetOnAxis(ap=mt[:, h, 0, i:i + 1], axis=0)).then_inc(gathered[h], 16)

                g.memset(zrow[:, :], 0.0).then_inc(rows_made, 1)
                g.wait_ge(rows_made, 1)
                g.memset(zrow[:, C:3 * C].rearrange("p (i a o) -> p i a o", i=D, a=2)[:, :, 0, :], 1.0).then_inc(rows_made, 1)
                g.memset(hrow[:, 0:C], -BIG).then_inc(rows_made, 1)
                g.memset(hrow[:, C:3 * C], 0.0).then_inc(rows_made, 1)
                gather(0, 0, 0)
                gather(1, 1, 0)
                with g.Fori(1, NBLK // 2) as t:
                    for h in range(2):
                        gather(2 * t + h, h, t)

            @block.vector
            def _(v):
                v.memset(zb[:, :], 0.0).then_inc(zeroed, 1)
                v.sem_inc(used, 2)

                def messages(k, h, t):
                    v.wait_ge(gathered[h], 16 * J * (t + 1))
                    z = bg[:, h, :, :].rearrange("p s (j h) -> p s j h", j=DE)
                    v.tensor_tensor(z, z, e8[:, h, :, :].unsqueeze(3).to_broadcast([P, J, DE, D]), ALU.mult).then_inc(z_done, 1)
                    v.wait_ge(z_done, k + 1)
                    v.tensor_copy(hilo[:, h, :, :], mt[:, h, 1:3, :]).then_inc(hilo_done, 1)
                    v.tensor_reduce(msg[:, h, :, :], bg[:, h, :, :].rearrange("p s (j h) -> p s h j", j=DE), AX,
                                    ALU.add).then_inc(msg_done, 1)
                    v.wait_ge(hilo_done, k + 1)
                    v.tensor_tensor(ohl[:, h, :, :], iota_lo[0:P, :].unsqueeze(1).to_broadcast([P, J, LO]),
                                    hilo[:, h, 1, :].unsqueeze(2).to_broadcast([P, J, LO]), ALU.is_equal).then_inc(ohl_done, 1)

                def stationaries(k, h):
                    v.wait_ge(used, k + 1)
                    v.wait_ge(act_done, 2 * k + 2)
                    v.tensor_tensor(res[:, h, :, :], sact[:, h, :, :], s1[:, h, :, :], ALU.subtract).then_inc(res_done, 1)
                    for i in range(J):
                        v.tensor_scalar(ohh[:, h, i, :], iota_hi[0:P, :], hilo[:, h, 0, i:i + 1], None,
                                        ALU.is_equal).then_inc(ohh_done, 1)
                        if i == 0:
                            v.wait_ge(res_done, k + 1)
                            v.tensor_copy(s2[:, h, :, :], res[:, h, :, :]).then_inc(s2_done, 1)
                        if i == 2:
                            v.wait_ge(s2_done, k + 1)
                            v.tensor_tensor(s3[:, h, :, :], res[:, h, :, :], s2[:, h, :, :], ALU.subtract).then_inc(s3_done, 1)
                        if i == 1:
                            v.wait_ge(ohx_done, k + 1)
                        if i in (3, 4, 5):
                            part = (s1, s2, s3)[i - 3]
                            if i == 5:
                                v.wait_ge(s3_done, k + 1)
                            v.tensor_tensor(stt[:, h, i - 3, :, :, :],
                                            part[:, h, :, :].unsqueeze(2).to_broadcast([P, J, LO, D]),
                                            ohx[:, h, :, :, :],
                                            ALU.mult).then_inc(stt_done, 1)

                def pair(t):
                    messages(2 * t + 1, 1, t)
                    stationaries(2 * t, 0)
                    messages(2 * t + 2, 0, t + 1)
                    stationaries(2 * t + 1, 1)

                messages(0, 0, 0)
                with v.Fori(0, NBLK // 2 - 1) as t:
                    pair(t)
                messages(NBLK - 1, 1, NBLK // 2 - 1)
                stationaries(NBLK - 2, 0)
                stationaries(NBLK - 1, 1)
                v.memset(aggt[:, HI:HIP], 0.0)
                v.wait_ge(summed, 1)
                v.tensor_copy(aggt[:, 0:CUT], pagg[:, 0, :]).then_inc(agg_copied, 1)
                v.tensor_copy(aggt[:, CUT:HI], pagg[:, 1, 0:HI - CUT]).then_inc(agg_copied, 1)

            @block.scalar
            def _(act):
                for h in range(2):
                    act.sem_inc(join_out[h], 16)
                with act.Fori(0, NBLK // 2) as t:
                    for h in range(2):
                        k = 2 * t + h
                        act.wait_ge(loaded[h], 48 * (t + 1))
                        act.wait_ge(join_out[h], 16 * (t + 1))
                        act.copy(joined[:, h, :, 0:D].bitcast(F32), e16[:, h, :, :])
                        act.copy(joined[:, h, :, D], mt[:, h, 3, :]).then_inc(join_done, 1)
                        act.wait_ge(ohl_done, k + 1)
                        act.copy(ohx[:, h, :, :, :], ohl[:, h, :, :].unsqueeze(3).to_broadcast([P, J, LO, D])).then_inc(ohx_done, 1)
                        act.wait_ge(msg_done, k + 1)
                        act.activation(sact[:, h, :, :], msg[:, h, :, :], ACT.Silu, scale=float((D * DE) ** -0.5)).then_inc(act_done, 1)
                        act.activation(s1[:, h, :, :], msg[:, h, :, :], ACT.Silu, scale=float((D * DE) ** -0.5)).then_inc(act_done, 1)


            @block.tensor
            def _(pe):
                pe.wait_ge(zeroed, 1)
                pe.matmul(pagg[:, 0, :], zb[:, 0:128], zb[:, :], start=True, stop=False, skip_group_check=True)
                pe.matmul(pagg[:, 1, 0:HI - CUT], zb[:, 0:128], zb[:, 0:HI - CUT], start=True, stop=False, skip_group_check=True)
                with pe.Fori(0, NBLK // 2) as t:
                    for h in range(2):
                        k = 2 * t + h
                        pe.wait_ge(stt_done, 3 * k + 3)
                        pe.wait_ge(ohh_done, J * k + J)
                        for i in range(J):
                            for a in range(3):
                                w = stt[:, h, a, i, :, :].rearrange("p l c -> p (l c)")
                                pe.matmul(pagg[:, 0, :], w, ohh[:, h, i, 0:CUT], start=False, stop=False, skip_group_check=True)
                                ins = pe.matmul(pagg[:, 1, 0:HI - CUT], w, ohh[:, h, i, CUT:HI], start=False, stop=False,
                                                skip_group_check=True)
                        ins.then_inc(used, 1)
                pe.matmul(pagg[:, 0, :], zb[:, 0:128], zb[:, :], start=False, stop=True, skip_group_check=True)
                pe.matmul(pagg[:, 1, 0:HI - CUT], zb[:, 0:128], zb[:, 0:HI - CUT], start=False, stop=True,
                          skip_group_check=True).then_inc(summed, 1)

        def layer_norm(v, step, base):
            a = lambda t: t[:, :, :, :].rearrange("p b l c -> p (b l) c")
            v.tensor_reduce(stat[:, 0, :], a(y), AX, ALU.add).then_inc(step, 1)
            v.wait_ge(step, base + 1)
            v.tensor_scalar(stat[:, 1, :], stat[:, 0, :], 1.0 / D, None, ALU.mult).then_inc(step, 1)
            v.wait_ge(step, base + 2)
            v.tensor_tensor(a(yc), a(y), stat[:, 1, :].unsqueeze(2).to_broadcast([128, NG, D]), ALU.subtract).then_inc(step, 1)
            v.wait_ge(step, base + 3)
            v.tensor_tensor(a(y), a(yc), a(yc), ALU.mult).then_inc(step, 1)
            v.wait_ge(step, base + 4)
            v.tensor_reduce(stat[:, 0, :], a(y), AX, ALU.add).then_inc(step, 1)
            v.wait_ge(step, base + 5)
            v.tensor_scalar(stat[:, 1, :], stat[:, 0, :], 1.0 / D, EPS, ALU.mult, ALU.add).then_inc(step, 1)
            return base + 6

        def layer_norm_end(v, step, base, root):
            a = lambda t: t[:, :, :, :].rearrange("p b l c -> p (b l) c")
            v.wait_ge(root, 1)
            v.reciprocal(stat[:, 0, :], stat[:, 2, :]).then_inc(step, 1)
            v.wait_ge(step, base + 1)
            v.tensor_tensor(a(y), a(yc), stat[:, 0, :].unsqueeze(2).to_broadcast([128, NG, D]), ALU.mult).then_inc(step, 1)
            return base + 2

        with ExitStack() as st:
            def tsb(name, shape, dt=F32):
                return st.enter_context(nc.sbuf_tensor(name, shape, dt))

            agg = tsb("agg", [128, NB, LO, D])
            prod = tsb("prod", [128, 2, 2, D, D])
            u = tsb("u", [128, NB, LO, D])
            us = tsb("us", [128, NB, LO, D])
            ut = tsb("ut", [128, NB, 128])
            pa = st.enter_context(nc.psum_tensor("pa", [128, 2, CUT], F32))
            pc = st.enter_context(nc.psum_tensor("pc", [128, 2, CUT], F32))
            pu = st.enter_context(nc.psum_tensor("pu", [128, 2, CUT], F32))
            pv = st.enter_context(nc.psum_tensor("pv", [128, 2, CUT], F32))
            agg_made = sem("agg_made")
            agg_in = sem("agg_in")
            c_made = sem("c_made")
            prod_done = sem("prod_done")
            u_done = sem("u_done")
            us_done = sem("us_done")
            ut_made = sem("ut_made")
            ut_copied = sem("ut_copied")
            v_made = sem("v_made")
            n_step = sem("l0_norm_step")
            n_root = sem("l0_norm_root")
            block = st.enter_context(nc.Block())

            def bank(t, b):
                return t[:, b // 4, (b % 4) * 128:(b % 4) * 128 + 128]

            @block.tensor
            def _(pe):
                for b in range(NB):
                    ins = pe.matmul(bank(pa, b), aggt[:, b * 128:(b + 1) * 128], wlin[:, :], start=True, stop=True)
                ins.then_inc(agg_made, 1)
                for s in range(NG // 2):
                    if s >= 2:
                        pe.wait_ge(prod_done, s - 1)
                    for r in range(2):
                        ins = pe.matmul(pc[:, s % 2, r * C:(r + 1) * C], xt[:, 2 * s + r, :], wu[:, :], start=True, stop=True)
                    ins.then_inc(c_made, 1)
                pe.wait_ge(us_done, 1)
                for b in range(NB):
                    ins = pe.transpose(bank(pu, b), us[:, b, :, :].rearrange("p l c -> p (l c)"), ident[:, :])
                ins.then_inc(ut_made, 1)
                pe.wait_ge(ut_copied, 1)
                for b in range(NB):
                    ins = pe.matmul(bank(pv, b), ut[:, b, :], wul[:, :], start=True, stop=True)
                ins.then_inc(v_made, 1)

            @block.vector
            def _(v):
                flat = lambda t: t[:, :, :, :].rearrange("p b l c -> p (b l c)")
                n = NB * 128
                psum_flat = lambda t: t[:, :, :].rearrange("p a c -> p (a c)")[:, 0:n]
                v.wait_ge(agg_made, 1)
                v.tensor_scalar(flat(agg), psum_flat(pa), D ** -0.5, None, ALU.mult).then_inc(agg_in, 1)
                v.wait_ge(agg_in, 1)
                ag = agg[:, :, :, :].rearrange("p b l c -> p (b l) c")
                uu = u[:, :, :, :].rearrange("p b l c -> p (b l) c")
                for s in range(NG // 2):
                    v.wait_ge(c_made, s + 1)
                    if s >= 2:
                        v.wait_ge(u_done, s - 1)
                    v.tensor_tensor(prod[:, s % 2, :, :, :], pc[:, s % 2, :].rearrange("p (r h k) -> p r h k", r=2, h=D),
                                    ag[:, 2 * s:2 * s + 2, :].unsqueeze(3).to_broadcast([128, 2, D, D]),
                                    ALU.mult).then_inc(prod_done, 1)
                    v.wait_ge(prod_done, s + 1)
                    v.tensor_reduce(uu[:, 2 * s:2 * s + 2, :], prod[:, s % 2, :, :, :].rearrange("p r h k -> p r k h"), AX,
                                    ALU.add).then_inc(u_done, 1)
                v.tensor_scalar(flat(yc), flat(xa), 2.0, None, ALU.mult).then_inc(n_step, 1)
                v.wait_ge(ut_made, 1)
                v.tensor_copy(ut[:, :, :].rearrange("p b c -> p (b c)"), psum_flat(pu)).then_inc(ut_copied, 1)
                v.wait_ge(v_made, 1)
                v.wait_ge(n_step, 1)
                v.scalar_tensor_tensor(out=flat(y), in0=psum_flat(pv), scalar=D ** -0.5, in1=flat(yc), op0=ALU.mult,
                                       op1=ALU.add).then_inc(n_step, 1)
                v.wait_ge(n_step, 2)
                base = layer_norm(v, n_step, 2)
                layer_norm_end(v, n_step, base, n_root)

            @block.scalar
            def _(act):
                act.wait_ge(u_done, NG // 2)
                act.activation(us[:, :, :, :], u[:, :, :, :], ACT.Silu, scale=float((D * D) ** -0.5)).then_inc(us_done, 1)
                act.wait_ge(n_step, 8)
                act.activation(stat[:, 2, :], stat[:, 1, :], ACT.Sqrt).then_inc(n_root, 1)

            @block.sync
            def _(sp):
                sp.wait_ge(n_step, 10)
                sp.dma_start(x1tab.rearrange("(b p l) c -> p b (l c)", p=128, l=LO),
                             y[:, :, :, :].rearrange("p b l c -> p b (l c)")).then_inc(x1_out, 16)
                sp.wait_ge(x1_out, 16)

        with ExitStack() as st:
            def tsb(name, shape, dt=F32):
                return st.enter_context(nc.sbuf_tensor(name, shape, dt))

            mt = tsb("mt1", [GP, U, MW], I32)
            edge = tsb("edge", [GP, U, J, D + 1], I32)
            xg = tsb("xg", [GP, 4, J, D])
            res = tsb("res1", [GP, 4, J, D])
            parts = tsb("parts", [GP, 4, J, 128], BF16)
            et = tsb("et", [KS, 2, J, 128], BF16)
            work = tsb("work", [GP, 4, J, D, 2, D])
            state = tsb("state", [GP, U, 3 * C])
            top = tsb("top1", [GP, 7, C])
            gap = tsb("gap", [GP, C])
            corr = tsb("corr", [GP, 4, C])
            carry = tsb("carry", [GP, 2, 2 * C])
            pt = st.enter_context(nc.psum_tensor("pt1", [128, 2, J, 128], BF16))
            pw = st.enter_context(nc.psum_tensor("pw", [128, 4, CUT], F32))
            ps = st.enter_context(nc.psum_tensor("ps", [128, 2, CUT], F32))

            meta_in = [sem(f"l1_meta_in{q}") for q in range(U)]
            edge_in = [sem(f"l1_edge_in{q}") for q in range(4)]
            x_in = [sem(f"l1_x_in{q}") for q in range(4)]
            scattered = [sem(f"l1_scattered{q}") for q in range(U)]
            primed = sem("l1_primed")
            high_cut = sem("l1_high_cut")
            rest_cut = sem("l1_rest_cut")
            mid_cut = sem("l1_mid_cut")
            low_cut = sem("l1_low_cut")
            turned = sem("l1_turned")
            et_copied = sem("l1_et_copied")
            w_made = sem("l1_w_made")
            w_used = sem("l1_w_used")
            masked = sem("l1_masked")
            chain = sem("l1_chain")
            gap_done = sem("l1_gap_done")
            less = sem("l1_less")
            corr_done = sem("l1_corr_done")
            exped = sem("l1_exped")
            p_done = sem("l1_p_done")
            summed = sem("l1_summed")
            carried = sem("l1_carried")
            st_done = sem("l1_st_done")
            block = st.enter_context(nc.Block())
            H = J // 2
            MS = 4

            def tile(t, q, off):
                m = q + off
                if isinstance(t, int) and not 0 <= U * t + m < NT:
                    return None
                return U * t + m, m % U, t + m // U

            def channels(t, a=None):
                return t.rearrange("p (i o) -> p i o", i=D) if a is None else t.rearrange("p (i a o) -> p i a o", i=D, a=a)

            def wait(eng, what, value):
                if not isinstance(value, int) or value > 0:
                    eng.wait_ge(what, value)

            def rounds(eng, body, before, after):
                for n in range(-before, U):
                    body(n // U, n % U)
                with eng.Fori(1, NT // U - 1) as t:
                    for q in range(U):
                        body(t, q)
                for n in range(NT - U, NT + after):
                    body(n // U, n % U)

            @block.sync
            def _(sp):
                def load(n, q):
                    sp.dma_start(mt[:, q, :], meta1.rearrange("p t c -> p (t c)")[:, bass.ds(n * MW, MW)]).then_inc(meta_in[q], 16)

                for q in range(U):
                    load(q, q)
                with sp.Fori(0, NT // U - 1) as t:
                    for q in range(U):
                        sp.wait_ge(scattered[q], 16 * (t + 1))
                        sp.nop(nofuse=True)
                        load(U * t + q + U, q)

            @block.gpsimd
            def _(g):
                g.memset(state[:, U - 1, :], 0.0).then_inc(primed, 1)
                g.memset(parts[:, :, :, :], 1.0).then_inc(primed, 1)
                g.wait_ge(primed, 2)

                def body(t, q):
                    if at := tile(t, q, -2):
                        n, b, r = at
                        g.wait_ge(st_done, n + 1)
                        g.nop(nofuse=True)
                        g.indirect_dma_start(rtab, bass.IndirectOffsetOnAxis(ap=mt[:, b, 1:2], axis=0),
                                             state[:, b, :], None,
                                             bounds_check=ROWS - 1, oob_is_err=False).then_inc(scattered[b], 16)
                    if at := tile(t, q, -1):
                        n, b, r = at
                        g.wait_ge(corr_done, n + 1)
                        wait(g, st_done, n)
                        g.tensor_tensor(channels(carry[:, b % 2, :], 2), channels(state[:, (b - 1) % U, C:3 * C], 2),
                                        channels(corr[:, b % 4, :]).unsqueeze(2).to_broadcast([GP, D, 2, D]),
                                        ALU.mult).then_inc(carried, 1)
                    if at := tile(t, q, 3):
                        n, b, r = at
                        g.wait_ge(high_cut, n + 1)
                        g.tensor_tensor(res[:, b % 4, :, :], edge[:, b, :, 0:D].bitcast(F32), parts[:, b % 4, :, 0:D],
                                        ALU.subtract).then_inc(rest_cut, 1)
                    if at := tile(t, q, 2):
                        n, b, r = at
                        g.wait_ge(mid_cut, n + 1)
                        g.tensor_tensor(parts[:, b % 4, :, 5 * D:6 * D], res[:, b % 4, :, :], parts[:, b % 4, :, 3 * D:4 * D],
                                        ALU.subtract).then_inc(low_cut, 1)
                    if at := tile(t, q, 2):
                        n, b, r = at
                        g.wait_ge(edge_in[b % 4], 16 * (2 * r + b // 4 + 1))
                        wait(g, w_used, 2 + H * (n - 3) if not isinstance(n, int) or n >= 4 else 0)
                        g.nop(nofuse=True)
                        for i in range(J):
                            g.indirect_dma_start(xg[:, b % 4, i, :], None, x1tab,
                                                 bass.IndirectOffsetOnAxis(ap=edge[:, b, i, D:D + 1], axis=0)).then_inc(x_in[b % 4], 16)
                    if at := tile(t, q, 5):
                        n, b, r = at
                        g.wait_ge(meta_in[b], 16 * (r + 1))
                        g.nop(nofuse=True)
                        g.indirect_dma_start(edge[:, b, :, :].rearrange("p j c -> p (j c)"), None, etab,
                                             bass.IndirectOffsetOnAxis(ap=mt[:, b, 0:1], axis=0)).then_inc(edge_in[b % 4], 16)

                rounds(g, body, 5, 2)
                for q in range(U):
                    g.wait_ge(scattered[q], 16 * (NT // U))

            @block.scalar
            def _(act):
                act.wait_ge(primed, 2)

                def body(t, q):
                    now, ahead = tile(t, q, 0), tile(t, q, 1)
                    if now:
                        n, b, r = now
                        act.wait_ge(gap_done, n + 1)
                        act.activation(corr[:, b % 4, :], gap[:, :], ACT.Exp).then_inc(corr_done, 1)
                        for half in range(2):
                            act.wait_ge(less, 2 * n + half + 1)
                            s = work[:, b % 4, half * H:(half + 1) * H, :, 0, :]
                            act.activation(s, s, ACT.Exp).then_inc(exped, 1)
                    if at := tile(t, q, 2):
                        n, b, r = at
                        act.wait_ge(turned, n + 1)
                        wait(act, w_made, J * (n - 1))
                        act.copy(et[:, b % 2, :, :], pt[0:KS, b % 2, :, :]).then_inc(et_copied, 1)
                    if ahead:
                        n, b, r = ahead
                        for i in range(J):
                            if i % 2 == 0:
                                act.wait_ge(w_used, 2 + H * n + i // 2 + 1)
                            s = work[:, b % 4, i, :, 0, :]
                            act.activation(s, s, ACT.Identity, bias=mt[:, b, 3 + i:4 + i].bitcast(F32)).then_inc(masked, 1)
                    if at := tile(t, q, 3):
                        n, b, r = at
                        act.wait_ge(rest_cut, n + 1)
                        act.copy(parts[:, b % 4, :, 3 * D:5 * D].rearrange("p j (a c) -> p j a c", a=2),
                                 res[:, b % 4, :, :].unsqueeze(2).to_broadcast([GP, J, 2, D])).then_inc(mid_cut, 1)
                    if at := tile(t, q, 4):
                        n, b, r = at
                        act.wait_ge(edge_in[b % 4], 16 * (2 * r + b // 4 + 1))
                        wait(act, turned, n - 3)
                        act.copy(parts[:, b % 4, :, 0:3 * D].rearrange("p j (a c) -> p j a c", a=3),
                                 edge[:, b, :, 0:D].bitcast(F32).unsqueeze(2).to_broadcast([GP, J, 3, D])).then_inc(high_cut, 1)

                    if at := tile(t, q, -1):
                        n, b, r = at
                        act.wait_ge(summed, n + 1)
                        act.copy(state[:, b, C:3 * C], ps[:, b % 2, :]).then_inc(st_done, 1)

                rounds(act, body, 4, 1)

            @block.tensor
            def _(pe):
                pe.wait_ge(primed, 2)

                def body(t, q):
                    def weigh(at, i):
                        n, b, r = at
                        if i % 2 == 0:
                            wait(pe, w_used, H * n + i // 2 + 1)
                        pe.matmul(pw[:, i % 4, :], et[:, b % 2, i, :], w99[:, :],
                                  start=True, stop=True).then_inc(w_made, 1)

                    def total(at, i):
                        n, b, r = at
                        if i == 0:
                            wait(pe, st_done, n - 1)
                        if i % H == 0:
                            pe.wait_ge(p_done, 2 * n + i // H + 1)
                        pe.matmul(ps[:, b % 2, :], ident[:, :], work[:, b % 4, i, :, :, :].rearrange("p i a o -> p (i a o)"),
                                  start=i == 0, stop=False)

                    done, ahead, next_but_one = tile(t, q, -1), tile(t, q, 1), tile(t, q, 2)
                    if done:
                        for i in range(J - 3):
                            total(done, i)
                    if next_but_one:
                        n, b, r = next_but_one
                        pe.wait_ge(low_cut, n + 1)
                        wait(pe, et_copied, n - 1)
                        for i in range(J):
                            ins = pe.transpose(pt[0:KS, b % 2, i, :], parts[:, b % 4, i, 0:KS], identb[:, :])
                        ins.then_inc(turned, 1)
                    if ahead:
                        for i in range(4, J):
                            weigh(ahead, i)
                    if done:
                        total(done, J - 3)
                    if next_but_one:
                        pe.wait_ge(et_copied, next_but_one[0] + 1)
                        for i in range(2):
                            weigh(next_but_one, i)
                    if done:
                        total(done, J - 2)
                    if next_but_one:
                        for i in range(2, 4):
                            weigh(next_but_one, i)
                    if done:
                        total(done, J - 1)
                        n, b, r = done
                        pe.wait_ge(carried, n + 1)
                        pe.matmul(ps[:, b % 2, :], ident[:, :], carry[:, b % 2, :], start=False, stop=True).then_inc(summed, 1)

                rounds(pe, body, 2, 1)

            @block.vector
            def _(v):
                v.sem_inc(w_used, 2)
                v.wait_ge(primed, 2)

                def word(b, i):
                    return mt[:, b, i:i + 1].bitcast(F32)

                def edges(at, i):
                    n, b, r = at
                    v.wait_ge(w_made, J * n + i + 2)
                    v.tensor_tensor(work[:, b % 4, i:i + 2, :, :, :].rearrange("p j i a o -> p (j i) (a o)"),
                                    pw[:, i % 4:i % 4 + 2, :].rearrange("p j (i c) -> p (j i) c", i=D),
                                    xg[:, b % 4, i:i + 2, :].rearrange("p j i -> p (j i)").unsqueeze(2).to_broadcast([GP, 2 * D, 2 * D]),
                                    ALU.mult).then_inc(w_used, 1)

                def maxima(at):
                    n, b, r = at
                    s = work[:, b % 4, :, :, 0, :]
                    out = lambda lo, hi: top[:, lo:hi, :].rearrange("p j (i o) -> p j i o", i=D)
                    v.wait_ge(masked, J * (n + 1))
                    v.tensor_tensor(out(0, 4), s[:, 0:4], s[:, 4:8], ALU.max).then_inc(chain, 1)
                    v.wait_ge(chain, MS * n + 1)
                    v.tensor_tensor(top[:, 4:6, :], top[:, 0:2, :], top[:, 2:4, :], ALU.max).then_inc(chain, 1)
                    v.wait_ge(chain, MS * n + 2)
                    v.tensor_tensor(top[:, 6, :], top[:, 4, :], top[:, 5, :], ALU.max).then_inc(chain, 1)
                    wait(v, scattered[b], 16 * r)
                    v.wait_ge(chain, MS * n + 3)
                    v.scalar_tensor_tensor(out=state[:, b, 0:C], in0=state[:, (b - 1) % U, 0:C], scalar=word(b, 2),
                                           in1=top[:, 6, :], op0=ALU.add, op1=ALU.max).then_inc(chain, 1)
                    v.wait_ge(chain, MS * n + 4)
                    wait(v, corr_done, n)
                    v.scalar_tensor_tensor(out=gap[:, :], in0=state[:, (b - 1) % U, 0:C], scalar=word(b, 2),
                                           in1=state[:, b, 0:C], op0=ALU.add, op1=ALU.subtract).then_inc(gap_done, 1)
                    for half in range(2):
                        s = work[:, b % 4, half * H:(half + 1) * H, :, 0, :]
                        v.tensor_tensor(s, s, channels(state[:, b, 0:C]).unsqueeze(1).to_broadcast([GP, H, D, D]),
                                        ALU.subtract).then_inc(less, 1)

                def products(at, half):
                    n, b, r = at
                    v.wait_ge(exped, 2 * n + half + 1)
                    w = work[:, b % 4, half * H:(half + 1) * H, :, :, :]
                    v.tensor_tensor(w[:, :, :, 1, :], w[:, :, :, 1, :], w[:, :, :, 0, :], ALU.mult).then_inc(p_done, 1)

                def body(t, q):
                    now, ahead = tile(t, q, 0), tile(t, q, 1)
                    if now:
                        maxima(now)
                    if ahead:
                        v.wait_ge(x_in[ahead[1] % 4], 16 * J * (2 * ahead[2] + ahead[1] // 4 + 1))
                        for i in range(0, J, 2):
                            edges(ahead, i)
                    if now:
                        for half in range(2):
                            products(now, half)

                rounds(v, body, 1, 0)

        with ExitStack() as st:
            def tsb(name, shape, dt=F32):
                return st.enter_context(nc.sbuf_tensor(name, shape, dt))

            ht = tsb("ht", [GP, 2, 3 * C])
            both = tsb("both", [GP, 2, 2 * C])
            cs = tsb("cs", [128, 2, 4, GP, 2])
            kd = tsb("kd", [GP, 2, GP])
            kr = tsb("kr", [128, GP, 2])
            neg = tsb("neg", [128, 2 * GP])
            top = tsb("top", [128, 4, 2 * GP])
            dec = tsb("dec", [128, 4, 2 * GP])
            wgt = tsb("wgt", [128, 4, 2 * GP])
            run = tsb("run", [128, 4, 2 * GP])
            rows = tsb("rows", [GP, 2], I32)
            rowf = tsb("rowf", [GP, 4])
            pm = st.enter_context(nc.psum_tensor("pm", [128, 5, 4, 128], F32))
            ht_in = sem("ht_in")
            turned = sem("merge_turned")
            m_beside = sem("merge_m_beside")
            LAST_STEP = 22
            cs_made = sem("merge_cs_made")
            step = sem("merge_step")
            exped = sem("merge_exped")
            back = sem("merge_back")
            ht_made = sem("merge_ht_made")
            weighed = sem("merge_weighed")
            merged = sem("merged")
            block = st.enter_context(nc.Block())

            def part(s, a, f):
                c = slice(f * 128, (f + 1) * 128)
                return both[:, s, c] if a == 0 else ht[:, s, C:3 * C][:, c]

            @block.sync
            def _(sp):
                sp.dma_start(ht[:, 0, :], rtab[HEAD:HEAD + GP, :]).then_inc(ht_in, 16)
                sp.dma_start(ht[:, 1, :], rtab[TAIL:TAIL + GP, :]).then_inc(ht_in, 16)

            @block.tensor
            def _(pe):
                pe.wait_ge(ht_in, 32)
                pe.wait_ge(m_beside, 2)
                n = 0
                for a in range(2):
                    for f in range(4):
                        for s in range(2):
                            pe.transpose(pm[:, n // 4, n % 4, :], part(s, a, f), ident[:, :])
                            n += 1
                pe.wait_ge(step, 2)
                for s in range(2):
                    ins = pe.matmul(pm[:, 4, s, :], ones[:, :], kd[:, s, :], start=True, stop=True)
                ins.then_inc(turned, 1)
                pe.wait_ge(step, LAST_STEP)
                n = 0
                for f in range(4):
                    for s in range(2):
                        ins = pe.transpose(pm[:, n // 4, n % 4, :], run[:, f, :].rearrange("c (p s) -> c p s", s=2)[:, :, s], ident[:, :])
                        n += 1
                ins.then_inc(back, 1)

            @block.vector
            def _(v):
                for s in range(2):
                    v.tensor_scalar(kd[:, s, :], ident[0:GP, 0:GP], ends[:, s:s + 1], None, ALU.mult).then_inc(step, 1)
                v.tensor_tensor(rowf[:, 0:1], ends[:, 0:1], ends[:, 1:2], ALU.not_equal).then_inc(step, 1)
                v.tensor_tensor(rowf[:, 1:2], ends[:, 1:2], ends[:, 2:3], ALU.not_equal).then_inc(step, 1)
                v.tensor_scalar(rowf[:, 2:4], ends[:, 0:2], -float(SKIP), None, ALU.add).then_inc(step, 1)
                v.wait_ge(step, 5)
                v.tensor_tensor(rowf[:, 0:2], rowf[:, 0:2], rowf[:, 2:4], ALU.mult).then_inc(step, 1)
                v.wait_ge(step, 6)
                v.tensor_scalar(rows[:, :], rowf[:, 0:2], float(SKIP), None, ALU.add).then_inc(step, 1)
                v.wait_ge(ht_in, 32)
                for s in range(2):
                    v.tensor_copy(both[:, s, :].rearrange("p (i a o) -> p i a o", i=D, a=2),
                                  ht[:, s, 0:C].rearrange("p (i o) -> p i o", i=D).unsqueeze(2).to_broadcast([GP, D, 2, D])).then_inc(m_beside, 1)
                v.wait_ge(turned, 1)
                n = 0
                for a in range(2):
                    for f in range(4):
                        v.tensor_copy(cs[:, a, f, :, :].rearrange("c p s -> c s p"),
                                      pm[:, n // 4, n % 4:n % 4 + 2, 0:GP]).then_inc(step, 1)
                        n += 2
                v.tensor_copy(kr[:, :, :].rearrange("c p s -> c s p"), pm[:, 4, 0:2, 0:GP]).then_inc(step, 1)
                v.wait_ge(step, 16)
                k = kr[:, :, :].rearrange("c p s -> c (p s)")
                v.memset(neg[:, 0:1], 1.0)
                v.tensor_tensor(neg[:, 1:], k[:, 1:], k[:, 0:2 * GP - 1], ALU.not_equal).then_inc(step, 1)
                v.wait_ge(step, 17)
                v.tensor_scalar(neg[:, :], neg[:, :], -BIG, None, ALU.mult).then_inc(step, 1)
                v.wait_ge(step, 18)
                seq = lambda a, f: cs[:, a, f, :, :].rearrange("c p s -> c (p s)")
                v.memset(dec[:, :, 0:1], -BIG)
                for f in range(4):
                    ins = v.tensor_tensor_scan(top[:, f, :], neg[:, :], seq(0, f), 0.0, ALU.add, ALU.max)
                ins.then_inc(step, 1)
                v.wait_ge(step, 19)
                wide = neg[:, 1:].unsqueeze(1).to_broadcast([128, 4, 2 * GP - 1])
                v.tensor_tensor(dec[:, :, 1:], top[:, :, 0:2 * GP - 1], wide, ALU.add)
                v.tensor_tensor(wgt[:, :, :], cs[:, 0, :, :, :].rearrange("c f p s -> c f (p s)"), top[:, :, :],
                                ALU.subtract).then_inc(step, 1)
                v.wait_ge(step, 20)
                v.tensor_tensor(dec[:, :, 1:], dec[:, :, 1:], top[:, :, 1:], ALU.subtract).then_inc(step, 1)
                v.wait_ge(exped, 2)
                sums = cs[:, 1, :, :, :].rearrange("c f p s -> c f (p s)")
                v.tensor_tensor(sums, sums, wgt[:, :, :], ALU.mult).then_inc(weighed, 1)
                v.wait_ge(weighed, 1)
                for f in range(4):
                    ins = v.tensor_tensor_scan(run[:, f, :], dec[:, f, :], seq(1, f), 0.0, ALU.mult, ALU.add)
                ins.then_inc(step, 1)
                v.wait_ge(back, 1)
                for s in range(2):
                    v.tensor_copy(ht[:, s, C:3 * C].rearrange("p (b f c) -> p b f c", b=2, f=2),
                                  pm[:, 0:2, :, :].rearrange("p b (f s) c -> p b f s c", s=2)[:, :, :, s, :]).then_inc(ht_made, 1)

            @block.scalar
            def _(act):
                act.wait_ge(step, 21)
                act.activation(dec[:, :, :], dec[:, :, :], ACT.Exp).then_inc(exped, 1)
                act.activation(wgt[:, :, :], wgt[:, :, :], ACT.Exp).then_inc(exped, 1)

            @block.gpsimd
            def _(g):
                g.wait_ge(ht_made, 2)
                for s in range(2):
                    g.indirect_dma_start(rtab, bass.IndirectOffsetOnAxis(ap=rows[:, s:s + 1], axis=0),
                                         ht[:, s, :], None,
                                         bounds_check=ROWS - 1, oob_is_err=False).then_inc(merged, 16)
                g.wait_ge(merged, 32)

        with ExitStack() as st:
            def tsb(name, shape, dt=F32):
                return st.enter_context(nc.sbuf_tensor(name, shape, dt))

            tab = tsb("tab", [128, 3, LO * D, 2, D])
            ft = tsb("ft", [128, NB, LO, D])
            row_in = [sem(f"row_in{b}") for b in range(NB)]
            inv = tsb("inv", [128, 2, LO * D, D])
            logged = sem("logged")
            guessed = sem("guessed")
            off_by = sem("off_by")
            f_step = sem("f_step")
            n_step = sem("l1_norm_step")
            n_root = sem("l1_norm_root")
            block = st.enter_context(nc.Block())
            view = rtab[0:NPAD, :].rearrange("(b p l) c -> b p l c", p=128, l=LO)

            @block.sync
            def _(sp):
                for b in range(NB):
                    if b >= 3:
                        sp.wait_ge(f_step, 3 * (b - 2))
                    sp.dma_start(tab[:, b % 3, :, :, :].rearrange("p (l i) a o -> p l (i a o)", l=LO), view[b, :, :, C:3 * C]).then_inc(row_in[b], 16)
                sp.wait_ge(n_step, 9)
                nfull = FULL * 128 * LO
                sp.dma_start(out[0:nfull, :].rearrange("(b p l) c -> p b (l c)", p=128, l=LO),
                             y[:, 0:FULL, :, :].rearrange("p b l c -> p b (l c)")).then_inc(out_out, 16)
                sp.dma_start(out[nfull:nfull + REST * LO, :].rearrange("(p l) c -> p (l c)", l=LO),
                             y[0:REST, FULL, :, :].rearrange("p l c -> p (l c)")).then_inc(out_out, 16)
                sp.dma_start(out[N - LAST:N, :].rearrange("(p l) c -> p (l c)", l=LAST),
                             y[REST:REST + 1, FULL, 0:LAST, :].rearrange("p l c -> p (l c)")).then_inc(out_out, 16)
                sp.wait_ge(out_out, 48)

            @block.gpsimd
            def _(g):
                for b in range(NB):
                    s = tab[:, b % 3, :, 0, :]
                    g.wait_ge(guessed, b + 1)
                    g.tensor_tensor(s, s, inv[:, b % 2, :, :], ALU.mult).then_inc(off_by, 1)

            @block.vector
            def _(v):
                for b in range(NB):
                    s, t = tab[:, b % 3, :, 0, :], tab[:, b % 3, :, 1, :]
                    v.wait_ge(row_in[b], 16)
                    v.wait_ge(guessed, b + 1)
                    v.tensor_tensor(t, t, inv[:, b % 2, :, :], ALU.mult).then_inc(f_step, 1)
                    v.wait_ge(off_by, b + 1)
                    v.wait_ge(f_step, 3 * b + 1)
                    v.scalar_tensor_tensor(out=t, in0=s, scalar=-2.0, in1=t, op0=ALU.add, op1=ALU.mult).then_inc(f_step, 1)
                    v.wait_ge(f_step, 3 * b + 2)
                    v.tensor_reduce(ft[:, b, :, :], t.rearrange("p (l i) o -> p l o i", i=D), AX, ALU.add).then_inc(f_step, 1)
                v.wait_ge(f_step, 3 * NB)
                v.tensor_tensor(y[:, :, :, :], y[:, :, :, :], ft[:, :, :, :], ALU.subtract).then_inc(n_step, 1)
                v.wait_ge(n_step, 1)
                base = layer_norm(v, n_step, 1)
                layer_norm_end(v, n_step, base, n_root)

            @block.scalar
            def _(act):
                for b in range(NB):
                    act.wait_ge(row_in[b], 16)
                    if b >= 2:
                        act.wait_ge(f_step, 3 * (b - 2) + 2)
                    act.activation(inv[:, b % 2, :, :], tab[:, b % 3, :, 0, :], ACT.Ln).then_inc(logged, 1)
                    act.wait_ge(logged, b + 1)
                    act.activation(inv[:, b % 2, :, :], inv[:, b % 2, :, :], ACT.Exp, scale=-1.0).then_inc(guessed, 1)
                act.wait_ge(n_step, 7)
                act.activation(stat[:, 2, :], stat[:, 1, :], ACT.Sqrt).then_inc(n_root, 1)


_INS = ['x', 'src', 'dst', 'edge_attr_16', 'edge_attr_8', 'node_vec1', 'L0_gnn_W_msg_tp', 'L0_gnn_W_msg_lin',
        'L0_gnn_W_upd_tp', 'L0_gnn_W_upd_lin', 'L1_gnn_W_msg', 'L1_gnn_b_msg', 'L1_gnn_W_attn', 'L1_gnn_b_attn']
_OUTS = [((N, D), 'float32')]


def kernel(**inputs):
    import numpy as _np
    import concourse.bacc as _bacc
    from concourse import mybir as _mybir
    from concourse.bass_utils import run_bass_kernel_spmd as _run

    nc = _bacc.Bacc("TRN2", target_bir_lowering=False, num_devices=1)
    arrays, args = {}, []
    for name in _INS:
        a = _np.ascontiguousarray(inputs[name])
        arrays[f"in_{name}_dram"] = a
        args.append(nc.dram_tensor(f"in_{name}_dram", a.shape, _mybir.dt.from_np(a.dtype), kind="ExternalInput").ap())
    for i, (shape, dtype) in enumerate(_OUTS):
        dt = _mybir.dt.from_np(_np.dtype(dtype))
        args.append(nc.dram_tensor(f"out_{i}_dram", shape, dt, kind="ExternalOutput").ap())
    gnn(nc, *args)
    r = _run(nc, [arrays], core_ids=[0])
    return r.results[0]["out_0_dram"]
```
